# Optimizing a Trainium2 kernel written in Bass

```python
import numpy as np
import jax
import jax.numpy as jnp

def _softmax(x, axis=-1):
    return jax.nn.softmax(x, axis=axis)

def _gelu(x):
    return jax.nn.gelu(x, approximate=True)

def _silu(x):
    return jax.nn.silu(x)

def _sigmoid(x):
    return jax.nn.sigmoid(x)

def _layernorm(x, axis=-1, eps=1e-05):
    m = jnp.mean(x, axis=axis, keepdims=True)
    v = jnp.var(x, axis=axis, keepdims=True)
    return (x - m) / jnp.sqrt(v + eps)

def _scatter_add(tgt, idx, src, axis=0):
    return tgt.at[idx].add(src)

def _segment_sum(src, seg, n):
    return jax.ops.segment_sum(src, seg, n)
kernel_name = 'mk_conv_seq_d4_conv_nchw256_r4_8ed606'

def setup_inputs(seed: int=0):
    np.random.seed(seed)
    _w = jnp.asarray

    def _rec_inputs():
        import jax
        import jax.numpy as jnp
        _gk = jax.random.key(seed)
        x = -0.0003929 + 0.9999 * jax.random.normal(jax.random.fold_in(_gk, 1), (16, 64, 16, 16), jnp.float32)
        return x
    x = _rec_inputs()

    def _L0_conv_setup():
        import jax, jax.numpy as jnp
        import numpy as np
        B, C_IN, C_OUT, H, W = (16, 64, 64, 16, 16)
        key = jax.random.key(seed)
        ks = jax.random.split(key, 7)
        s = 1.0 / np.sqrt(C_IN)
        return {'x': jax.random.normal(ks[0], (B, C_IN, H, W), dtype=jnp.float32), 'wq': jax.random.uniform(ks[1], (C_OUT, C_IN), jnp.float32, -s, s), 'bq': jax.random.uniform(ks[2], (C_OUT,), jnp.float32, -s, s), 'wk': jax.random.uniform(ks[3], (C_OUT, C_IN), jnp.float32, -s, s), 'bk': jax.random.uniform(ks[4], (C_OUT,), jnp.float32, -s, s), 'wv': jax.random.uniform(ks[5], (C_OUT, C_IN), jnp.float32, -s, s), 'bv': jax.random.uniform(ks[6], (C_OUT,), jnp.float32, -s, s)}
    _L0_conv_all = _L0_conv_setup()
    _L0_conv_in = {k: v for k, v in _L0_conv_all.items() if k in ('wq', 'bq', 'wk', 'bk', 'wv', 'bv')}
    del _L0_conv_all

    def _L1_conv_setup():
        import jax, jax.numpy as jnp
        import numpy as np
        KK = 9
        PAD = 1
        EPS = 1e-05

        def _conv2d(x, w, b):
            y = jax.lax.conv_general_dilated(x, w, window_strides=(1, 1), padding=((PAD, PAD), (PAD, PAD)), dimension_numbers=('NCHW', 'OIHW', 'NCHW'))
            return y + b[None, :, None, None]

        def _bilinear_sample_one(img, py, px):
            C, H, W = img.shape
            y0 = jnp.floor(py).astype(jnp.int32)
            x0 = jnp.floor(px).astype(jnp.int32)
            wy = py - y0
            wx = px - x0

            def g(yi, xi):
                ok = ((yi >= 0) & (yi < H) & (xi >= 0) & (xi < W)).astype(img.dtype)
                v = img[:, jnp.clip(yi, 0, H - 1), jnp.clip(xi, 0, W - 1)]
                return v * ok[None]
            v00 = g(y0, x0)
            v01 = g(y0, x0 + 1)
            v10 = g(y0 + 1, x0)
            v11 = g(y0 + 1, x0 + 1)
            return v00 * (1 - wy) * (1 - wx) + v01 * (1 - wy) * wx + v10 * wy * (1 - wx) + v11 * wy * wx
        key = jax.random.key(seed)
        ks = jax.random.split(key, 8)
        B, C, H, W = (8, 64, 24, 24)
        O = 64
        x = jax.random.normal(ks[0], (B, C, H, W), dtype=jnp.float32)
        w_off = jax.random.normal(ks[1], (3 * KK, C, 3, 3), dtype=jnp.float32) * 0.01
        b_off = jnp.zeros((3 * KK,), dtype=jnp.float32)
        w_dcn = jax.random.normal(ks[2], (O, C, 3, 3), dtype=jnp.float32) * (1.0 / np.sqrt(C * KK))
        b_dcn = jnp.zeros((O,), dtype=jnp.float32)
        gamma = jnp.ones((O,), dtype=jnp.float32)
        beta = jnp.zeros((O,), dtype=jnp.float32)
        running_mean = jax.random.normal(ks[3], (O,), dtype=jnp.float32) * 0.1
        running_var = jax.random.uniform(ks[4], (O,), dtype=jnp.float32, minval=0.5, maxval=1.5)
        return {'x': x, 'w_off': w_off, 'b_off': b_off, 'w_dcn': w_dcn, 'b_dcn': b_dcn, 'gamma': gamma, 'beta': beta, 'running_mean': running_mean, 'running_var': running_var}
    _L1_conv_all = _L1_conv_setup()
    _L1_conv_in = {k: v for k, v in _L1_conv_all.items() if k in ('w_off', 'b_off', 'w_dcn', 'b_dcn', 'gamma', 'beta', 'running_mean', 'running_var')}
    del _L1_conv_all

    def _L2_conv_setup():
        import jax, jax.numpy as jnp
        import numpy as np
        B, C, H, W = (4, 64, 16, 16)
        key = jax.random.key(seed)
        ks = jax.random.split(key, 6)
        scale = 1.0 / np.sqrt(C)
        x = jax.random.normal(ks[0], (B, C, H, W), dtype=jnp.float32)
        wq = jax.random.normal(ks[1], (C, C), dtype=jnp.float32) * scale
        wk = jax.random.normal(ks[2], (C, C), dtype=jnp.float32) * scale
        wv = jax.random.normal(ks[3], (C, C), dtype=jnp.float32) * scale
        wp = jax.random.normal(ks[4], (C, C), dtype=jnp.float32) * scale
        zb = jnp.zeros((C,), dtype=jnp.float32)
        return {'x': x, 'wq': wq, 'bq': zb, 'wk': wk, 'bk': zb, 'wv': wv, 'bv': zb, 'wp': wp, 'bp': zb}
    _L2_conv_all = _L2_conv_setup()
    _L2_conv_in = {k: v for k, v in _L2_conv_all.items() if k in ('wq', 'bq', 'wk', 'bk', 'wv', 'bv', 'wp', 'bp')}
    del _L2_conv_all

    def _L3_conv_setup():
        import jax, jax.numpy as jnp
        from jax import lax
        import numpy as np
        N, C, H, W = (8, 64, 24, 24)
        K = 5
        HID = 2 * C

        def _ln2d(x, w, b, eps=1e-06):
            m = x.mean(axis=(2, 3), keepdims=True)
            v = ((x - m) ** 2).mean(axis=(2, 3), keepdims=True)
            return (x - m) * lax.rsqrt(v + eps) * w[None, :, None, None] + b[None, :, None, None]

        def _scan1d(seq, dw_w, dw_b, g_w, g_b):
            c = seq.shape[-1]
            y = lax.conv_general_dilated(seq, dw_w, (1,), [(K // 2, K // 2)], dimension_numbers=('NWC', 'WIO', 'NWC'), feature_group_count=c) + dw_b
            g = jax.nn.sigmoid(jnp.einsum('blc,dc->bld', seq, g_w) + g_b)
            return y * g

        def _forward(x, ln1_w, ln1_b, dw_w, dw_b, lr_dw_w, lr_dw_b, lr_g_w, lr_g_b, rl_dw_w, rl_dw_b, rl_g_w, rl_g_b, tb_dw_w, tb_dw_b, tb_g_w, tb_g_b, bt_dw_w, bt_dw_b, bt_g_w, bt_g_b, fuse_w, fuse_b, ln2_w, ln2_b, ff1_w, ff1_b, ff2_w, ff2_b):
            n, c, hh, ww = x.shape
            y = _ln2d(x, ln1_w, ln1_b)
            y = lax.conv_general_dilated(y, dw_w, (1, 1), [(1, 1), (1, 1)], dimension_numbers=('NCHW', 'HWIO', 'NCHW'), feature_group_count=c) + dw_b[None, :, None, None]
            y = jnp.transpose(y, (0, 2, 3, 1))
            o = _scan1d(y.reshape(n * hh, ww, c), lr_dw_w, lr_dw_b, lr_g_w, lr_g_b).reshape(n, hh, ww, c)
            yf = jnp.flip(y, 2).reshape(n * hh, ww, c)
            o = o + jnp.flip(_scan1d(yf, rl_dw_w, rl_dw_b, rl_g_w, rl_g_b).reshape(n, hh, ww, c), 2)
            yt = jnp.transpose(y, (0, 2, 1, 3)).reshape(n * ww, hh, c)
            o = o + jnp.transpose(_scan1d(yt, tb_dw_w, tb_dw_b, tb_g_w, tb_g_b).reshape(n, ww, hh, c), (0, 2, 1, 3))
            yb = jnp.transpose(jnp.flip(y, 1), (0, 2, 1, 3)).reshape(n * ww, hh, c)
            o = o + jnp.flip(jnp.transpose(_scan1d(yb, bt_dw_w, bt_dw_b, bt_g_w, bt_g_b).reshape(n, ww, hh, c), (0, 2, 1, 3)), 1)
            y = jnp.transpose(o, (0, 3, 1, 2))
            y = jnp.einsum('nchw,dc->ndhw', y, fuse_w) + fuse_b[None, :, None, None]
            x = x + y
            z = _ln2d(x, ln2_w, ln2_b)
            z = jnp.einsum('nchw,dc->ndhw', z, ff1_w) + ff1_b[None, :, None, None]
            a, g = jnp.split(z, 2, axis=1)
            z = a * jax.nn.sigmoid(g)
            z = jnp.einsum('nchw,dc->ndhw', z, ff2_w) + ff2_b[None, :, None, None]
            return x + z
        key = jax.random.key(seed)
        ks = iter(jax.random.split(key, 40))
        nrm = lambda *s: jax.random.normal(next(ks), s, jnp.float32) * 0.02
        inp = {'x': jax.random.normal(next(ks), (N, C, H, W), jnp.float32)}
        inp['ln1_w'] = jnp.ones((C,), jnp.float32)
        inp['ln1_b'] = jnp.zeros((C,), jnp.float32)
        inp['dw_w'] = nrm(3, 3, 1, C)
        inp['dw_b'] = jnp.zeros((C,), jnp.float32)
        for d in ('lr', 'rl', 'tb', 'bt'):
            inp[d + '_dw_w'] = nrm(K, 1, C)
            inp[d + '_dw_b'] = jnp.zeros((C,), jnp.float32)
            inp[d + '_g_w'] = nrm(C, C)
            inp[d + '_g_b'] = jnp.zeros((C,), jnp.float32)
        inp['fuse_w'] = nrm(C, C)
        inp['fuse_b'] = jnp.zeros((C,), jnp.float32)
        inp['ln2_w'] = jnp.ones((C,), jnp.float32)
        inp['ln2_b'] = jnp.zeros((C,), jnp.float32)
        inp['ff1_w'] = nrm(2 * HID, C)
        inp['ff1_b'] = jnp.zeros((2 * HID,), jnp.float32)
        inp['ff2_w'] = nrm(C, HID)
        inp['ff2_b'] = jnp.zeros((C,), jnp.float32)
        return inp
    _L3_conv_all = _L3_conv_setup()
    _L3_conv_in = {k: v for k, v in _L3_conv_all.items() if k in ('ln1_w', 'ln1_b', 'dw_w', 'dw_b', 'lr_dw_w', 'lr_dw_b', 'lr_g_w', 'lr_g_b', 'rl_dw_w', 'rl_dw_b', 'rl_g_w', 'rl_g_b', 'tb_dw_w', 'tb_dw_b', 'tb_g_w', 'tb_g_b', 'bt_dw_w', 'bt_dw_b', 'bt_g_w', 'bt_g_b', 'fuse_w', 'fuse_b', 'ln2_w', 'ln2_b', 'ff1_w', 'ff1_b', 'ff2_w', 'ff2_b')}
    del _L3_conv_all
    return {'x': x, 'L0_conv_wq': _L0_conv_in['wq'], 'L0_conv_bq': _L0_conv_in['bq'], 'L0_conv_wk': _L0_conv_in['wk'], 'L0_conv_bk': _L0_conv_in['bk'], 'L0_conv_wv': _L0_conv_in['wv'], 'L0_conv_bv': _L0_conv_in['bv'], 'L1_conv_w_off': _L1_conv_in['w_off'], 'L1_conv_b_off': _L1_conv_in['b_off'], 'L1_conv_w_dcn': _L1_conv_in['w_dcn'], 'L1_conv_b_dcn': _L1_conv_in['b_dcn'], 'L1_conv_gamma': _L1_conv_in['gamma'], 'L1_conv_beta': _L1_conv_in['beta'], 'L1_conv_running_mean': _L1_conv_in['running_mean'], 'L1_conv_running_var': _L1_conv_in['running_var'], 'L2_conv_wq': _L2_conv_in['wq'], 'L2_conv_bq': _L2_conv_in['bq'], 'L2_conv_wk': _L2_conv_in['wk'], 'L2_conv_bk': _L2_conv_in['bk'], 'L2_conv_wv': _L2_conv_in['wv'], 'L2_conv_bv': _L2_conv_in['bv'], 'L2_conv_wp': _L2_conv_in['wp'], 'L2_conv_bp': _L2_conv_in['bp'], 'L3_conv_ln1_w': _L3_conv_in['ln1_w'], 'L3_conv_ln1_b': _L3_conv_in['ln1_b'], 'L3_conv_dw_w': _L3_conv_in['dw_w'], 'L3_conv_dw_b': _L3_conv_in['dw_b'], 'L3_conv_lr_dw_w': _L3_conv_in['lr_dw_w'], 'L3_conv_lr_dw_b': _L3_conv_in['lr_dw_b'], 'L3_conv_lr_g_w': _L3_conv_in['lr_g_w'], 'L3_conv_lr_g_b': _L3_conv_in['lr_g_b'], 'L3_conv_rl_dw_w': _L3_conv_in['rl_dw_w'], 'L3_conv_rl_dw_b': _L3_conv_in['rl_dw_b'], 'L3_conv_rl_g_w': _L3_conv_in['rl_g_w'], 'L3_conv_rl_g_b': _L3_conv_in['rl_g_b'], 'L3_conv_tb_dw_w': _L3_conv_in['tb_dw_w'], 'L3_conv_tb_dw_b': _L3_conv_in['tb_dw_b'], 'L3_conv_tb_g_w': _L3_conv_in['tb_g_w'], 'L3_conv_tb_g_b': _L3_conv_in['tb_g_b'], 'L3_conv_bt_dw_w': _L3_conv_in['bt_dw_w'], 'L3_conv_bt_dw_b': _L3_conv_in['bt_dw_b'], 'L3_conv_bt_g_w': _L3_conv_in['bt_g_w'], 'L3_conv_bt_g_b': _L3_conv_in['bt_g_b'], 'L3_conv_fuse_w': _L3_conv_in['fuse_w'], 'L3_conv_fuse_b': _L3_conv_in['fuse_b'], 'L3_conv_ln2_w': _L3_conv_in['ln2_w'], 'L3_conv_ln2_b': _L3_conv_in['ln2_b'], 'L3_conv_ff1_w': _L3_conv_in['ff1_w'], 'L3_conv_ff1_b': _L3_conv_in['ff1_b'], 'L3_conv_ff2_w': _L3_conv_in['ff2_w'], 'L3_conv_ff2_b': _L3_conv_in['ff2_b']}

def reference(x, L0_conv_wq, L0_conv_bq, L0_conv_wk, L0_conv_bk, L0_conv_wv, L0_conv_bv, L1_conv_w_off, L1_conv_b_off, L1_conv_w_dcn, L1_conv_b_dcn, L1_conv_gamma, L1_conv_beta, L1_conv_running_mean, L1_conv_running_var, L2_conv_wq, L2_conv_bq, L2_conv_wk, L2_conv_bk, L2_conv_wv, L2_conv_bv, L2_conv_wp, L2_conv_bp, L3_conv_ln1_w, L3_conv_ln1_b, L3_conv_dw_w, L3_conv_dw_b, L3_conv_lr_dw_w, L3_conv_lr_dw_b, L3_conv_lr_g_w, L3_conv_lr_g_b, L3_conv_rl_dw_w, L3_conv_rl_dw_b, L3_conv_rl_g_w, L3_conv_rl_g_b, L3_conv_tb_dw_w, L3_conv_tb_dw_b, L3_conv_tb_g_w, L3_conv_tb_g_b, L3_conv_bt_dw_w, L3_conv_bt_dw_b, L3_conv_bt_g_w, L3_conv_bt_g_b, L3_conv_fuse_w, L3_conv_fuse_b, L3_conv_ln2_w, L3_conv_ln2_b, L3_conv_ff1_w, L3_conv_ff1_b, L3_conv_ff2_w, L3_conv_ff2_b):
    import jax
    import jax.numpy as jnp

    def _L0_conv_ref(x, wq, bq, wk, bk, wv, bv):
        import jax, jax.numpy as jnp
        import numpy as np
        B, C_IN, C_OUT, H, W = (16, 64, 64, 16, 16)
        b, c_in, h, w = x.shape
        xf = x.reshape(b, c_in, h * w)
        q = jnp.einsum('oc,bcn->bon', wq, xf) + bq[None, :, None]
        k = jnp.einsum('oc,bcn->bon', wk, xf) + bk[None, :, None]
        v = jnp.einsum('oc,bcn->bon', wv, xf) + bv[None, :, None]
        c = q.shape[1]
        attn = jnp.einsum('bcn,bdn->bcd', q, k) / jnp.sqrt(jnp.asarray(c, x.dtype))
        attn = jax.nn.softmax(attn, axis=-1)
        attended = jnp.einsum('bcd,bdn->bcn', attn, v)
        return x + attended.reshape(b, c, h, w)

    def _L1_conv_ref(x, w_off, b_off, w_dcn, b_dcn, gamma, beta, running_mean, running_var):
        import jax, jax.numpy as jnp
        import numpy as np
        KK = 9
        PAD = 1
        EPS = 1e-05

        def _conv2d(x, w, b):
            y = jax.lax.conv_general_dilated(x, w, window_strides=(1, 1), padding=((PAD, PAD), (PAD, PAD)), dimension_numbers=('NCHW', 'OIHW', 'NCHW'))
            return y + b[None, :, None, None]

        def _bilinear_sample_one(img, py, px):
            C, H, W = img.shape
            y0 = jnp.floor(py).astype(jnp.int32)
            x0 = jnp.floor(px).astype(jnp.int32)
            wy = py - y0
            wx = px - x0

            def g(yi, xi):
                ok = ((yi >= 0) & (yi < H) & (xi >= 0) & (xi < W)).astype(img.dtype)
                v = img[:, jnp.clip(yi, 0, H - 1), jnp.clip(xi, 0, W - 1)]
                return v * ok[None]
            v00 = g(y0, x0)
            v01 = g(y0, x0 + 1)
            v10 = g(y0 + 1, x0)
            v11 = g(y0 + 1, x0 + 1)
            return v00 * (1 - wy) * (1 - wx) + v01 * (1 - wy) * wx + v10 * wy * (1 - wx) + v11 * wy * wx
        B, C, H, W = x.shape
        O = w_dcn.shape[0]
        om = _conv2d(x, w_off, b_off)
        offset = om[:, :2 * KK]
        mask = jax.nn.sigmoid(om[:, 2 * KK:])
        off_y = offset[:, 0::2]
        off_x = offset[:, 1::2]
        ky, kx = jnp.meshgrid(jnp.arange(3), jnp.arange(3), indexing='ij')
        ky = ky.reshape(KK).astype(x.dtype)
        kx = kx.reshape(KK).astype(x.dtype)
        hh = jnp.arange(H, dtype=x.dtype)
        ww = jnp.arange(W, dtype=x.dtype)
        py = off_y + hh[None, None, :, None] + ky[None, :, None, None] - PAD
        px = off_x + ww[None, None, None, :] + kx[None, :, None, None] - PAD
        sampled = jax.vmap(_bilinear_sample_one)(x, py, px)
        sampled = sampled * mask[:, None]
        out = jnp.einsum('bckhw,ock->bohw', sampled, w_dcn.reshape(O, C, KK))
        out = out + b_dcn[None, :, None, None]
        inv = jax.lax.rsqrt(running_var + EPS)
        out = (out - running_mean[None, :, None, None]) * (gamma * inv)[None, :, None, None]
        out = out + beta[None, :, None, None]
        return jax.nn.relu(out)

    def _L2_conv_ref(x, wq, bq, wk, bk, wv, bv, wp, bp):
        import jax, jax.numpy as jnp
        import numpy as np
        B, C, H, W = (4, 64, 16, 16)
        b, c, h, w = x.shape
        n = h * w
        xf = x.reshape(b, c, n)
        q = jnp.einsum('oc,bcn->bon', wq, xf) + bq[:, None]
        k = jnp.einsum('oc,bcn->bon', wk, xf) + bk[:, None]
        v = jnp.einsum('oc,bcn->bon', wv, xf) + bv[:, None]
        logits = jnp.einsum('bci,bcj->bij', q, k) * c ** (-0.5)
        attn = jax.nn.softmax(logits, axis=-1)
        out = jnp.einsum('bij,bcj->bci', attn, v)
        proj = jnp.einsum('oc,bcn->bon', wp, out) + bp[:, None]
        return x + proj.reshape(b, c, h, w)

    def _L3_conv_ref(x, ln1_w, ln1_b, dw_w, dw_b, lr_dw_w, lr_dw_b, lr_g_w, lr_g_b, rl_dw_w, rl_dw_b, rl_g_w, rl_g_b, tb_dw_w, tb_dw_b, tb_g_w, tb_g_b, bt_dw_w, bt_dw_b, bt_g_w, bt_g_b, fuse_w, fuse_b, ln2_w, ln2_b, ff1_w, ff1_b, ff2_w, ff2_b):
        import jax, jax.numpy as jnp
        from jax import lax
        import numpy as np
        N, C, H, W = (8, 64, 24, 24)
        K = 5
        HID = 2 * C

        def _ln2d(x, w, b, eps=1e-06):
            m = x.mean(axis=(2, 3), keepdims=True)
            v = ((x - m) ** 2).mean(axis=(2, 3), keepdims=True)
            return (x - m) * lax.rsqrt(v + eps) * w[None, :, None, None] + b[None, :, None, None]

        def _scan1d(seq, dw_w, dw_b, g_w, g_b):
            c = seq.shape[-1]
            y = lax.conv_general_dilated(seq, dw_w, (1,), [(K // 2, K // 2)], dimension_numbers=('NWC', 'WIO', 'NWC'), feature_group_count=c) + dw_b
            g = jax.nn.sigmoid(jnp.einsum('blc,dc->bld', seq, g_w) + g_b)
            return y * g

        def _forward(x, ln1_w, ln1_b, dw_w, dw_b, lr_dw_w, lr_dw_b, lr_g_w, lr_g_b, rl_dw_w, rl_dw_b, rl_g_w, rl_g_b, tb_dw_w, tb_dw_b, tb_g_w, tb_g_b, bt_dw_w, bt_dw_b, bt_g_w, bt_g_b, fuse_w, fuse_b, ln2_w, ln2_b, ff1_w, ff1_b, ff2_w, ff2_b):
            n, c, hh, ww = x.shape
            y = _ln2d(x, ln1_w, ln1_b)
            y = lax.conv_general_dilated(y, dw_w, (1, 1), [(1, 1), (1, 1)], dimension_numbers=('NCHW', 'HWIO', 'NCHW'), feature_group_count=c) + dw_b[None, :, None, None]
            y = jnp.transpose(y, (0, 2, 3, 1))
            o = _scan1d(y.reshape(n * hh, ww, c), lr_dw_w, lr_dw_b, lr_g_w, lr_g_b).reshape(n, hh, ww, c)
            yf = jnp.flip(y, 2).reshape(n * hh, ww, c)
            o = o + jnp.flip(_scan1d(yf, rl_dw_w, rl_dw_b, rl_g_w, rl_g_b).reshape(n, hh, ww, c), 2)
            yt = jnp.transpose(y, (0, 2, 1, 3)).reshape(n * ww, hh, c)
            o = o + jnp.transpose(_scan1d(yt, tb_dw_w, tb_dw_b, tb_g_w, tb_g_b).reshape(n, ww, hh, c), (0, 2, 1, 3))
            yb = jnp.transpose(jnp.flip(y, 1), (0, 2, 1, 3)).reshape(n * ww, hh, c)
            o = o + jnp.flip(jnp.transpose(_scan1d(yb, bt_dw_w, bt_dw_b, bt_g_w, bt_g_b).reshape(n, ww, hh, c), (0, 2, 1, 3)), 1)
            y = jnp.transpose(o, (0, 3, 1, 2))
            y = jnp.einsum('nchw,dc->ndhw', y, fuse_w) + fuse_b[None, :, None, None]
            x = x + y
            z = _ln2d(x, ln2_w, ln2_b)
            z = jnp.einsum('nchw,dc->ndhw', z, ff1_w) + ff1_b[None, :, None, None]
            a, g = jnp.split(z, 2, axis=1)
            z = a * jax.nn.sigmoid(g)
            z = jnp.einsum('nchw,dc->ndhw', z, ff2_w) + ff2_b[None, :, None, None]
            return x + z
        return _forward(x, ln1_w, ln1_b, dw_w, dw_b, lr_dw_w, lr_dw_b, lr_g_w, lr_g_b, rl_dw_w, rl_dw_b, rl_g_w, rl_g_b, tb_dw_w, tb_dw_b, tb_g_w, tb_g_b, bt_dw_w, bt_dw_b, bt_g_w, bt_g_b, fuse_w, fuse_b, ln2_w, ln2_b, ff1_w, ff1_b, ff2_w, ff2_b)

    def _gn(v, G=32, eps=1e-05):
        B_, C_, H_, W_ = v.shape
        g = v.reshape(B_, G, C_ // G, H_, W_)
        m = jnp.mean(g, axis=(2, 3, 4), keepdims=True)
        s = jnp.var(g, axis=(2, 3, 4), keepdims=True)
        return ((g - m) / jnp.sqrt(s + eps)).reshape(v.shape)

    def _ln_c(v, eps=1e-06):
        m = jnp.mean(v, axis=1, keepdims=True)
        s = jnp.var(v, axis=1, keepdims=True)
        return (v - m) / jnp.sqrt(s + eps)

    def _ln_t(v, eps=1e-05):
        m = jnp.mean(v, axis=-1, keepdims=True)
        s = jnp.var(v, axis=-1, keepdims=True)
        return (v - m) / jnp.sqrt(s + eps)

    def _to_tokens(v):
        B_, C_, H_, W_ = v.shape
        return v.reshape(B_, C_, H_ * W_).transpose(0, 2, 1)

    def _from_tokens(t, like):
        B_, C_, H_, W_ = like.shape
        return t.transpose(0, 2, 1).reshape(B_, C_, H_, W_)
    x = _L0_conv_ref(x, L0_conv_wq, L0_conv_bq, L0_conv_wk, L0_conv_bk, L0_conv_wv, L0_conv_bv)
    x = _L1_conv_ref(x, L1_conv_w_off, L1_conv_b_off, L1_conv_w_dcn, L1_conv_b_dcn, L1_conv_gamma, L1_conv_beta, L1_conv_running_mean, L1_conv_running_var)
    x = _L2_conv_ref(x, L2_conv_wq, L2_conv_bq, L2_conv_wk, L2_conv_bk, L2_conv_wv, L2_conv_bv, L2_conv_wp, L2_conv_bp)
    x = _L3_conv_ref(x, L3_conv_ln1_w, L3_conv_ln1_b, L3_conv_dw_w, L3_conv_dw_b, L3_conv_lr_dw_w, L3_conv_lr_dw_b, L3_conv_lr_g_w, L3_conv_lr_g_b, L3_conv_rl_dw_w, L3_conv_rl_dw_b, L3_conv_rl_g_w, L3_conv_rl_g_b, L3_conv_tb_dw_w, L3_conv_tb_dw_b, L3_conv_tb_g_w, L3_conv_tb_g_b, L3_conv_bt_dw_w, L3_conv_bt_dw_b, L3_conv_bt_g_w, L3_conv_bt_g_b, L3_conv_fuse_w, L3_conv_fuse_b, L3_conv_ln2_w, L3_conv_ln2_b, L3_conv_ff1_w, L3_conv_ff1_b, L3_conv_ff2_w, L3_conv_ff2_b)
    return x

_drawn_inputs = setup_inputs


def setup_inputs(seed=0):
    import zlib

    import numpy as np

    out = dict(_drawn_inputs(seed))
    spreads = {'L1_conv_b_off': (0.0, 0.1),
     'L1_conv_b_dcn': (0.0, 0.1),
     'L1_conv_gamma': (1.0, 0.2),
     'L1_conv_beta': (0.0, 0.1),
     'L2_conv_bq': (0.0, 0.8),
     'L2_conv_bk': (0.0, 2.0),
     'L2_conv_bv': (0.0, 0.1),
     'L2_conv_bp': (0.0, 0.1),
     'L3_conv_ln1_w': (1.0, 0.6),
     'L3_conv_ln1_b': (0.0, 0.8),
     'L3_conv_dw_b': (0.0, 0.8),
     'L3_conv_lr_dw_b': (0.0, 0.452),
     'L3_conv_lr_g_b': (0.0, 2.0),
     'L3_conv_rl_dw_b': (0.0, 0.438),
     'L3_conv_rl_g_b': (0.0, 0.8),
     'L3_conv_tb_dw_b': (0.0, 0.557),
     'L3_conv_tb_g_b': (0.0, 2.0),
     'L3_conv_bt_dw_b': (0.0, 0.409),
     'L3_conv_bt_g_b': (0.0, 2.0),
     'L3_conv_fuse_b': (0.0, 0.1),
     'L3_conv_ln2_w': (1.0, 0.6),
     'L3_conv_ln2_b': (0.0, 2.0),
     'L3_conv_ff1_b': (0.0, 0.277),
     'L3_conv_ff2_b': (0.0, 0.1)}
    factors = {'L0_conv_bq': 3.028,
     'L0_conv_bk': 3.297,
     'L2_conv_wq': 8.0,
     'L2_conv_wk': 8.0,
     'L3_conv_dw_w': 8.0,
     'L3_conv_lr_dw_w': 8.0,
     'L3_conv_lr_g_w': 8.0,
     'L3_conv_rl_dw_w': 8.0,
     'L3_conv_rl_g_w': 8.0,
     'L3_conv_tb_dw_w': 8.0,
     'L3_conv_tb_g_w': 8.0,
     'L3_conv_bt_dw_w': 8.0,
     'L3_conv_bt_g_w': 8.0}
    for name, (base, spread) in spreads.items():
        noise = np.random.default_rng([zlib.crc32(name.encode()), seed]).standard_normal(out[name].shape)
        drawn = base * np.exp(spread * noise) if base else spread * noise
        out[name] = jnp.asarray(drawn.astype(out[name].dtype))
    for name, factor in factors.items():
        out[name] = (out[name] * factor).astype(out[name].dtype)
    return out
```

```python
from contextlib import ExitStack

import numpy as np

import concourse.bass as bass
from concourse import mybir

F32 = mybir.dt.float32
F16 = mybir.dt.float16
ALU = mybir.AluOpType
ACT = mybir.ActivationFunctionType
AX_X = mybir.AxisListType.X

IMAGES, C, H, W = 16, 64, 16, 16
PIX = H * W
PAIRS = IMAGES // 2
P = 128
HALVES = PIX // P
HALF_ROWS = H // HALVES
TAPS = 9
AXES = 2 * TAPS
OM = 32
GROUPS = 5
SLOT = 2 * H
SCANS, KS = 4, 5
HID = 2 * C
PW = W + 2
SW = W + 4
UNIT = float(2 ** 12)
BN_EPS, LN_EPS = 1e-5, 1e-6
QK_SCALE = float(C) ** -0.5

PARTS = [
    ("ident", P), ("qk_w", 2 * P), ("qk_b", 2 * P), ("av_w", P + 1), ("off_w", TAPS * 2 * OM), ("off_b", 1),
    ("base", 4 * AXES), ("iota", H), ("dcn_w", TAPS * P), ("bn", 5), ("q_w", P), ("k_w", P), ("v_w", P),
    ("p_w", P), ("v_b", P), ("q_b", 1), ("k_b", 1), ("p_b", 1), ("ln1", 2), ("dw_w", TAPS), ("dw_b", 1),
    ("scan_w", SCANS * KS), ("scan_b", SCANS), ("gate_w", SCANS * P), ("gate_b", SCANS), ("fuse_w", P),
    ("fuse_b", 1), ("ln2", 2), ("ff1_w", 2 * HID), ("ff1_b", 2), ("ff2_w", C), ("ff2_b", 1),
]
AT, PACK = {}, 0
for _name, _n in PARTS:
    AT[_name] = (PACK, PACK + _n)
    PACK += _n
EARLY = AT["dcn_w"][0]

SLOTS = 2 * TAPS
PLAN_A = {0: ["qk"], 1: ["attn"], 2: ["attn_norm"], 3: ["attn_t"], 4: ["mix"], 5: ["x1"], 7: ["off"],
          8: ["off_t"], 9: ["hat"], 11: ["abs"], 12: ["hat_y"], 13: ["split"], 15: ["tr0"], 16: ["tr1"],
          17: ["tr2"]}
PLAN_B = {1: ["qk2"], 2: ["v2"], 3: ["logit0"], 4: ["soft0"], 5: ["logit1", "nrm0"], 6: ["soft1"],
          7: ["et0", "nrm1"], 8: ["et1"], 10: ["av"], 11: ["x3"], 12: ["ln1"], 13: ["dw"], 15: ["gate0"],
          16: ["gate1"]}
PLAN_C = {0: ["scan3", "scan0"], 1: ["scan1"], 2: ["scan2"], 3: ["gated"], 4: ["scan_end"], 6: ["fuse"],
          7: ["ln2"], 9: ["ff0"], 10: ["u0"], 12: ["ff1"], 13: ["u1"], 14: ["ff2"]}


def program(nc, x, par, sel, out):
    ctx = ExitStack()
    with ctx:
        def sb(name, shape, dt=F32):
            return ctx.enter_context(nc.sbuf_tensor("sb_" + name, shape, dt))

        def bank(name):
            return ctx.enter_context(nc.psum_tensor("ps_" + name, [P, 512], F32))

        def sem(name):
            return ctx.enter_context(nc.semaphore(name))

        par_sb = sb("par", [P, PACK])
        sel_sb = sb("sel", [P, 7 * P], F16)
        diag = sb("diag", [P, TAPS, P])
        half = sb("half", [P, 1])
        bn_s = sb("bn_s", [P, 5])
        fuse_h = sb("fuse_h", [P, P])
        ff2_h = sb("ff2_h", [P, C])
        gate_bh = sb("gate_bh", [P, SCANS])
        ff1_bh = sb("ff1_bh", [P, 1])
        x_in = sb("x_in", [P, PIX])
        qk_sb = sb("qk", [P, HALVES, 2, 2, C])
        a_max = sb("a_max", [P, 1])
        a_neg = sb("a_neg", [P, 1])
        a_exp = sb("a_exp", [P, C])
        a_sum = sb("a_sum", [P, 1])
        a_rec = sb("a_rec", [P, 1])
        a_nrm = sb("a_nrm", [P, C])
        at_sb = sb("at", [C, P])
        mix = sb("mix", [P, P])
        mix_b = sb("mix_b", [P, 1])
        x1 = sb("x1", [P, PIX])
        x1_pad = sb("x1_pad", [P, H + 2, PW])
        off = sb("off", [P, P])
        pos = sb("pos", [P, 4 * AXES])
        msk = sb("msk", [P, 4, TAPS])
        dist = sb("dist", [P, 4 * AXES, H])
        hat = sb("hat", [P, 4, AXES, H])
        parts = sb("parts", [P, 4, 4 * GROUPS, 2, H], F16)
        hats = sb("hats", [P, GROUPS, 2 * PIX], F16)
        x1t = sb("x1t", [P, HALVES, P])
        xe = [sb(f"xe{i}", [P, 2 * PIX]) for i in range(2)]
        wt = [[sb(f"wt{i}{h}", [P, 2 * PIX]) for h in range(HALVES)] for i in range(2)]
        smp = [sb(f"smp{i}", [P, PIX]) for i in range(2)]
        x2 = sb("x2", [P, PIX])
        q2 = sb("q2", [P, PIX])
        k2 = sb("k2", [P, PIX])
        v2 = sb("v2", [P, HALVES, P])
        b_max = [sb(f"b_max{b}", [P, HALVES]) for b in range(2)]
        b_neg = [sb(f"b_neg{b}", [P, HALVES]) for b in range(2)]
        b_sum = [sb(f"b_sum{b}", [P, HALVES]) for b in range(2)]
        b_rec = [sb(f"b_rec{b}", [P, HALVES]) for b in range(2)]
        b_exp = [sb(f"b_exp{b}", [P, HALVES, PIX]) for b in range(2)]
        b_nrm = [sb(f"b_nrm{b}", [P, HALVES, PIX]) for b in range(2)]
        e_t = [sb(f"e_t{b}", [P, HALVES, PIX]) for b in range(2)]
        att2 = sb("att2", [P, PIX])
        x3 = sb("x3", [P, PIX])
        st1, mv1, sc1 = sb("st1", [P, 6]), sb("mv1", [P, 2]), sb("sc1", [P, 4])
        z_pad = sb("z_pad", [P, H + 2, PW])
        y_pad = sb("y_pad", [P, H + 4, SW])
        gates = sb("gates", [P, SCANS, PIX])
        acc = [[sb(f"acc{d}{i}", [P, PIX]) for i in range(2)] for d in range(SCANS)]
        prod = [sb(f"prod{d}", [P, PIX]) for d in range(SCANS)]
        g_tmp = [sb(f"g_tmp{i}", [P, PIX]) for i in range(2)]
        o_a, o_b, o_sum = sb("o_a", [P, PIX]), sb("o_b", [P, PIX]), sb("o_sum", [P, PIX])
        x3c = sb("x3c", [P, PIX])
        x4 = sb("x4", [P, PIX])
        st2, mv2, sc2 = sb("st2", [P, 6]), sb("mv2", [P, 2]), sb("sc2", [P, 4])
        z2 = sb("z2", [P, PIX])
        ff_a = [sb(f"ff_a{b}", [P, PIX]) for b in range(2)]
        ff_g = [sb(f"ff_g{b}", [P, PIX]) for b in range(2)]
        ff_u = [sb(f"ff_u{b}", [P, PIX]) for b in range(2)]
        y_out = sb("y_out", [P, PIX])

        def part(name, rows=P):
            a, b = AT[name]
            return par_sb[0:rows, a:b]

        def col(name, i=0):
            a = AT[name][0] + i
            return par_sb[:, a:a + 1]

        def image(ap):
            return ap.rearrange("p (h w) -> p h w", h=H)

        yb = [bank(f"yb{h}") for h in range(HALVES)]
        xb = bank("xb")
        sm = [bank(f"sm{i}") for i in range(2)]
        cv = bank("cv")
        ma = bank("ma")
        mb = bank("mb")
        ma16 = ma[:, :].bitcast(F16)

        par_in, par_late, sel_in = sem("par_in"), sem("par_late"), sem("sel_in")
        diag_ok, zero_ok, half_ok = sem("diag_ok"), sem("zero_ok"), sem("half_ok")
        prep_act, bn_step = sem("prep_act"), sem("bn_step")
        x_loaded, stored = sem("x_loaded"), sem("stored")
        S = {}

        def ev(name):
            if name not in S:
                S[name] = sem(name)
            return S[name]

        names_a = ["qk_mm", "qk_ok", "attn_mm", "a_max_ok", "a_neg_ok", "a_exp_ok", "a_rec_ok", "a_nrm_ok",
                   "at_mm", "at_ok", "mix_mm", "mix_ok", "x1_mm", "x1_ok", "x1_pad_ok", "off_mm", "off_ok",
                   "pos_mm", "pos_ok", "tanh_ok", "msk_ok", "dist_ok", "abs_ok", "hat_ok", "hat_y_ok",
                   "high_ok", "low_ok", "tr_mm0", "tr_mm1", "tr_mm2", "hats_ok0", "hats_ok1", "hats_ok2",
                   "x1t_mm", "x1t_ok"]
        names_m = ["xb_mm", "xe_ok", "smp_mm", "smp_ok", "conv_mm", "yb_mm", "wt_ok", "x2_ok"]
        names_b = ["qk2_mm", "qk2_ok", "v2_mm", "v2_ok", "av_mm", "av_ok", "x3_mm", "x3_ok", "st1_ok", "mv1_ok",
                   "var1_ok", "rstd1_ok", "g1_ok", "h1_ok", "z_ok", "dw_mm", "y_ok", "gate_mm0", "gate_mm1",
                   "gate_ok0", "gate_ok1", "o_a", "o_b", "o_ok"]
        names_b += [f"scan{d}" for d in range(SCANS)]
        names_b += [f"prod{d}" for d in range(SCANS)] + ["term"]
        names_b += [f"{e}{b}" for b in range(2) for e in ("logit_mm", "max_ok", "neg_ok", "exp_ok", "rec_ok",
                                                         "nrm_ok", "et_mm", "et_ok")]
        names_c = ["fuse_mm", "x4_ok", "st2_ok", "mv2_ok", "var2_ok", "rstd2_ok", "g2_ok", "h2_ok", "z2_ok",
                   "ff_mm0", "ff_mm1", "ff_act0", "ff_act1", "ff_u0", "ff_u1", "out_mm", "y_out_ok"]
        for name in names_a + names_m + names_b + names_c:
            ev(name)

        def tap(n, k):
            return n * TAPS - TAPS + (k + 1)

        def slot(n, s):
            return n * SLOTS - SLOTS + (s + 1)

        def scan_count(n, j):
            return n * KS - KS + (j + 1)

        def wait_past(eng, semaphore, value):
            if not isinstance(value, int) or value > 0:
                eng.wait_ge(semaphore, value)

        def settle(eng):
            eng.wait_ge(par_in, 16)

        def schedule(eng, iteration):
            iteration(0, True, False, False, False)
            iteration(1, True, True, False, False)
            iteration(2, True, True, True, False)
            iteration(3, True, True, True, True)
            with eng.Fori(4, PAIRS) as n:
                iteration(n, True, True, True, True)
            iteration(PAIRS, False, True, True, True)
            iteration(PAIRS + 1, False, False, True, True)
            iteration(PAIRS + 2, False, False, False, True)

        def walk(eng, steps_a, steps_b, steps_c, main, n, do_a, do_m, do_b, do_c, last_a=None):
            after, before, before2 = n + 1, n - 1, n - 2
            if not isinstance(n, int):
                for value in (after, before, before2):
                    eng.lower_val(value)
            for s in range(SLOTS):
                if do_m:
                    main(n, s)
                for step in PLAN_C.get(s, ()):
                    if do_c and step in steps_c:
                        steps_c[step](before2, before if do_b else before2)
                for step in PLAN_A.get(s, ()):
                    if do_a and step in steps_a:
                        steps_a[step](after)
                for step in PLAN_B.get(s, ()):
                    if do_b and step in steps_b:
                        steps_b[step](before)
            if do_m:
                main(n, SLOTS)
            if do_a and last_a:
                last_a(after)

        block = ctx.enter_context(nc.Block())

        @block.sync
        def _(sp):
            sp.dma_start(par_sb[:, 0:EARLY], par[:, 0:EARLY]).then_inc(par_in, 16)
            sp.dma_start(x_in[:, :], x[0, :, :]).then_inc(x_loaded, 16)
            sp.dma_start(sel_sb[:, :], sel[:, :]).then_inc(sel_in, 16)
            sp.dma_start(par_sb[:, EARLY:PACK], par[:, EARLY:PACK]).then_inc(par_late, 16)

            def load(n):
                sp.wait_ge(ev("x1_ok"), n)
                sp.dma_start(x_in[:, :], x[n, :, :]).then_inc(x_loaded, 16)

            def store(n):
                sp.wait_ge(ev("y_out_ok"), n)
                sp.dma_start(out[n - 1, :, :], y_out[:, :]).then_inc(stored, 16)

            for n in range(1, 4):
                load(n)
            with sp.Fori(4, PAIRS) as n:
                store(n - 3)
                load(n)
            for n in range(PAIRS - 3, PAIRS + 1):
                store(n)
            sp.wait_ge(stored, 16 * PAIRS)

        @block.tensor
        def _(pe):
            ident = part("ident")
            ident16 = sel_sb[:, 0:P]

            def qk(n):
                pe.wait_ge(x_loaded, 16 * n)
                pe.wait_ge(ev("x1t_ok"), n - 1)
                for h in range(HALVES):
                    mm = nc.tensor.matmul(ma[:, 2 * P * h:2 * P * (h + 1)], x_in[:, P * h:P * (h + 1)],
                                          part("qk_w"), start=True, stop=True)
                mm.then_inc(ev("qk_mm"), 1)

            def attn(n):
                pe.wait_ge(ev("qk_ok"), n)
                for h in range(HALVES):
                    for b in range(2):
                        mm = nc.tensor.matmul(ma[C * b:C * (b + 1), 0:C], qk_sb[:, h, b, 0, :], qk_sb[:, h, b, 1, :],
                                              start=(h == 0), stop=(h == HALVES - 1))
                mm.then_inc(ev("attn_mm"), 1)

            def attn_t(n):
                settle(pe)
                pe.wait_ge(ev("a_nrm_ok"), n)
                nc.tensor.transpose(ma[0:C, 0:P], a_nrm[:, :], ident).then_inc(ev("at_mm"), 1)

            def mix_step(n):
                pe.wait_ge(ev("at_ok"), n)
                a, b = AT["av_w"]
                nc.tensor.matmul(ma[:, 0:P], par_sb[0:C, a:b - 1], at_sb[:, :], start=True, stop=True)
                nc.tensor.matmul(ma[:, P:P + 1], at_sb[:, :], par_sb[0:C, b - 1:b], start=True, stop=True)\
                    .then_inc(ev("mix_mm"), 1)

            def x1_step(n):
                pe.wait_ge(ev("mix_ok"), n)
                nc.tensor.matmul(ma[:, 0:PIX], mix[:, :], x_in[:, :], start=True, stop=True).then_inc(ev("x1_mm"), 1)

            def off_step(n):
                pe.wait_ge(ev("x1_pad_ok"), n)
                pe.wait_ge(ev("x1_ok"), n)
                a = AT["off_w"][0]
                for t in range(TAPS):
                    for h in range(HALVES):
                        r = t // 3 + HALF_ROWS * h
                        mm = nc.tensor.matmul(ma[C * h:C * (h + 1), 0:P],
                                              par_sb[:, a + 2 * OM * t:a + 2 * OM * (t + 1)],
                                              x1_pad[:, r:r + HALF_ROWS, t % 3:t % 3 + W],
                                              start=(t == 0), stop=(t == TAPS - 1))
                mm.then_inc(ev("off_mm"), 1)

            def off_t(n):
                pe.wait_ge(ev("off_ok"), n)
                nc.tensor.transpose(ma[:, 0:P], off[:, :], ident).then_inc(ev("pos_mm"), 1)

            def tr(g0, g1, index):
                def step(n):
                    if index == 0:
                        pe.wait_ge(ev("high_ok"), n)
                        pe.wait_ge(ev("low_ok"), n)
                        pe.wait_ge(ev("tanh_ok"), n)
                    else:
                        pe.wait_ge(ev(f"hats_ok{index - 1}"), n)
                    for g in range(g0, g1):
                        for b in range(2):
                            for h in range(HALVES):
                                at = 2 * PIX * (g - g0) + PIX * b + P * h
                                mm = nc.tensor.transpose(ma16[:, at:at + P], parts[:, 2 * h + b, 4 * g:4 * g + 4, :, :],
                                                         ident16)
                    mm.then_inc(ev(f"tr_mm{index}"), 1)
                return step

            def x1_t(n):
                pe.wait_ge(ev("hats_ok2"), n)
                pe.wait_ge(ev("x1_ok"), n)
                for h in range(HALVES):
                    mm = nc.tensor.transpose(ma[:, P * h:P * (h + 1)], x1[:, P * h:P * (h + 1)], ident)
                mm.then_inc(ev("x1t_mm"), 1)

            def spread(n, s):
                k, h = divmod(s, 2)
                g, odd = divmod(k, 2)
                if h == 0:
                    if k % 4 == 0:
                        pe.wait_ge(ev(f"hats_ok{k // 4}"), n)
                    wait_past(pe, ev("xe_ok"), tap(n, k - 1))
                    nc.tensor.matmul(xb[:, :], sel_sb[:, P * (1 + odd):P * (2 + odd)], hats[:, g, :],
                                     start=True, stop=True).then_inc(ev("xb_mm"), 1)
                wait_past(pe, ev("wt_ok"), slot(n, s - 2))
                nc.tensor.matmul(yb[h][:, :], sel_sb[:, P * (3 + 2 * odd + h):P * (4 + 2 * odd + h)], hats[:, g, :],
                                 start=True, stop=True).then_inc(ev("yb_mm"), 1)

            def conv(n, k):
                pe.wait_ge(ev("smp_ok"), tap(n, k))
                if k == 0:
                    pe.wait_ge(ev("x2_ok"), n - 1)
                a = AT["dcn_w"][0] + P * k
                nc.tensor.matmul(cv[:, 0:PIX], par_sb[:, a:a + P], smp[k % 2][:, :],
                                 start=(k == 0), stop=(k == TAPS - 1)).then_inc(ev("conv_mm"), 1)

            def main(n, s):
                if s == SLOTS:
                    conv(n, TAPS - 1)
                    return
                k, h = divmod(s, 2)
                if s == 0:
                    spread(n, 0)
                    spread(n, 1)
                if s + 2 < SLOTS:
                    spread(n, s + 2)
                if s == 0:
                    pe.wait_ge(ev("x1t_ok"), n)
                pe.wait_ge(ev("wt_ok"), slot(n, s))
                if h == 0:
                    wait_past(pe, ev("smp_ok"), tap(n, k - 2))
                for b in range(2):
                    mm = nc.tensor.matmul(sm[k % 2][C * b:C * (b + 1), 0:PIX], x1t[:, h, C * b:C * (b + 1)],
                                          wt[k % 2][h][:, PIX * b:PIX * (b + 1)], start=(h == 0), stop=(h == HALVES - 1))
                if h == 1:
                    mm.then_inc(ev("smp_mm"), 1)
                if h == 0 and k >= 1:
                    conv(n, k - 1)

            def qk2(n):
                pe.wait_ge(ev("x2_ok"), n)
                pe.wait_ge(ev("gate_ok1"), n - 1)
                nc.tensor.matmul(mb[:, 0:PIX], part("q_w"), x2[:, :], start=True, stop=True)
                nc.tensor.matmul(mb[:, PIX:2 * PIX], part("k_w"), x2[:, :], start=True, stop=True)\
                    .then_inc(ev("qk2_mm"), 1)

            def v2_step(n):
                pe.wait_ge(ev("qk2_ok"), n)
                for h in range(HALVES):
                    mm = nc.tensor.matmul(mb[:, P * h:P * (h + 1)], x2[:, P * h:P * (h + 1)], part("v_w"),
                                          start=True, stop=True)
                mm.then_inc(ev("v2_mm"), 1)

            def logit(b):
                def step(n):
                    if b == 0:
                        pe.wait_ge(ev("v2_ok"), n)
                    else:
                        pe.wait_ge(ev("exp_ok0"), n)
                    for h in range(HALVES):
                        mm = nc.tensor.matmul(mb[:, PIX * h:PIX * (h + 1)], q2[C * b:C * (b + 1), P * h:P * (h + 1)],
                                              k2[C * b:C * (b + 1), :], start=True, stop=True)
                    mm.then_inc(ev(f"logit_mm{b}"), 1)
                return step

            def e_transpose(b):
                def step(n):
                    pe.wait_ge(ev(f"nrm_ok{b}"), n)
                    if b == 0:
                        pe.wait_ge(ev("exp_ok1"), n)
                        pe.wait_ge(ev("x4_ok"), n - 1)
                    else:
                        pe.wait_ge(ev("et_ok0"), n)
                    for j in range(HALVES):
                        for h in range(HALVES):
                            mm = nc.tensor.transpose(mb[:, PIX * j + P * h:PIX * j + P * (h + 1)],
                                                     b_nrm[b][:, h, P * j:P * (j + 1)], ident)
                    mm.then_inc(ev(f"et_mm{b}"), 1)
                return step

            def av(n):
                pe.wait_ge(ev("et_ok1"), n)
                pe.wait_ge(ev("ff_act0"), n - 1)
                for j in range(HALVES):
                    for b in range(2):
                        mm = nc.tensor.matmul(mb[C * b:C * (b + 1), 0:PIX], v2[:, j, C * b:C * (b + 1)],
                                              e_t[b][:, j, :], start=(j == 0), stop=(j == HALVES - 1))
                mm.then_inc(ev("av_mm"), 1)

            def x3_step(n):
                pe.wait_ge(ev("av_ok"), n)
                nc.tensor.matmul(mb[:, 0:PIX], part("p_w"), att2[:, :], start=True, stop=True)\
                    .then_inc(ev("x3_mm"), 1)

            def dw(n):
                pe.wait_ge(ev("z_ok"), n)
                pe.wait_ge(ev("x3_ok"), n)
                pe.wait_ge(ev("ff_act1"), n - 1)
                for t in range(TAPS):
                    mm = nc.tensor.matmul(mb[:, 0:PIX], diag[:, t, :], z_pad[:, t // 3:t // 3 + H, t % 3:t % 3 + W],
                                          start=(t == 0), stop=(t == TAPS - 1))
                mm.then_inc(ev("dw_mm"), 1)

            def gate(i):
                def step(n):
                    if i == 0:
                        pe.wait_ge(ev("y_ok"), n)
                        pe.wait_ge(ev("y_out_ok"), n - 1)
                    else:
                        pe.wait_ge(ev("gate_ok0"), n)
                    for j in range(2):
                        a = AT["gate_w"][0] + P * (2 * i + j)
                        mm = nc.tensor.matmul(mb[:, PIX * j:PIX * (j + 1)], par_sb[:, a:a + P],
                                              y_pad[:, 2:2 + H, 2:2 + W], start=True, stop=True)
                    mm.then_inc(ev(f"gate_mm{i}"), 1)
                return step

            def fuse(n, nb):
                pe.wait_ge(ev("o_ok"), n)
                pe.wait_ge(ev("exp_ok1"), nb)
                nc.tensor.matmul(mb[:, 0:PIX], fuse_h[:, :], o_sum[:, :], start=True, stop=True)\
                    .then_inc(ev("fuse_mm"), 1)

            def ff(b):
                def step(n, nb):
                    pe.wait_ge(ev("z2_ok"), n)
                    pe.wait_ge(ev("et_ok1" if b == 0 else "x3_ok"), nb)
                    if b == 1:
                        pe.wait_ge(ev("ff_act0"), n)
                    a = AT["ff1_w"][0]
                    for j in range(2):
                        mm = nc.tensor.matmul(mb[:, PIX * j:PIX * (j + 1)],
                                              par_sb[C * b:C * (b + 1), a + HID * j:a + HID * (j + 1)],
                                              z2[C * b:C * (b + 1), :], start=True, stop=True)
                    mm.then_inc(ev(f"ff_mm{b}"), 1)
                return step

            def ff2(n, nb):
                pe.wait_ge(ev("y_ok"), nb)
                pe.wait_ge(ev("ff_u0"), n)
                pe.wait_ge(ev("ff_u1"), n)
                for b in range(2):
                    mm = nc.tensor.matmul(mb[C * b:C * (b + 1), 0:PIX], ff2_h[:, :], ff_u[b][:, :],
                                          start=True, stop=True)
                mm.then_inc(ev("out_mm"), 1)

            steps_a = {"qk": qk, "attn": attn, "attn_t": attn_t, "mix": mix_step, "x1": x1_step, "off": off_step,
                       "off_t": off_t, "tr0": tr(0, 2, 0), "tr1": tr(2, 4, 1), "tr2": tr(4, 5, 2)}
            steps_b = {"qk2": qk2, "v2": v2_step, "logit0": logit(0), "logit1": logit(1), "et0": e_transpose(0),
                       "et1": e_transpose(1), "av": av, "x3": x3_step, "dw": dw, "gate0": gate(0),
                       "gate1": gate(1)}
            steps_c = {"fuse": fuse, "ff0": ff(0), "ff1": ff(1), "ff2": ff2}

            def iteration(n, do_a, do_m, do_b, do_c):
                walk(pe, steps_a, steps_b, steps_c, main, n, do_a, do_m, do_b, do_c, x1_t)

            pe.wait_ge(par_in, 16)
            pe.wait_ge(sel_in, 16)
            pe.wait_ge(par_late, 16)
            pe.wait_ge(diag_ok, TAPS)
            pe.wait_ge(prep_act, 4)
            schedule(pe, iteration)

        @block.scalar
        def _(act):
            def attn(n):
                act.wait_ge(ev("a_neg_ok"), n)
                nc.scalar.activation(a_exp[:, :], ma[:, 0:C], ACT.Exp, bias=a_neg[:, 0:1], scale=QK_SCALE,
                                     accum_out=a_sum[:, 0:1]).then_inc(ev("a_exp_ok"), 1)

            def attn_t(n):
                act.wait_ge(ev("at_mm"), n)
                nc.scalar.activation(at_sb[:, :], ma[0:C, 0:P], ACT.Copy).then_inc(ev("at_ok"), 1)

            def mix_step(n):
                act.wait_ge(ev("mix_mm"), n)
                for b in range(2):
                    r = slice(C * b, C * (b + 1))
                    nc.scalar.activation(mix[r, r], ma[r, r], ACT.Copy)
                nc.scalar.activation(mix_b[:, :], ma[:, P:P + 1], ACT.Copy).then_inc(ev("mix_ok"), 1)

            def off_step(n):
                act.wait_ge(ev("off_mm"), n)
                nc.scalar.activation(off[:, :], ma[:, 0:P], ACT.Identity, bias=col("off_b"))\
                    .then_inc(ev("off_ok"), 1)

            def off_t(n):
                act.wait_ge(ev("pos_ok"), n)
                nc.scalar.activation(msk[:, :, :], ma[:, 0:4 * OM].rearrange("p (g m) -> p g m", m=OM)[:, :, AXES:AXES + TAPS],
                                     ACT.Tanh, scale=0.5).then_inc(ev("tanh_ok"), 1)

            def hat_step(n):
                act.wait_ge(ev("dist_ok"), n)
                nc.scalar.activation(hat[:, :, :, :].rearrange("p g a i -> p (g a i)"),
                                     dist[:, :, :].rearrange("p a i -> p (a i)"), ACT.Abs).then_inc(ev("abs_ok"), 1)

            def split(n):
                act.wait_ge(ev("hat_y_ok"), n)
                act.wait_ge(ev("tr_mm2"), n - 1)
                nc.scalar.activation(parts[:, :, 0:AXES, 0, :], hat[:, :, :, :], ACT.Copy)\
                    .then_inc(ev("high_ok"), 1)

            def tr(g0, g1, index):
                def step(n):
                    act.wait_ge(ev(f"tr_mm{index}"), n)
                    k = 2 * PIX * (g1 - g0)
                    nc.scalar.activation(hats[:, g0:g1, :].rearrange("p g q -> p (g q)"), ma16[:, 0:k], ACT.Copy)\
                        .then_inc(ev(f"hats_ok{index}"), 1)
                return step

            def x1_t(n):
                act.wait_ge(ev("x1t_mm"), n)
                nc.scalar.activation(x1t[:, :, :].rearrange("p h c -> p (h c)"), ma[:, 0:PIX], ACT.Copy)\
                    .then_inc(ev("x1t_ok"), 1)

            def samples(n, k):
                act.wait_ge(ev("smp_mm"), tap(n, k))
                nc.scalar.activation(smp[k % 2][:, :], sm[k % 2][:, 0:PIX], ACT.Copy, scale=0.5 / UNIT / UNIT)\
                    .then_inc(ev("smp_ok"), 1)

            def columns(n, k):
                act.wait_ge(ev("xb_mm"), tap(n, k))
                wait_past(act, ev("wt_ok"), slot(n, 2 * k - 3))
                nc.scalar.activation(xe[k % 2][:, :], xb[:, :], ACT.Copy).then_inc(ev("xe_ok"), 1)

            def main(n, s):
                if s == SLOTS:
                    samples(n, TAPS - 1)
                    act.wait_ge(ev("conv_mm"), tap(n, TAPS - 1))
                    nc.scalar.activation(x2[:, :], cv[:, 0:PIX], ACT.Relu, bias=bn_s[:, 3:4], scale=bn_s[:, 2:3])\
                        .then_inc(ev("x2_ok"), 1)
                    return
                k, h = divmod(s, 2)
                if s == 0:
                    columns(n, 0)
                if h == 0 and k >= 1:
                    samples(n, k - 1)
                if h == 0 and k + 1 < TAPS:
                    columns(n, k + 1)

            def qk2(n):
                act.wait_ge(ev("qk2_mm"), n)
                nc.scalar.activation(q2[:, :], mb[:, 0:PIX], ACT.Identity, bias=col("q_b"))
                nc.scalar.activation(k2[:, :], mb[:, PIX:2 * PIX], ACT.Identity, bias=col("k_b"))\
                    .then_inc(ev("qk2_ok"), 1)

            def soft(b):
                def step(n):
                    act.wait_ge(ev(f"neg_ok{b}"), n)
                    for h in range(HALVES):
                        last = nc.scalar.activation(b_exp[b][:, h, :], mb[:, PIX * h:PIX * (h + 1)], ACT.Exp,
                                                    bias=b_neg[b][:, h:h + 1], scale=QK_SCALE,
                                                    accum_out=b_sum[b][:, h:h + 1])
                    last.then_inc(ev(f"exp_ok{b}"), 1)
                return step

            def e_transpose(b):
                def step(n):
                    act.wait_ge(ev(f"et_mm{b}"), n)
                    nc.scalar.activation(e_t[b][:, :, :].rearrange("p j i -> p (j i)"), mb[:, :], ACT.Copy)\
                        .then_inc(ev(f"et_ok{b}"), 1)
                return step

            def av(n):
                act.wait_ge(ev("av_mm"), n)
                nc.scalar.activation(att2[:, :], mb[:, 0:PIX], ACT.Copy).then_inc(ev("av_ok"), 1)

            def dw(n):
                act.wait_ge(ev("dw_mm"), n)
                nc.scalar.activation(y_pad[:, 2:2 + H, 2:2 + W], image(mb[:, 0:PIX]), ACT.Identity,
                                     bias=col("dw_b")).then_inc(ev("y_ok"), 1)

            def gate(i):
                def step(n):
                    act.wait_ge(ev(f"gate_mm{i}"), n)
                    for j in range(2):
                        d = 2 * i + j
                        last = nc.scalar.activation(gates[:, d, :], mb[:, PIX * j:PIX * (j + 1)], ACT.Tanh,
                                                    bias=gate_bh[:, d:d + 1], scale=0.5)
                    last.then_inc(ev(f"gate_ok{i}"), 1)
                return step

            def ff(b):
                def step(n, nb):
                    act.wait_ge(ev(f"ff_mm{b}"), n)
                    nc.scalar.activation(ff_a[b][:, :], mb[:, 0:PIX], ACT.Identity, bias=col("ff1_b", 0))
                    nc.scalar.activation(ff_g[b][:, :], mb[:, PIX:2 * PIX], ACT.Tanh, bias=ff1_bh[:, 0:1], scale=0.5)\
                        .then_inc(ev(f"ff_act{b}"), 1)
                return step

            steps_a = {"attn": attn, "attn_t": attn_t, "mix": mix_step, "off": off_step, "off_t": off_t,
                       "abs": hat_step, "split": split, "tr0": tr(0, 2, 0), "tr1": tr(2, 4, 1), "tr2": tr(4, 5, 2)}
            steps_b = {"qk2": qk2, "soft0": soft(0), "soft1": soft(1), "et0": e_transpose(0), "et1": e_transpose(1),
                       "av": av, "dw": dw, "gate0": gate(0), "gate1": gate(1)}
            steps_c = {"ff0": ff(0), "ff1": ff(1)}

            def iteration(n, do_a, do_m, do_b, do_c):
                walk(act, steps_a, steps_b, steps_c, main, n, do_a, do_m, do_b, do_c, x1_t)

            act.wait_ge(par_late, 16)
            nc.scalar.mul(fuse_h[:, :], part("fuse_w"), 0.5).then_inc(prep_act, 1)
            nc.scalar.mul(ff2_h[:, :], part("ff2_w"), 0.5).then_inc(prep_act, 1)
            nc.scalar.mul(gate_bh[:, :], part("gate_b"), 0.5).then_inc(prep_act, 1)
            nc.scalar.mul(ff1_bh[:, :], col("ff1_b", 1), 0.5).then_inc(prep_act, 1)
            act.wait_ge(prep_act, 4)
            act.wait_ge(par_in, 16)
            act.wait_ge(bn_step, 5)
            act.wait_ge(zero_ok, 4)
            schedule(act, iteration)

        @block.vector
        def _(dve):
            def qk(n):
                dve.wait_ge(ev("qk_mm"), n)
                nc.vector.tensor_tensor(qk_sb[:, :, :, :, :].rearrange("p h b k c -> p h (b k c)"),
                                        ma[:, :].rearrange("p (h c) -> p h c", h=HALVES),
                                        part("qk_b").unsqueeze(1).to_broadcast([P, HALVES, 2 * P]),
                                        ALU.add).then_inc(ev("qk_ok"), 1)

            def attn(n):
                dve.wait_ge(ev("attn_mm"), n)
                nc.vector.tensor_reduce(a_max[:, :], ma[:, 0:C], AX_X, ALU.max).then_inc(ev("a_max_ok"), 1)
                dve.wait_ge(ev("a_max_ok"), n)
                nc.vector.tensor_scalar(a_neg[:, :], a_max[:, :], -QK_SCALE, None, ALU.mult)\
                    .then_inc(ev("a_neg_ok"), 1)

            def attn_norm(n):
                dve.wait_ge(ev("a_exp_ok"), n)
                nc.vector.reciprocal(a_rec[:, :], a_sum[:, :]).then_inc(ev("a_rec_ok"), 1)
                dve.wait_ge(ev("a_rec_ok"), n)
                nc.vector.tensor_scalar(a_nrm[:, :], a_exp[:, :], a_rec[:, 0:1], None, ALU.mult)\
                    .then_inc(ev("a_nrm_ok"), 1)

            def x1_step(n):
                dve.wait_ge(ev("x1_mm"), n)
                nc.vector.scalar_tensor_tensor(out=x1[:, :], in0=ma[:, 0:PIX], scalar=mix_b[:, 0:1], in1=x_in[:, :],
                                               op0=ALU.add, op1=ALU.add).then_inc(ev("x1_ok"), 1)

            def off_t(n):
                dve.wait_ge(ev("pos_mm"), n)
                nc.vector.scalar_tensor_tensor(
                    out=pos[:, :].rearrange("p (g a) -> p g a", g=4),
                    in0=ma[:, 0:4 * OM].rearrange("p (g m) -> p g m", m=OM)[:, :, 0:AXES], scalar=UNIT,
                    in1=part("base").rearrange("p (g a) -> p g a", g=4), op0=ALU.mult, op1=ALU.add)\
                    .then_inc(ev("pos_ok"), 1)

            def hat_step(n):
                dve.wait_ge(ev("tanh_ok"), n)
                nc.vector.tensor_scalar(msk[:, :, :], msk[:, :, :], 1.0, None, ALU.add).then_inc(ev("msk_ok"), 1)

            def hat_y(n):
                dve.wait_ge(ev("abs_ok"), n)
                nc.vector.tensor_scalar(hat[:, :, :, :], hat[:, :, :, :], UNIT, 0.0, ALU.subtract, ALU.min)\
                    .then_inc(ev("hat_ok"), 1)
                dve.wait_ge(ev("hat_ok"), n)
                dve.wait_ge(ev("msk_ok"), n)
                for g in range(4):
                    rows = hat[:, g, 0:AXES:2, :]
                    last = nc.vector.tensor_tensor(rows, rows, msk[:, g, :].unsqueeze(2).to_broadcast([P, TAPS, H]),
                                                   ALU.mult)
                last.then_inc(ev("hat_y_ok"), 1)

            def main(n, s):
                if s == 0:
                    weights(n, 0)
                if s + 1 < SLOTS:
                    weights(n, s + 1)

            def weights(n, s):
                k, h = divmod(s, 2)
                dve.wait_ge(ev("yb_mm"), slot(n, s))
                if h == 0:
                    dve.wait_ge(ev("xe_ok"), tap(n, k))
                nc.vector.tensor_tensor(wt[k % 2][h][:, :], yb[h][:, :], xe[k % 2][:, :], ALU.mult)\
                    .then_inc(ev("wt_ok"), 1)

            def v2_step(n):
                dve.wait_ge(ev("v2_mm"), n)
                nc.vector.tensor_tensor(v2[:, :, :], mb[:, 0:PIX].rearrange("p (h c) -> p h c", h=HALVES),
                                        part("v_b").unsqueeze(1).to_broadcast([P, HALVES, P]), ALU.add)\
                    .then_inc(ev("v2_ok"), 1)

            def logit(b):
                def step(n):
                    dve.wait_ge(ev(f"logit_mm{b}"), n)
                    nc.vector.tensor_reduce(b_max[b][:, :], mb[:, :].rearrange("p (h j) -> p h j", h=HALVES), AX_X,
                                            ALU.max).then_inc(ev(f"max_ok{b}"), 1)
                    dve.wait_ge(ev(f"max_ok{b}"), n)
                    nc.vector.tensor_scalar(b_neg[b][:, :], b_max[b][:, :], -QK_SCALE, None, ALU.mult)\
                        .then_inc(ev(f"neg_ok{b}"), 1)
                return step

            def soft(b):
                def step(n):
                    dve.wait_ge(ev(f"exp_ok{b}"), n)
                    nc.vector.reciprocal(b_rec[b][:, :], b_sum[b][:, :]).then_inc(ev(f"rec_ok{b}"), 1)
                    dve.wait_ge(ev(f"rec_ok{b}"), n)
                    for h in range(HALVES):
                        last = nc.vector.tensor_scalar(b_nrm[b][:, h, :], b_exp[b][:, h, :], b_rec[b][:, h:h + 1], None,
                                                       ALU.mult)
                    last.then_inc(ev(f"nrm_ok{b}"), 1)
                return step

            def stats(src, st, mv, n, st_ok, mv_ok):
                nc.vector.bn_stats(st[:, :], src[:, :]).then_inc(ev(st_ok), 1)
                settle(dve)
                dve.wait_ge(ev(st_ok), n)
                nc.vector.bn_aggr(mv[:, :], st[:, :]).then_inc(ev(mv_ok), 1)

            def x3_step(n):
                dve.wait_ge(ev("x3_mm"), n)
                nc.vector.scalar_tensor_tensor(out=x3[:, :], in0=mb[:, 0:PIX], scalar=col("p_b"), in1=x2[:, :],
                                               op0=ALU.add, op1=ALU.add).then_inc(ev("x3_ok"), 1)
                dve.wait_ge(ev("x3_ok"), n)
                stats(x3, st1, mv1, n, "st1_ok", "mv1_ok")

            def ln1(n):
                dve.wait_ge(ev("h1_ok"), n)
                nc.vector.tensor_scalar(z_pad[:, 1:1 + H, 1:1 + W], image(x3[:, :]), sc1[:, 2:3], sc1[:, 3:4],
                                        ALU.mult, ALU.subtract).then_inc(ev("z_ok"), 1)

            def window(d, j):
                return y_pad[:, 2:2 + H, j:j + W] if d < 2 else y_pad[:, j:j + H, 2:2 + W]

            def scan_conv(n, d, base):
                a = d * KS
                nc.vector.tensor_scalar(image(acc[d][0][:, :]), window(d, 0), col("scan_w", a), col("scan_b", d),
                                        ALU.mult, ALU.add).then_inc(ev(f"scan{d}"), 1)
                for j in range(1, KS):
                    dve.wait_ge(ev(f"scan{d}"), scan_count(n, j - 1))
                    nc.vector.scalar_tensor_tensor(out=image(acc[d][j % 2][:, :]), in0=window(d, j),
                                                   scalar=col("scan_w", a + j), in1=image(acc[d][(j - 1) % 2][:, :]),
                                                   op0=ALU.mult, op1=ALU.add).then_inc(ev(f"scan{d}"), 1)

            def gated(n, d):
                dve.wait_ge(ev(f"scan{d}"), scan_count(n, KS - 1))
                dve.wait_ge(ev(f"gate_ok{d // 2}"), n)
                nc.vector.scalar_tensor_tensor(out=prod[d][:, :], in0=gates[:, d, :], scalar=1.0,
                                               in1=acc[d][(KS - 1) % 2][:, :], op0=ALU.add, op1=ALU.mult)\
                    .then_inc(ev(f"prod{d}"), 1)

            def scan(d):
                def step(n, nb):
                    if d == 0:
                        dve.wait_ge(ev("y_ok"), n)
                    scan_conv(n, d, 0)
                return step

            def gated_all(n, nb):
                gated(n, 0)
                gated(n, 1)
                gated(n, 2)
                gated(n, 3)

            def fuse(n, nb):
                dve.wait_ge(ev("fuse_mm"), n)
                nc.vector.scalar_tensor_tensor(out=x4[:, :], in0=mb[:, 0:PIX], scalar=col("fuse_b"), in1=x3[:, :],
                                               op0=ALU.add, op1=ALU.add).then_inc(ev("x4_ok"), 1)
                dve.wait_ge(ev("x4_ok"), n)
                stats(x4, st2, mv2, n, "st2_ok", "mv2_ok")

            def ln2(n, nb):
                dve.wait_ge(ev("h2_ok"), n)
                nc.vector.tensor_scalar(z2[:, :], x4[:, :], sc2[:, 2:3], sc2[:, 3:4], ALU.mult, ALU.subtract)\
                    .then_inc(ev("z2_ok"), 1)

            def ff(b):
                def step(n, nb):
                    dve.wait_ge(ev(f"ff_act{b}"), n)
                    nc.vector.scalar_tensor_tensor(out=ff_u[b][:, :], in0=ff_g[b][:, :], scalar=1.0, in1=ff_a[b][:, :],
                                                   op0=ALU.add, op1=ALU.mult).then_inc(ev(f"ff_u{b}"), 1)
                return step

            def ff2(n, nb):
                dve.wait_ge(ev("out_mm"), n)
                dve.wait_ge(stored, 16 * n - 16)
                nc.vector.scalar_tensor_tensor(out=y_out[:, :], in0=mb[:, 0:PIX], scalar=col("ff2_b"), in1=x4[:, :],
                                               op0=ALU.add, op1=ALU.add).then_inc(ev("y_out_ok"), 1)

            steps_a = {"qk": qk, "attn": attn, "attn_norm": attn_norm, "x1": x1_step, "off_t": off_t,
                       "hat": hat_step, "hat_y": hat_y}
            steps_b = {"v2": v2_step, "logit0": logit(0), "logit1": logit(1), "nrm0": soft(0), "nrm1": soft(1),
                       "x3": x3_step, "ln1": ln1}
            steps_c = {"scan0": scan(0), "scan1": scan(1), "scan2": scan(2), "gated": gated_all, "fuse": fuse,
                       "ln2": ln2, "u0": ff(0), "u1": ff(1), "ff2": ff2}

            def iteration(n, do_a, do_m, do_b, do_c):
                walk(dve, steps_a, steps_b, steps_c, main, n, do_a, do_m, do_b, do_c)

            nc.vector.memset(mix[:, :], 0.0).then_inc(zero_ok, 1)
            nc.vector.memset(z_pad[:, :, :], 0.0).then_inc(zero_ok, 1)
            nc.vector.memset(y_pad[:, :, :], 0.0).then_inc(zero_ok, 1)
            nc.vector.memset(parts[:, :, AXES:4 * GROUPS, :, :], 0.0).then_inc(zero_ok, 1)
            dve.wait_ge(zero_ok, 4)
            dve.wait_ge(par_in, 16)
            dve.wait_ge(par_late, 16)
            schedule(dve, iteration)

        @block.gpsimd
        def _(pool):
            def x1_step(n):
                settle(pool)
                pool.wait_ge(ev("x1_ok"), n)
                nc.gpsimd.tensor_copy(x1_pad[:, 1:1 + H, 1:1 + W], image(x1[:, :])).then_inc(ev("x1_pad_ok"), 1)

            def hat_step(n):
                pool.wait_ge(ev("pos_ok"), n)
                nc.gpsimd.tensor_tensor(dist[:, :, :], pos[:, :].unsqueeze(2).to_broadcast([P, 4 * AXES, H]),
                                        part("iota").unsqueeze(1).to_broadcast([P, 4 * AXES, H]), ALU.subtract)\
                    .then_inc(ev("dist_ok"), 1)

            def split(n):
                pool.wait_ge(ev("high_ok"), n)
                nc.gpsimd.tensor_tensor(parts[:, :, 0:AXES, 1, :], hat[:, :, :, :], parts[:, :, 0:AXES, 0, :],
                                        ALU.subtract).then_inc(ev("low_ok"), 1)

            def norm(src_mv, scl, gain, mv_ok, var_ok, rstd_ok, g_ok, h_ok):
                def step(n, *_):
                    settle(pool)
                    pool.wait_ge(ev(mv_ok), n)
                    nc.gpsimd.tensor_scalar(scl[:, 0:1], src_mv[:, 1:2], LN_EPS, 1.0, ALU.add, ALU.mult)\
                        .then_inc(ev(var_ok), 1)
                    pool.wait_ge(ev(var_ok), n)
                    nc.gpsimd.tensor_tensor(scl[:, 1:2], scl[:, 0:1], half[:, :], ALU.pow).then_inc(ev(rstd_ok), 1)
                    pool.wait_ge(ev(rstd_ok), n)
                    nc.gpsimd.tensor_tensor(scl[:, 2:3], scl[:, 1:2], col(gain, 0), ALU.mult).then_inc(ev(g_ok), 1)
                    settle(pool)
                    pool.wait_ge(ev(g_ok), n)
                    nc.gpsimd.tensor_scalar(scl[:, 3:4], src_mv[:, 0:1], scl[:, 2:3], col(gain, 1), ALU.mult,
                                            ALU.subtract).then_inc(ev(h_ok), 1)
                return step

            def scan3(n, nb):
                d = 3
                settle(pool)
                pool.wait_ge(ev("y_ok"), n)
                a = d * KS
                nc.gpsimd.tensor_scalar(image(acc[d][0][:, :]), y_pad[:, 0:H, 2:2 + W], col("scan_w", a),
                                        col("scan_b", d), ALU.mult, ALU.add).then_inc(ev(f"scan{d}"), 1)
                for j in range(1, KS):
                    nc.gpsimd.tensor_scalar(image(g_tmp[j % 2][:, :]), y_pad[:, j:j + H, 2:2 + W], col("scan_w", a + j),
                                            0.0, ALU.mult, ALU.add).then_inc(ev("term"), 1)
                    pool.wait_ge(ev("term"), n * (KS - 1) - (KS - 1) + j)
                    pool.wait_ge(ev(f"scan{d}"), scan_count(n, j - 1))
                    nc.gpsimd.tensor_tensor(acc[d][j % 2][:, :], acc[d][(j - 1) % 2][:, :], g_tmp[j % 2][:, :], ALU.add)\
                        .then_inc(ev(f"scan{d}"), 1)

            def scan_end(n, nb):
                pool.wait_ge(ev("prod1"), n)
                nc.gpsimd.tensor_tensor(o_a[:, :], prod[0][:, :], prod[1][:, :], ALU.add).then_inc(ev("o_a"), 1)
                pool.wait_ge(ev("prod3"), n)
                nc.gpsimd.tensor_tensor(o_b[:, :], prod[2][:, :], prod[3][:, :], ALU.add).then_inc(ev("o_b"), 1)
                pool.wait_ge(ev("o_b"), n)
                pool.wait_ge(ev("o_a"), n)
                nc.gpsimd.tensor_tensor(o_sum[:, :], o_a[:, :], o_b[:, :], ALU.add).then_inc(ev("o_ok"), 1)

            steps_a = {"x1": x1_step, "hat": hat_step, "split": split}
            steps_b = {"x3": norm(mv1, sc1, "ln1", "mv1_ok", "var1_ok", "rstd1_ok", "g1_ok", "h1_ok")}
            steps_c = {"fuse": norm(mv2, sc2, "ln2", "mv2_ok", "var2_ok", "rstd2_ok", "g2_ok", "h2_ok"),
                       "scan3": scan3, "scan_end": scan_end}

            def iteration(n, do_a, do_m, do_b, do_c):
                walk(pool, steps_a, steps_b, steps_c, lambda n, s: None, n, do_a, do_m, do_b, do_c)

            nc.gpsimd.memset(half[:, :], -0.5).then_inc(half_ok, 1)
            nc.gpsimd.memset(x1_pad[:, :, :], 0.0).then_inc(half_ok, 1)
            pool.wait_ge(par_in, 16)
            pool.wait_ge(par_late, 16)
            pool.wait_ge(half_ok, 2)
            nc.gpsimd.tensor_scalar(bn_s[:, 0:1], col("bn", 1), BN_EPS, 1.0, ALU.add, ALU.mult).then_inc(bn_step, 1)
            pool.wait_ge(bn_step, 1)
            nc.gpsimd.tensor_tensor(bn_s[:, 1:2], bn_s[:, 0:1], half[:, :], ALU.pow).then_inc(bn_step, 1)
            pool.wait_ge(bn_step, 2)
            nc.gpsimd.tensor_tensor(bn_s[:, 2:3], bn_s[:, 1:2], col("bn", 0), ALU.mult).then_inc(bn_step, 1)
            nc.gpsimd.tensor_tensor(bn_s[:, 4:5], col("bn", 4), col("bn", 2), ALU.subtract).then_inc(bn_step, 1)
            pool.wait_ge(bn_step, 4)
            nc.gpsimd.tensor_scalar(bn_s[:, 3:4], bn_s[:, 4:5], bn_s[:, 2:3], col("bn", 3), ALU.mult, ALU.add)\
                .then_inc(bn_step, 1)
            for t in range(TAPS):
                nc.gpsimd.tensor_scalar(diag[:, t, :], part("ident"), col("dw_w", t), 0.0, ALU.mult, ALU.add)\
                    .then_inc(diag_ok, 1)
            schedule(pool, iteration)


def _pack(a):
    f = np.float32
    wt = lambda w: np.ascontiguousarray(w.T)

    def twice(m):
        k, n = m.shape
        out = np.zeros((2, k, 2, n), f)
        out[0, :, 0], out[1, :, 1] = m, m
        return out.reshape(2 * k, 2 * n)

    def both(v):
        v = np.asarray(v).reshape(C, -1)
        return np.concatenate([v, v], 0)

    def spread(v):
        return np.broadcast_to(np.asarray(v).reshape(1, -1), (P, np.asarray(v).size))

    d = {"ident": np.eye(P, dtype=f)}
    d["qk_w"] = twice(np.concatenate([wt(a["L0_conv_wq"]), wt(a["L0_conv_wk"])], 1))
    d["qk_b"] = spread(np.concatenate([a["L0_conv_bq"], a["L0_conv_bk"]] * 2))
    wv, bv = a["L0_conv_wv"], a["L0_conv_bv"]
    d["av_w"] = np.concatenate([np.concatenate([wv, wv, bv[:, None]], 1), np.zeros((P - C, P + 1), f)], 0)
    w = np.zeros((TAPS, C, OM), f)
    w[:, :, 0:AXES + TAPS] = a["L1_conv_w_off"].reshape(AXES + TAPS, C, TAPS).transpose(2, 1, 0)
    d["off_w"] = np.concatenate([twice(w[t]) for t in range(TAPS)], 1)
    b = np.zeros((4, OM), f)
    b[:, 0:AXES + TAPS] = a["L1_conv_b_off"]
    d["off_b"] = b.reshape(P, 1)
    p, h, k = np.arange(P)[:, None, None], np.arange(HALVES)[None, :, None], np.arange(TAPS)[None, None, :]
    yx = np.stack([HALF_ROWS * h + p // W + k // 3 - 1 + 0 * k, p % W + k % 3 - 1 + 0 * h], -1)
    d["base"] = np.repeat(yx.reshape(P, HALVES, 1, AXES), 2, 2).reshape(P, 4 * AXES).astype(f) * f(UNIT)
    d["iota"] = spread(np.arange(H, dtype=f) * f(UNIT))
    w = a["L1_conv_w_dcn"].reshape(C, C, TAPS).transpose(2, 1, 0)
    d["dcn_w"] = np.concatenate([twice(w[t]) for t in range(TAPS)], 1)
    d["bn"] = np.concatenate([both(a["L1_conv_" + n]) for n in
                              ("gamma", "running_var", "running_mean", "beta", "b_dcn")], 1)
    for n in "qkvp":
        d[n + "_w"] = twice(wt(a["L2_conv_w" + n]))
        d[n + "_b"] = both(a["L2_conv_b" + n])
    d["v_b"] = spread(np.concatenate([a["L2_conv_bv"]] * 2))
    for n in ("1", "2"):
        d["ln" + n] = np.concatenate([both(a[f"L3_conv_ln{n}_w"]), both(a[f"L3_conv_ln{n}_b"])], 1)
    d["dw_w"] = both(a["L3_conv_dw_w"].reshape(TAPS, C).T)
    d["dw_b"] = both(a["L3_conv_dw_b"])
    taps = [a[f"L3_conv_{n}_dw_w"].reshape(KS, C)[::r] for n, r in (("lr", 1), ("rl", -1), ("tb", 1), ("bt", -1))]
    d["scan_w"] = both(np.concatenate(taps, 0).T)
    names = ("lr", "rl", "tb", "bt")
    d["scan_b"] = both(np.stack([a[f"L3_conv_{n}_dw_b"] for n in names], 1))
    d["gate_w"] = np.concatenate([twice(wt(a[f"L3_conv_{n}_g_w"])) for n in names], 1)
    d["gate_b"] = both(np.stack([a[f"L3_conv_{n}_g_b"] for n in names], 1))
    d["fuse_w"] = twice(wt(a["L3_conv_fuse_w"]))
    d["fuse_b"] = both(a["L3_conv_fuse_b"])
    w = wt(a["L3_conv_ff1_w"])
    d["ff1_w"] = np.concatenate([w, w], 0)
    d["ff1_b"] = a["L3_conv_ff1_b"].reshape(2, HID).T
    d["ff2_w"] = wt(a["L3_conv_ff2_w"])
    d["ff2_b"] = both(a["L3_conv_ff2_b"])
    return np.ascontiguousarray(np.concatenate([np.asarray(d[n], f).reshape(P, k) for n, k in PARTS], 1))


def _selectors():
    row = np.arange(P).reshape(4, 2, H, 1)
    slot, i = row // SLOT, row % H
    q = np.arange(P).reshape(1, 1, 1, P)
    out = [np.eye(P)]
    for odd in range(2):
        out.append(((slot == 2 * odd + 1) & (i == q % W)).reshape(P, P))
    for odd in range(2):
        for h in range(HALVES):
            out.append(((slot == 2 * odd) & (i == HALF_ROWS * h + q // W)).reshape(P, P))
    return np.ascontiguousarray(np.concatenate(out, 1).astype(np.float16))


def kernel(**inputs):
    import concourse.bacc as bacc
    from concourse.bass_utils import run_bass_kernel_spmd

    a = {k: np.asarray(v) for k, v in inputs.items()}
    arrays = {
        "in_x": np.ascontiguousarray(a["x"].reshape(PAIRS, P, PIX)),
        "in_par": _pack(a),
        "in_sel": _selectors(),
    }
    nc = bacc.Bacc("TRN2", target_bir_lowering=False, num_devices=1)
    args = [nc.dram_tensor(n, v.shape, mybir.dt.from_np(v.dtype), kind="ExternalInput").ap() for n, v in arrays.items()]
    args.append(nc.dram_tensor("out_y", (PAIRS, P, PIX), F32, kind="ExternalOutput").ap())
    program(nc, *args)
    r = run_bass_kernel_spmd(nc, [arrays], core_ids=[0])
    return np.asarray(r.results[0]["out_y"]).reshape(IMAGES, C, H, W)
```

```python
from contextlib import ExitStack

import numpy as np

import concourse.bass as bass
from concourse import mybir

F32 = mybir.dt.float32
F16 = mybir.dt.float16
ALU = mybir.AluOpType
ACT = mybir.ActivationFunctionType
AX_X = mybir.AxisListType.X

IMAGES, C, H, W = 16, 64, 16, 16
PIX = H * W
PAIRS = IMAGES // 2
P = 128
HALVES = PIX // P
HALF_ROWS = H // HALVES
TAPS = 9
AXES = 2 * TAPS
OM = 32
GROUPS = 5
SLOT = 2 * H
SCANS, KS = 4, 5
HID = 2 * C
PW = W + 2
SW = W + 4
UNIT = float(2 ** 12)
BN_EPS, LN_EPS = 1e-5, 1e-6
QK_SCALE = float(C) ** -0.5

PARTS = [
    ("qk_w", 2 * P), ("qk_b", 2 * P), ("ident", P), ("av_w", P + 1), ("off_w", TAPS * 2 * OM), ("off_b", 1),
    ("base", 4 * AXES), ("iota", H), ("dcn_w", TAPS * P), ("bn", 5), ("q_w", P), ("k_w", P), ("v_w", P),
    ("p_w", P), ("v_b", 1), ("q_b", 1), ("k_b", 1), ("p_b", 1), ("ln1", 2), ("dw_w", TAPS), ("dw_b", 1),
    ("scan_w", SCANS * KS), ("scan_b", SCANS), ("gate_w", SCANS * P), ("gate_b", SCANS), ("fuse_w", P),
    ("fuse_b", 1), ("ln2", 2), ("ff1_w", 2 * HID), ("ff1_b", 2), ("ff2_w", C), ("ff2_b", 1),
]
AT, PACK = {}, 0
for _name, _n in PARTS:
    AT[_name] = (PACK, PACK + _n)
    PACK += _n
FIRST = AT["av_w"][0]
EARLY = AT["dcn_w"][0]

SLOTS = 2 * TAPS
PLAN = {
    "pe": {0: ["qk"], 1: ["attn", "qk2"], 2: ["v2", "logit0"], 3: ["attn_t"], 4: ["mix", "logit1"], 5: ["x1"],
           6: ["fuse", "off", "et0"], 7: ["et1"], 8: ["off_t", "av"], 9: ["ff0"], 12: ["ff1"], 13: ["ff2"],
           15: ["tr0", "gate0"], 16: ["tr1", "gate1", "tr2"]},
    "act": {0: ["scan_first", "qk2"], 1: ["attn"], 2: ["v2"], 3: ["attn_t", "soft0"], 4: ["mix"], 5: ["soft1"],
            6: ["off", "et0"], 7: ["et1"], 8: ["ln2", "off_t", "ff0"], 10: ["abs"], 11: ["ln1"],
            12: ["dw_first", "ff1", "split"], 15: ["tr0", "gate0", "tr1"], 16: ["tr2"], 17: ["gate1"]},
    "dve": {1: ["qk", "scan_t1", "attn"], 2: ["scan_t2", "scan_t3", "scan_t4", "attn_norm"], 3: ["logit0", "gated0"],
            4: ["gated1", "gated3", "gated2", "scan_sum", "logit1"], 5: ["x1", "nrm0"], 6: ["fuse", "nrm1"],
            8: ["off_t"], 9: ["x3"], 10: ["hat", "u0"], 12: ["hat_y", "split"], 13: ["dw0", "u1", "dw1"],
            14: ["dw2", "ff2"]},
    "pool": {0: ["scan3"], 4: ["scan_end", "fuse"], 9: ["hat", "x3"], 13: ["split"]},
}
PLAN_END = {
    "pe": ["b.qk2", "b.v2", "b.logit0", "b.logit1", "b.et0", "b.et1", "c.fuse", "b.av", "c.ff0", "c.ff1", "c.ff2",
           "b.gate0", "b.gate1", "d.fuse", "d.ff0", "d.ff1", "d.ff2"],
    "act": ["b.qk2", "b.v2", "c.scan_first", "b.soft0", "b.soft1", "b.et0", "b.et1", "c.ln2", "b.ln1", "c.ff0",
            "b.dw_first", "c.ff1", "d.scan_first", "b.gate0", "b.gate1", "d.ln2", "d.ff0", "d.ff1"],
    "dve": ["c.scan_t1", "c.scan_t2", "b.logit0", "b.logit1", "b.nrm0", "b.nrm1", "c.scan_t3", "c.scan_t4",
            "c.gated0", "c.gated1", "c.gated3", "c.gated2", "c.scan_sum", "c.fuse", "b.x3", "b.dw0", "c.u0", "b.dw1",
            "c.u1", "b.dw2", "c.ff2", "d.scan_t1", "d.scan_t2", "d.scan_t3", "d.scan_t4", "d.gated0", "d.gated1",
            "d.gated2", "d.gated3", "d.scan_sum", "d.fuse", "d.u0", "d.u1", "d.ff2"],
    "pool": ["c.scan3", "c.scan_end", "c.fuse", "b.x3", "d.scan3", "d.scan_end", "d.fuse"],
}


def program(nc, x, par, sel, out):
    ctx = ExitStack()
    with ctx:
        def sb(name, shape, dt=F32):
            return ctx.enter_context(nc.sbuf_tensor("sb_" + name, shape, dt))

        def bank(name):
            return ctx.enter_context(nc.psum_tensor("ps_" + name, [P, 512], F32))

        def sem(name):
            return ctx.enter_context(nc.semaphore(name))

        par_sb = sb("par", [P, PACK])
        sel_sb = sb("sel", [P, 7 * P], F16)
        half = sb("half", [P, 1])
        bn_s = sb("bn_s", [P, 5])
        pv_w = sb("pv_w", [P, P])
        pv_b = sb("pv_b", [P, 1])
        fuse_h = sb("fuse_h", [P, P])
        ff2_h = sb("ff2_h", [P, C])
        gate_bh = sb("gate_bh", [P, SCANS])
        ff1_bh = sb("ff1_bh", [P, 1])
        x_in = sb("x_in", [P, PIX])
        qk_sb = sb("qk", [P, HALVES, 2, 2, C])
        a_max = sb("a_max", [P, 1])
        a_neg = sb("a_neg", [P, 1])
        a_exp = sb("a_exp", [P, C])
        a_sum = sb("a_sum", [P, 1])
        a_rec = sb("a_rec", [P, 1])
        a_nrm = sb("a_nrm", [P, C])
        at_sb = sb("at", [C, P])
        mix = sb("mix", [P, P])
        mix_b = sb("mix_b", [P, 1])
        x1 = sb("x1", [P, PIX])
        x1_pad = sb("x1_pad", [P, H + 2, PW])
        off = sb("off", [P, P])
        pos = sb("pos", [P, 4 * AXES])
        msk = sb("msk", [P, 4, TAPS])
        dist = sb("dist", [P, 4 * AXES, H])
        hat = sb("hat", [P, 4, AXES, H])
        parts = sb("parts", [P, 4, 4 * GROUPS, 2, H], F16)
        hats = sb("hats", [P, GROUPS, 2 * PIX], F16)
        x1t = sb("x1t", [P, HALVES, P])
        xe = [sb(f"xe{i}", [P, 2 * PIX]) for i in range(2)]
        wt = [[sb(f"wt{i}{h}", [P, 2 * PIX]) for h in range(HALVES)] for i in range(2)]
        smp = [sb(f"smp{i}", [P, PIX]) for i in range(2)]
        x2 = sb("x2", [P, PIX])
        q2 = sb("q2", [P, PIX])
        k2 = sb("k2", [P, PIX])
        v2 = sb("v2", [P, HALVES, P])
        b_max = [sb(f"b_max{b}", [P, HALVES]) for b in range(2)]
        b_neg = [sb(f"b_neg{b}", [P, HALVES]) for b in range(2)]
        b_sum = [sb(f"b_sum{b}", [P, HALVES]) for b in range(2)]
        b_rec = [sb(f"b_rec{b}", [P, HALVES]) for b in range(2)]
        b_exp = [sb(f"b_exp{b}", [P, HALVES, PIX]) for b in range(2)]
        b_dia = [sb(f"b_dia{b}", [P, HALVES, P]) for b in range(2)]
        e_t = [sb(f"e_t{b}", [P, HALVES, PIX]) for b in range(2)]
        x3 = sb("x3", [P, PIX])
        st1, mv1, sc1 = sb("st1", [P, 6]), sb("mv1", [P, 2]), sb("sc1", [P, 5])
        z_pad = sb("z_pad", [P, H + 2, PW])
        dw_acc = [sb(f"dw_acc{i}", [P, PIX]) for i in range(2)]
        y_pad = sb("y_pad", [P, H + 4, SW])
        gates = sb("gates", [P, SCANS, PIX])
        acc = [[sb(f"acc{d}{i}", [P, PIX]) for i in range(2)] for d in range(SCANS)]
        prod = [sb(f"prod{d}", [P, PIX]) for d in range(SCANS)]
        g_tmp = [sb(f"g_tmp{i}", [P, PIX]) for i in range(2)]
        o_a, o_b, o_sum = sb("o_a", [P, PIX]), sb("o_b", [P, PIX]), sb("o_sum", [P, PIX])
        x3c = sb("x3c", [P, PIX])
        x4 = sb("x4", [P, PIX])
        st2, mv2, sc2 = sb("st2", [P, 6]), sb("mv2", [P, 2]), sb("sc2", [P, 5])
        z2 = sb("z2", [P, PIX])
        ff_a = [sb(f"ff_a{b}", [P, PIX]) for b in range(2)]
        ff_g = [sb(f"ff_g{b}", [P, PIX]) for b in range(2)]
        ff_u = [sb(f"ff_u{b}", [P, PIX]) for b in range(2)]
        y_out = sb("y_out", [P, PIX])

        def part(name, rows=P):
            a, b = AT[name]
            return par_sb[0:rows, a:b]

        def col(name, i=0):
            a = AT[name][0] + i
            return par_sb[:, a:a + 1]

        def image(ap):
            return ap.rearrange("p (h w) -> p h w", h=H)

        def is_first(n):
            return isinstance(n, int) and n == 1

        def is_last(n):
            return isinstance(n, int) and n == PAIRS

        yb = [bank(f"yb{h}") for h in range(HALVES)]
        xb = bank("xb")
        sm = [bank(f"sm{i}") for i in range(2)]
        cv = bank("cv")
        ma = bank("ma")
        mb = bank("mb")

        def bank_of(step, n):
            if not is_last(n):
                return mb
            return {"qk2": cv, "v2": sm[0], "logit0": yb[0], "logit1": yb[1], "et0": xb, "et1": sm[1], "av": cv,
                    "gate0": yb[0], "gate1": yb[1], "fuse": xb, "ff0": sm[0], "ff1": sm[1], "ff2": cv}[step]

        def bank_tr(index, n):
            return (ma, mb, cv)[index] if is_first(n) else ma


        par_first, par_in, par_late, sel_in = sem("par_first"), sem("par_in"), sem("par_late"), sem("sel_in")
        zero_ok, half_ok = sem("zero_ok"), sem("half_ok")
        prep_mm, prep_act, bn_step = sem("prep_mm"), sem("prep_act"), sem("bn_step")
        x_loaded, stored = sem("x_loaded"), sem("stored")
        S = {}

        def ev(name):
            if name not in S:
                S[name] = sem(name)
            return S[name]

        names_a = ["qk_mm", "qk_ok", "attn_mm", "a_max_ok", "a_neg_ok", "a_exp_ok", "a_rec_ok", "a_nrm_ok",
                   "at_mm", "at_ok", "mix_mm", "mix_ok", "x1_mm", "x1_ok", "x1_pad_ok", "off_mm", "off_ok",
                   "pos_mm", "pos_ok", "tanh_ok", "msk_ok", "dist_ok", "abs_ok", "hat_ok", "hat_y_ok",
                   "high_ok", "low_ok", "tr_mm0", "tr_mm1", "tr_mm2", "hats_ok0", "hats_ok1", "hats_ok2",
                   "x1t_mm", "x1t_ok"]
        names_m = ["xb_mm", "xe_ok", "smp_mm", "smp_ok", "conv_mm", "yb_mm", "wt_ok", "x2_ok"]
        names_a += ["dist_ok_dve", "low_ok_dve"]
        names_b = ["qk2_mm", "qk2_ok", "v2_mm", "v2_ok", "x3_mm", "x3_ok", "st1_ok", "mv1_ok",
                   "var1_ok", "rstd1_ok", "g1_ok", "m1_ok", "h1_ok", "z_ok", "dw_step0", "dw_step1", "y_ok", "gate_mm0", "gate_mm1",
                   "gate_ok0", "gate_ok1", "o_a", "o_b", "o_ok"]
        names_b += [f"scan{d}" for d in range(SCANS)]
        names_b += [f"prod{d}" for d in range(SCANS)] + ["term"]
        names_b += [f"{e}{b}" for b in range(2) for e in ("logit_mm", "max_ok", "neg_ok", "exp_ok", "rec_ok",
                                                         "nrm_ok", "et_mm", "et_ok")]
        names_c = ["fuse_mm", "x4_ok", "st2_ok", "mv2_ok", "var2_ok", "rstd2_ok", "g2_ok", "m2_ok", "h2_ok", "z2_ok",
                   "ff_mm0", "ff_mm1", "ff_act0", "ff_act1", "ff_u0", "ff_u1", "out_mm", "y_out_ok"]
        for name in names_a + names_m + names_b + names_c:
            ev(name)

        def tap(n, k):
            return n * TAPS - TAPS + (k + 1)

        def slot(n, s):
            return n * SLOTS - SLOTS + (s + 1)

        def scan_count(n, j):
            return n * KS - KS + (j + 1)

        def dw_count(n, t):
            total = (TAPS + 1 - t % 2) // 2
            return n * total - total + (t // 2 + 1)

        def window(d, j):
            return y_pad[:, 2:2 + H, j:j + W] if d < 2 else y_pad[:, j:j + H, 2:2 + W]

        def dw_source(t):
            return z_pad[:, t // 3:t // 3 + H, t % 3:t % 3 + W]

        def wait_past(eng, semaphore, value):
            if not isinstance(value, int) or value > 0:
                eng.wait_ge(semaphore, value)

        def once(eng, n, first, semaphore, count):
            if isinstance(n, int) and n == first:
                eng.wait_ge(semaphore, count)

        def settle(eng):
            eng.wait_ge(par_first, 16)

        def schedule(eng, iteration):
            iteration(0, True, False, False, False)
            iteration(1, True, True, False, False)
            iteration(2, True, True, True, False)
            iteration(3, True, True, True, True)
            with eng.Fori(4, PAIRS) as n:
                iteration(n, True, True, True, True)
            iteration(PAIRS, False, True, True, True)

        def finish(plan_end, steps_b, steps_c):
            for entry in plan_end:
                chain, step = entry.split(".")
                if chain == "b":
                    steps_b[step](PAIRS)
                elif chain == "c":
                    steps_c[step](PAIRS - 1, PAIRS)
                else:
                    steps_c[step](PAIRS, PAIRS)

        def walk(eng, plan, steps_a, steps_b, steps_c, main, n, do_a, do_m, do_b, do_c, last_a, main_end=lambda n: None):
            after, before, before2 = n + 1, n - 1, n - 2
            if not isinstance(n, int):
                for value in (after, before, before2):
                    eng.lower_val(value)
            for s in range(SLOTS):
                if do_m:
                    main(n, s)
                for step in plan.get(s, ()):
                    if step in steps_a:
                        if do_a:
                            steps_a[step](after)
                    elif step in steps_b:
                        if do_b:
                            steps_b[step](before)
                    elif do_c:
                        steps_c[step](before2, before if do_b else before2)
            if do_m:
                main_end(n)
            if do_a:
                last_a(after)
            if do_m:
                main(n, SLOTS)

        block = ctx.enter_context(nc.Block())

        @block.sync
        def _(sp):
            sp.dma_start(par_sb[:, 0:FIRST], par[:, 0:FIRST]).then_inc(par_first, 16)
            sp.dma_start(x_in[:, :], x[0, :, :]).then_inc(x_loaded, 16)
            sp.dma_start(par_sb[:, FIRST:EARLY], par[:, FIRST:EARLY]).then_inc(par_in, 16)
            sp.dma_start(sel_sb[:, :], sel[:, :]).then_inc(sel_in, 16)
            sp.dma_start(par_sb[:, EARLY:PACK], par[:, EARLY:PACK]).then_inc(par_late, 16)

            def load(n):
                sp.wait_ge(ev("x1_pad_ok"), n)
                sp.dma_start(x_in[:, :], x[n, :, :]).then_inc(x_loaded, 16)

            def store(n):
                sp.wait_ge(ev("y_out_ok"), n)
                sp.dma_start(out[n - 1, :, :], y_out[:, :]).then_inc(stored, 16)

            for n in range(1, 4):
                load(n)
            with sp.Fori(4, PAIRS) as n:
                store(n - 3)
                load(n)
            for n in range(PAIRS - 3, PAIRS + 1):
                store(n)
            sp.wait_ge(stored, 16 * PAIRS)

        @block.tensor
        def _(pe):
            ident = part("ident")
            ident16 = sel_sb[:, 0:P]

            def qk(n):
                pe.wait_ge(x_loaded, 16 * n)
                pe.wait_ge(ev("x1t_ok"), n - 1)
                for h in range(HALVES):
                    mm = nc.tensor.matmul(ma[:, 2 * P * h:2 * P * (h + 1)], x_in[:, P * h:P * (h + 1)],
                                          part("qk_w"), start=True, stop=True)
                mm.then_inc(ev("qk_mm"), 1)

            def attn(n):
                pe.wait_ge(ev("qk_ok"), n)
                for h in range(HALVES):
                    for b in range(2):
                        mm = nc.tensor.matmul(ma[C * b:C * (b + 1), 0:C], qk_sb[:, h, b, 0, :], qk_sb[:, h, b, 1, :],
                                              start=(h == 0), stop=(h == HALVES - 1))
                mm.then_inc(ev("attn_mm"), 1)

            def attn_t(n):
                settle(pe)
                pe.wait_ge(ev("a_nrm_ok"), n)
                nc.tensor.transpose(ma[0:C, 0:P], a_nrm[:, :], ident).then_inc(ev("at_mm"), 1)

            def mix_step(n):
                once(pe, n, 1, par_in, 16)
                pe.wait_ge(ev("at_ok"), n)
                a, b = AT["av_w"]
                nc.tensor.matmul(ma[:, 0:P], par_sb[0:C, a:b - 1], at_sb[:, :], start=True, stop=True)
                nc.tensor.matmul(ma[:, P:P + 1], at_sb[:, :], par_sb[0:C, b - 1:b], start=True, stop=True)\
                    .then_inc(ev("mix_mm"), 1)

            def x1_step(n):
                pe.wait_ge(ev("mix_ok"), n)
                nc.tensor.matmul(ma[:, 0:PIX], mix[:, :], x_in[:, :], start=True, stop=True).then_inc(ev("x1_mm"), 1)

            def off_step(n):
                pe.wait_ge(ev("x1_pad_ok"), n)
                a = AT["off_w"][0]
                for t in range(TAPS):
                    for h in range(HALVES):
                        r = t // 3 + HALF_ROWS * h
                        mm = nc.tensor.matmul(ma[C * h:C * (h + 1), 0:P],
                                              par_sb[:, a + 2 * OM * t:a + 2 * OM * (t + 1)],
                                              x1_pad[:, r:r + HALF_ROWS, t % 3:t % 3 + W],
                                              start=(t == 0), stop=(t == TAPS - 1))
                mm.then_inc(ev("off_mm"), 1)

            def off_t(n):
                pe.wait_ge(ev("off_ok"), n)
                nc.tensor.transpose(ma[:, 0:P], off[:, :], ident).then_inc(ev("pos_mm"), 1)
                if is_first(n):
                    x1_t(n)

            def tr(g0, g1, index):
                def step(n):
                    if index == 0:
                        once(pe, n, 1, sel_in, 16)
                        pe.wait_ge(ev("high_ok"), n)
                        pe.wait_ge(ev("low_ok"), n)
                        once(pe, n, 1, ev("low_ok_dve"), 1)
                        pe.wait_ge(ev("tanh_ok"), n)
                    elif not is_first(n):
                        pe.wait_ge(ev(f"hats_ok{index - 1}"), n)
                    bk = bank_tr(index, n)[:, :].bitcast(F16)
                    for g in range(g0, g1):
                        for b in range(2):
                            for h in range(HALVES):
                                at = 2 * PIX * (g - g0) + PIX * b + P * h
                                mm = nc.tensor.transpose(bk[:, at:at + P], parts[:, 2 * h + b, 4 * g:4 * g + 4, :, :],
                                                         ident16)
                    mm.then_inc(ev(f"tr_mm{index}"), 1)
                return step

            def x1_t(n):
                bk = sm[0] if is_first(n) else ma
                if not is_first(n):
                    pe.wait_ge(ev("hats_ok2"), n)
                pe.wait_ge(ev("x1_ok"), n)
                for h in range(HALVES):
                    mm = nc.tensor.transpose(bk[:, P * h:P * (h + 1)], x1[:, P * h:P * (h + 1)], ident)
                mm.then_inc(ev("x1t_mm"), 1)

            def spread(n, s):
                k, h = divmod(s, 2)
                g, odd = divmod(k, 2)
                if h == 0:
                    if k % 4 == 0:
                        pe.wait_ge(ev(f"hats_ok{k // 4}"), n)
                    wait_past(pe, ev("xe_ok"), tap(n, k - 1))
                    nc.tensor.matmul(xb[:, :], sel_sb[:, P * (1 + odd):P * (2 + odd)], hats[:, g, :],
                                     start=True, stop=True).then_inc(ev("xb_mm"), 1)
                wait_past(pe, ev("wt_ok"), slot(n, s - 2))
                nc.tensor.matmul(yb[h][:, :], sel_sb[:, P * (3 + 2 * odd + h):P * (4 + 2 * odd + h)], hats[:, g, :],
                                 start=True, stop=True).then_inc(ev("yb_mm"), 1)

            def conv(n, k):
                pe.wait_ge(ev("smp_ok"), tap(n, k))
                if k == 0:
                    once(pe, n, 1, par_late, 16)
                    once(pe, n, 1, ev("hats_ok2"), 1)
                    pe.wait_ge(ev("x2_ok"), n - 1)
                a = AT["dcn_w"][0] + P * k
                nc.tensor.matmul(cv[:, 0:PIX], par_sb[:, a:a + P], smp[k % 2][:, :],
                                 start=(k == 0), stop=(k == TAPS - 1)).then_inc(ev("conv_mm"), 1)

            def main(n, s):
                if s == SLOTS:
                    conv(n, TAPS - 1)
                    return
                k, h = divmod(s, 2)
                if s + 2 < SLOTS:
                    spread(n, s + 2)
                if s == 0:
                    pe.wait_ge(ev("x1t_ok"), n)
                pe.wait_ge(ev("wt_ok"), slot(n, s))
                if h == 0:
                    wait_past(pe, ev("smp_ok"), tap(n, k - 2))
                for b in range(2):
                    mm = nc.tensor.matmul(sm[k % 2][C * b:C * (b + 1), 0:PIX], x1t[:, h, C * b:C * (b + 1)],
                                          wt[k % 2][h][:, PIX * b:PIX * (b + 1)], start=(h == 0), stop=(h == HALVES - 1))
                if h == 1:
                    mm.then_inc(ev("smp_mm"), 1)
                if h == 1 and k >= 1:
                    conv(n, k - 1)

            def qk2(n):
                bk = bank_of("qk2", n)
                pe.wait_ge(ev("x2_ok"), n)
                if not is_last(n):
                    pe.wait_ge(ev("gate_ok1"), n - 1)
                nc.tensor.matmul(bk[:, 0:PIX], part("q_w"), x2[:, :], start=True, stop=True)
                nc.tensor.matmul(bk[:, PIX:2 * PIX], part("k_w"), x2[:, :], start=True, stop=True)\
                    .then_inc(ev("qk2_mm"), 1)

            def v2_step(n):
                bk = bank_of("v2", n)
                if not is_last(n):
                    pe.wait_ge(ev("qk2_ok"), n)
                for h in range(HALVES):
                    mm = nc.tensor.matmul(bk[:, P * h:P * (h + 1)], x2[:, P * h:P * (h + 1)], pv_w[:, :],
                                          start=True, stop=True)
                mm.then_inc(ev("v2_mm"), 1)

            def logit(b):
                def step(n):
                    bk = bank_of(f"logit{b}", n)
                    if b == 0:
                        pe.wait_ge(ev("qk2_ok"), n)
                    if b == 0:
                        if not is_last(n):
                            pe.wait_ge(ev("v2_ok"), n)
                    else:
                        if not is_last(n):
                            pe.wait_ge(ev("exp_ok0"), n)
                    for h in range(HALVES):
                        mm = nc.tensor.matmul(bk[:, PIX * h:PIX * (h + 1)], q2[C * b:C * (b + 1), P * h:P * (h + 1)],
                                              k2[C * b:C * (b + 1), :], start=True, stop=True)
                    mm.then_inc(ev(f"logit_mm{b}"), 1)
                return step

            def e_transpose(b):
                def step(n):
                    bk = bank_of(f"et{b}", n)
                    pe.wait_ge(ev(f"nrm_ok{b}"), n)
                    if b == 0:
                        if not is_last(n):
                            pe.wait_ge(ev("exp_ok1"), n)
                            pe.wait_ge(ev("x4_ok"), n - 1)
                    else:
                        if not is_last(n):
                            pe.wait_ge(ev("et_ok0"), n)
                    for j in range(HALVES):
                        for h in range(HALVES):
                            mm = nc.tensor.matmul(bk[:, PIX * j + P * h:PIX * j + P * (h + 1)],
                                                  b_exp[b][:, h, P * j:P * (j + 1)], b_dia[b][:, h, :],
                                                  start=True, stop=True)
                    mm.then_inc(ev(f"et_mm{b}"), 1)
                return step

            def av(n):
                bk = bank_of("av", n)
                pe.wait_ge(ev("et_ok1"), n)
                pe.wait_ge(ev("v2_ok"), n)
                if not is_last(n):
                    pe.wait_ge(ev("et_ok1"), n)
                for j in range(HALVES):
                    for b in range(2):
                        mm = nc.tensor.matmul(bk[C * b:C * (b + 1), 0:PIX], v2[:, j, C * b:C * (b + 1)],
                                              e_t[b][:, j, :], start=(j == 0), stop=(j == HALVES - 1))
                mm.then_inc(ev("x3_mm"), 1)

            def gate(i):
                def step(n):
                    bk = bank_of(f"gate{i}", n)
                    if i == 0:
                        pe.wait_ge(ev("y_ok"), n)
                    if i == 0:
                        if not is_last(n):
                            pe.wait_ge(ev("x3_ok"), n)
                            pe.wait_ge(ev("y_out_ok"), n - 1)
                    else:
                        if not is_last(n):
                            pe.wait_ge(ev("gate_ok0"), n)
                    for j in range(2):
                        a = AT["gate_w"][0] + P * (2 * i + j)
                        mm = nc.tensor.matmul(bk[:, PIX * j:PIX * (j + 1)], par_sb[:, a:a + P],
                                              y_pad[:, 2:2 + H, 2:2 + W], start=True, stop=True)
                    mm.then_inc(ev(f"gate_mm{i}"), 1)
                return step

            def fuse(n, nb):
                bk = bank_of("fuse", n)
                pe.wait_ge(ev("o_ok"), n)
                if not is_last(n):
                    if is_last(nb):
                        pe.wait_ge(ev("gate_ok1"), n)
                    else:
                        pe.wait_ge(ev("exp_ok1"), nb)
                nc.tensor.matmul(bk[:, 0:PIX], fuse_h[:, :], o_sum[:, :], start=True, stop=True)\
                    .then_inc(ev("fuse_mm"), 1)

            def ff(b):
                def step(n, nb):
                    bk = bank_of(f"ff{b}", n)
                    pe.wait_ge(ev("z2_ok"), n)
                    if b == 0:
                        if not is_last(n):
                            pe.wait_ge(ev("x4_ok"), n)
                            if not is_last(nb):
                                pe.wait_ge(ev("x3_ok"), nb)
                    else:
                        if not is_last(n):
                            pe.wait_ge(ev("ff_act0"), n)
                    a = AT["ff1_w"][0]
                    for j in range(2):
                        mm = nc.tensor.matmul(bk[:, PIX * j:PIX * (j + 1)],
                                              par_sb[C * b:C * (b + 1), a + HID * j:a + HID * (j + 1)],
                                              z2[C * b:C * (b + 1), :], start=True, stop=True)
                    mm.then_inc(ev(f"ff_mm{b}"), 1)
                return step

            def ff2(n, nb):
                bk = bank_of("ff2", n)
                if not is_last(n):
                    pe.wait_ge(ev("ff_act1"), n)
                pe.wait_ge(ev("ff_u0"), n)
                pe.wait_ge(ev("ff_u1"), n)
                for b in range(2):
                    mm = nc.tensor.matmul(bk[C * b:C * (b + 1), 0:PIX], ff2_h[:, :], ff_u[b][:, :],
                                          start=True, stop=True)
                mm.then_inc(ev("out_mm"), 1)

            steps_a = {"qk": qk, "attn": attn, "attn_t": attn_t, "mix": mix_step, "x1": x1_step, "off": off_step,
                       "off_t": off_t, "tr0": tr(0, 2, 0), "tr1": tr(2, 4, 1), "tr2": tr(4, 5, 2)}
            steps_b = {"qk2": qk2, "v2": v2_step, "logit0": logit(0), "logit1": logit(1), "et0": e_transpose(0),
                       "et1": e_transpose(1), "av": av, "gate0": gate(0),
                       "gate1": gate(1)}
            steps_c = {"fuse": fuse, "ff0": ff(0), "ff1": ff(1), "ff2": ff2}

            def last_a(n):
                if not is_first(n):
                    x1_t(n)
                spread(n, 0)
                spread(n, 1)

            def prepare():
                pe.wait_ge(par_late, 16)
                pe.wait_ge(ev("hats_ok1"), 1)
                nc.tensor.matmul(mb[:, 0:P], part("v_w"), part("p_w"), start=True, stop=True)
                nc.tensor.matmul(mb[:, P:P + 1], part("p_w"), col("v_b"), start=True, stop=True).then_inc(prep_mm, 1)

            def iteration(n, do_a, do_m, do_b, do_c):
                if isinstance(n, int) and n == 1:
                    prepare()
                once(pe, n, 2, prep_act, 6)
                walk(pe, PLAN["pe"], steps_a, steps_b, steps_c, main, n, do_a, do_m, do_b, do_c, last_a)

            pe.wait_ge(par_first, 16)
            schedule(pe, iteration)
            finish(PLAN_END["pe"], steps_b, steps_c)

        @block.scalar
        def _(act):
            def attn(n):
                act.wait_ge(ev("a_neg_ok"), n)
                nc.scalar.activation(a_exp[:, :], ma[:, 0:C], ACT.Exp, bias=a_neg[:, 0:1], scale=QK_SCALE,
                                     accum_out=a_sum[:, 0:1]).then_inc(ev("a_exp_ok"), 1)

            def attn_t(n):
                act.wait_ge(ev("at_mm"), n)
                nc.scalar.activation(at_sb[:, :], ma[0:C, 0:P], ACT.Copy).then_inc(ev("at_ok"), 1)

            def mix_step(n):
                once(act, n, 1, zero_ok, 5)
                act.wait_ge(ev("mix_mm"), n)
                for b in range(2):
                    r = slice(C * b, C * (b + 1))
                    nc.scalar.activation(mix[r, r], ma[r, r], ACT.Copy)
                nc.scalar.activation(mix_b[:, :], ma[:, P:P + 1], ACT.Copy).then_inc(ev("mix_ok"), 1)

            def off_step(n):
                once(act, n, 1, par_in, 16)
                act.wait_ge(ev("off_mm"), n)
                nc.scalar.activation(off[:, :], ma[:, 0:P], ACT.Identity, bias=col("off_b"))\
                    .then_inc(ev("off_ok"), 1)

            def off_t(n):
                act.wait_ge(ev("pos_ok"), n)
                nc.scalar.activation(msk[:, :, :], ma[:, 0:4 * OM].rearrange("p (g m) -> p g m", m=OM)[:, :, AXES:AXES + TAPS],
                                     ACT.Tanh, scale=0.5).then_inc(ev("tanh_ok"), 1)
                if is_first(n):
                    x1_t(n)

            def hat_step(n):
                act.wait_ge(ev("dist_ok"), n)
                once(act, n, 1, ev("dist_ok_dve"), 1)
                nc.scalar.activation(hat[:, :, :, :].rearrange("p g a i -> p (g a i)"),
                                     dist[:, :, :].rearrange("p a i -> p (a i)"), ACT.Abs).then_inc(ev("abs_ok"), 1)

            def split(n):
                act.wait_ge(ev("hat_y_ok"), n)
                act.wait_ge(ev("tr_mm2"), n - 1)
                nc.scalar.activation(parts[:, :, 0:AXES, 0, :], hat[:, :, :, :], ACT.Copy)\
                    .then_inc(ev("high_ok"), 1)

            def tr(g0, g1, index):
                def step(n):
                    act.wait_ge(ev(f"tr_mm{index}"), n)
                    k = 2 * PIX * (g1 - g0)
                    bk = bank_tr(index, n)[:, :].bitcast(F16)
                    nc.scalar.activation(hats[:, g0:g1, :].rearrange("p g q -> p (g q)"), bk[:, 0:k], ACT.Copy)\
                        .then_inc(ev(f"hats_ok{index}"), 1)
                return step

            def x1_t(n):
                act.wait_ge(ev("x1t_mm"), n)
                nc.scalar.activation(x1t[:, :, :].rearrange("p h c -> p (h c)"),
                                     (sm[0] if is_first(n) else ma)[:, 0:PIX], ACT.Copy)\
                    .then_inc(ev("x1t_ok"), 1)

            def samples(n, k):
                act.wait_ge(ev("smp_mm"), tap(n, k))
                nc.scalar.activation(smp[k % 2][:, :], sm[k % 2][:, 0:PIX], ACT.Copy, scale=0.5 / UNIT / UNIT)\
                    .then_inc(ev("smp_ok"), 1)

            def columns(n, k):
                act.wait_ge(ev("xb_mm"), tap(n, k))
                wait_past(act, ev("wt_ok"), slot(n, 2 * k - 3))
                nc.scalar.activation(xe[k % 2][:, :], xb[:, :], ACT.Copy).then_inc(ev("xe_ok"), 1)

            def main(n, s):
                if s == SLOTS:
                    once(act, n, 1, bn_step, 5)
                    act.wait_ge(ev("conv_mm"), tap(n, TAPS - 1))
                    nc.scalar.activation(x2[:, :], cv[:, 0:PIX], ACT.Relu, bias=bn_s[:, 3:4], scale=bn_s[:, 2:3])\
                        .then_inc(ev("x2_ok"), 1)
                    return
                k, h = divmod(s, 2)
                if h == 0 and k >= 1:
                    samples(n, k - 1)
                if h == 0 and k + 1 < TAPS:
                    columns(n, k + 1)

            def qk2(n):
                bk = bank_of("qk2", n)
                act.wait_ge(ev("qk2_mm"), n)
                nc.scalar.activation(q2[:, :], bk[:, 0:PIX], ACT.Identity, bias=col("q_b"))
                nc.scalar.activation(k2[:, :], bk[:, PIX:2 * PIX], ACT.Identity, bias=col("k_b"))\
                    .then_inc(ev("qk2_ok"), 1)

            def soft(b):
                def step(n):
                    bk = bank_of(f"logit{b}", n)
                    act.wait_ge(ev(f"neg_ok{b}"), n)
                    for h in range(HALVES):
                        last = nc.scalar.activation(b_exp[b][:, h, :], bk[:, PIX * h:PIX * (h + 1)], ACT.Exp,
                                                    bias=b_neg[b][:, h:h + 1], scale=QK_SCALE,
                                                    accum_out=b_sum[b][:, h:h + 1])
                    last.then_inc(ev(f"exp_ok{b}"), 1)
                return step

            def e_transpose(b):
                def step(n):
                    bk = bank_of(f"et{b}", n)
                    act.wait_ge(ev(f"et_mm{b}"), n)
                    nc.scalar.activation(e_t[b][:, :, :].rearrange("p j i -> p (j i)"), bk[:, :], ACT.Copy)\
                        .then_inc(ev(f"et_ok{b}"), 1)
                return step

            def v2_step(n):
                bk = bank_of("v2", n)
                act.wait_ge(ev("v2_mm"), n)
                nc.scalar.activation(v2[:, :, :].rearrange("p h c -> p (h c)"), bk[:, 0:PIX], ACT.Copy)\
                    .then_inc(ev("v2_ok"), 1)

            def ln1(n):
                act.wait_ge(ev("h1_ok"), n)
                act.wait_ge(ev("y_ok"), n - 1)
                nc.scalar.activation(z_pad[:, 1:1 + H, 1:1 + W], image(x3[:, :]), ACT.Identity, bias=sc1[:, 3:4],
                                     scale=sc1[:, 2:3]).then_inc(ev("z_ok"), 1)

            def dw_first(n):
                act.wait_ge(ev("z_ok"), n)
                nc.scalar.activation(image(dw_acc[0][:, :]), dw_source(0), ACT.Identity, bias=col("dw_b"),
                                     scale=col("dw_w", 0)).then_inc(ev("dw_step0"), 1)
                nc.scalar.activation(image(dw_acc[1][:, :]), dw_source(1), ACT.Copy,
                                     scale=col("dw_w", 1)).then_inc(ev("dw_step1"), 1)

            def ln2(n, nb):
                act.wait_ge(ev("h2_ok"), n)
                nc.scalar.activation(z2[:, :], x4[:, :], ACT.Identity, bias=sc2[:, 3:4], scale=sc2[:, 2:3])\
                    .then_inc(ev("z2_ok"), 1)

            def scan_first(n, nb):
                act.wait_ge(ev("y_ok"), n)
                for d in range(SCANS):
                    act.wait_ge(ev(f"prod{d}"), n - 1)
                    nc.scalar.activation(image(acc[d][0][:, :]), window(d, 0), ACT.Identity, bias=col("scan_b", d),
                                         scale=col("scan_w", d * KS)).then_inc(ev(f"scan{d}"), 1)

            def gate(i):
                def step(n):
                    bk = bank_of(f"gate{i}", n)
                    act.wait_ge(ev(f"gate_mm{i}"), n)
                    for j in range(2):
                        d = 2 * i + j
                        last = nc.scalar.activation(gates[:, d, :], bk[:, PIX * j:PIX * (j + 1)], ACT.Tanh,
                                                    bias=gate_bh[:, d:d + 1], scale=0.5)
                    last.then_inc(ev(f"gate_ok{i}"), 1)
                return step

            def ff(b):
                def step(n, nb):
                    bk = bank_of(f"ff{b}", n)
                    act.wait_ge(ev(f"ff_mm{b}"), n)
                    nc.scalar.activation(ff_a[b][:, :], bk[:, 0:PIX], ACT.Identity, bias=col("ff1_b", 0))
                    nc.scalar.activation(ff_g[b][:, :], bk[:, PIX:2 * PIX], ACT.Tanh, bias=ff1_bh[:, 0:1], scale=0.5)\
                        .then_inc(ev(f"ff_act{b}"), 1)
                return step

            steps_a = {"attn": attn, "attn_t": attn_t, "mix": mix_step, "off": off_step, "off_t": off_t,
                       "abs": hat_step, "split": split, "tr0": tr(0, 2, 0), "tr1": tr(2, 4, 1), "tr2": tr(4, 5, 2)}
            steps_b = {"qk2": qk2, "soft0": soft(0), "soft1": soft(1), "et0": e_transpose(0), "et1": e_transpose(1),
                       "v2": v2_step, "gate0": gate(0), "gate1": gate(1), "ln1": ln1,
                       "dw_first": dw_first}
            steps_c = {"ff0": ff(0), "ff1": ff(1), "ln2": ln2, "scan_first": scan_first}

            def prepare():
                act.wait_ge(par_late, 16)
                nc.scalar.mul(fuse_h[:, :], part("fuse_w"), 0.5).then_inc(prep_act, 1)
                nc.scalar.mul(ff2_h[:, :], part("ff2_w"), 0.5).then_inc(prep_act, 1)
                nc.scalar.mul(gate_bh[:, :], part("gate_b"), 0.5).then_inc(prep_act, 1)
                nc.scalar.mul(ff1_bh[:, :], col("ff1_b", 1), 0.5).then_inc(prep_act, 1)
                act.wait_ge(prep_mm, 1)
                nc.scalar.activation(pv_w[:, :], mb[:, 0:P], ACT.Copy).then_inc(prep_act, 1)
                nc.scalar.activation(pv_b[:, :], mb[:, P:P + 1], ACT.Identity, bias=col("p_b")).then_inc(prep_act, 1)

            def iteration(n, do_a, do_m, do_b, do_c):
                if isinstance(n, int) and n == 1:
                    prepare()
                once(act, n, 2, prep_act, 6)
                walk(act, PLAN["act"], steps_a, steps_b, steps_c, main, n, do_a, do_m, do_b, do_c, last_a,
                     lambda n: samples(n, TAPS - 1))

            def last_a(n):
                if not is_first(n):
                    x1_t(n)
                columns(n, 0)

            schedule(act, iteration)
            finish(PLAN_END["act"], steps_b, steps_c)

        @block.vector
        def _(dve):
            def qk(n):
                dve.wait_ge(ev("qk_mm"), n)
                nc.vector.tensor_tensor(qk_sb[:, :, :, :, :].rearrange("p h b k c -> p h (b k c)"),
                                        ma[:, :].rearrange("p (h c) -> p h c", h=HALVES),
                                        part("qk_b").unsqueeze(1).to_broadcast([P, HALVES, 2 * P]),
                                        ALU.add).then_inc(ev("qk_ok"), 1)

            def attn(n):
                dve.wait_ge(ev("attn_mm"), n)
                nc.vector.tensor_reduce(a_max[:, :], ma[:, 0:C], AX_X, ALU.max).then_inc(ev("a_max_ok"), 1)
                dve.wait_ge(ev("a_max_ok"), n)
                nc.vector.tensor_scalar(a_neg[:, :], a_max[:, :], -QK_SCALE, None, ALU.mult)\
                    .then_inc(ev("a_neg_ok"), 1)

            def attn_norm(n):
                dve.wait_ge(ev("a_exp_ok"), n)
                nc.vector.reciprocal(a_rec[:, :], a_sum[:, :]).then_inc(ev("a_rec_ok"), 1)
                dve.wait_ge(ev("a_rec_ok"), n)
                nc.vector.tensor_scalar(a_nrm[:, :], a_exp[:, :], a_rec[:, 0:1], None, ALU.mult)\
                    .then_inc(ev("a_nrm_ok"), 1)

            def x1_step(n):
                dve.wait_ge(ev("x1_mm"), n)
                nc.vector.scalar_tensor_tensor(out=x1[:, :], in0=ma[:, 0:PIX], scalar=mix_b[:, 0:1], in1=x_in[:, :],
                                               op0=ALU.add, op1=ALU.add).then_inc(ev("x1_ok"), 1)
                nc.vector.scalar_tensor_tensor(out=x1_pad[:, 1:1 + H, 1:1 + W], in0=image(ma[:, 0:PIX]),
                                               scalar=mix_b[:, 0:1], in1=image(x_in[:, :]),
                                               op0=ALU.add, op1=ALU.add).then_inc(ev("x1_pad_ok"), 1)

            def off_t(n):
                once(dve, n, 1, par_in, 16)
                dve.wait_ge(ev("pos_mm"), n)
                nc.vector.scalar_tensor_tensor(
                    out=pos[:, :].rearrange("p (g a) -> p g a", g=4),
                    in0=ma[:, 0:4 * OM].rearrange("p (g m) -> p g m", m=OM)[:, :, 0:AXES], scalar=UNIT,
                    in1=part("base").rearrange("p (g a) -> p g a", g=4), op0=ALU.mult, op1=ALU.add)\
                    .then_inc(ev("pos_ok"), 1)

            def hat_step(n):
                if is_first(n):
                    a = 2 * AXES
                    dve.wait_ge(ev("pos_ok"), n)
                    nc.vector.tensor_tensor(dist[:, a:2 * a, :], pos[:, a:2 * a].unsqueeze(2).to_broadcast([P, a, H]),
                                            part("iota").unsqueeze(1).to_broadcast([P, a, H]), ALU.subtract)\
                        .then_inc(ev("dist_ok_dve"), 1)
                dve.wait_ge(ev("tanh_ok"), n)
                nc.vector.tensor_scalar(msk[:, :, :], msk[:, :, :], 1.0, None, ALU.add).then_inc(ev("msk_ok"), 1)

            def hat_y(n):
                dve.wait_ge(ev("abs_ok"), n)
                nc.vector.tensor_scalar(hat[:, :, :, :], hat[:, :, :, :], UNIT, 0.0, ALU.subtract, ALU.min)\
                    .then_inc(ev("hat_ok"), 1)
                dve.wait_ge(ev("hat_ok"), n)
                dve.wait_ge(ev("msk_ok"), n)
                for g in range(4):
                    rows = hat[:, g, 0:AXES:2, :]
                    last = nc.vector.tensor_tensor(rows, rows, msk[:, g, :].unsqueeze(2).to_broadcast([P, TAPS, H]),
                                                   ALU.mult)
                last.then_inc(ev("hat_y_ok"), 1)

            def split(n):
                if is_first(n):
                    dve.wait_ge(ev("high_ok"), n)
                    nc.vector.tensor_tensor(parts[:, 2:4, 0:AXES, 1, :], hat[:, 2:4, :, :], parts[:, 2:4, 0:AXES, 0, :],
                                            ALU.subtract).then_inc(ev("low_ok_dve"), 1)

            def main(n, s):
                if s + 1 < SLOTS:
                    weights(n, s + 1)

            def weights(n, s):
                k, h = divmod(s, 2)
                dve.wait_ge(ev("yb_mm"), slot(n, s))
                if h == 0:
                    dve.wait_ge(ev("xe_ok"), tap(n, k))
                nc.vector.tensor_tensor(wt[k % 2][h][:, :], yb[h][:, :], xe[k % 2][:, :], ALU.mult)\
                    .then_inc(ev("wt_ok"), 1)

            def logit(b):
                def step(n):
                    bk = bank_of(f"logit{b}", n)
                    dve.wait_ge(ev(f"logit_mm{b}"), n)
                    nc.vector.tensor_reduce(b_max[b][:, :], bk[:, :].rearrange("p (h j) -> p h j", h=HALVES), AX_X,
                                            ALU.max).then_inc(ev(f"max_ok{b}"), 1)
                    dve.wait_ge(ev(f"max_ok{b}"), n)
                    nc.vector.tensor_scalar(b_neg[b][:, :], b_max[b][:, :], -QK_SCALE, None, ALU.mult)\
                        .then_inc(ev(f"neg_ok{b}"), 1)
                return step

            def soft(b):
                def step(n):
                    dve.wait_ge(ev(f"exp_ok{b}"), n)
                    nc.vector.reciprocal(b_rec[b][:, :], b_sum[b][:, :]).then_inc(ev(f"rec_ok{b}"), 1)
                    dve.wait_ge(ev(f"rec_ok{b}"), n)
                    for h in range(HALVES):
                        last = nc.vector.tensor_scalar(b_dia[b][:, h, :], part("ident"), b_rec[b][:, h:h + 1], None,
                                                       ALU.mult)
                    last.then_inc(ev(f"nrm_ok{b}"), 1)
                return step

            def stats(src, st, mv, n, st_ok, mv_ok):
                nc.vector.bn_stats(st[:, :], src[:, :]).then_inc(ev(st_ok), 1)
                settle(dve)
                dve.wait_ge(ev(st_ok), n)
                nc.vector.bn_aggr(mv[:, :], st[:, :]).then_inc(ev(mv_ok), 1)

            def x3_step(n):
                bk = bank_of("av", n)
                dve.wait_ge(ev("x3_mm"), n)
                nc.vector.scalar_tensor_tensor(out=x3[:, :], in0=bk[:, 0:PIX], scalar=pv_b[:, 0:1], in1=x2[:, :],
                                               op0=ALU.add, op1=ALU.add).then_inc(ev("x3_ok"), 1)
                dve.wait_ge(ev("x3_ok"), n)
                stats(x3, st1, mv1, n, "st1_ok", "mv1_ok")

            def dw(part_of):
                def step(n):
                    for t in ((2, 3), (4, 5), (6, 7, 8))[part_of]:
                        sum_of = image(dw_acc[t % 2][:, :])
                        dve.wait_ge(ev(f"dw_step{t % 2}"), dw_count(n, t - 2))
                        nc.vector.scalar_tensor_tensor(out=sum_of, in0=dw_source(t), scalar=col("dw_w", t), in1=sum_of,
                                                       op0=ALU.mult, op1=ALU.add).then_inc(ev(f"dw_step{t % 2}"), 1)
                    if part_of == 2:
                        dve.wait_ge(ev("dw_step0"), dw_count(n, TAPS - 1))
                        dve.wait_ge(ev("dw_step1"), dw_count(n, TAPS - 2))
                        nc.vector.tensor_tensor(y_pad[:, 2:2 + H, 2:2 + W], image(dw_acc[0][:, :]),
                                                image(dw_acc[1][:, :]), ALU.add).then_inc(ev("y_ok"), 1)
                return step

            def scan(j):
                def step(n, nb):
                    for d in range(3):
                        dve.wait_ge(ev(f"scan{d}"), scan_count(n, j - 1))
                        nc.vector.scalar_tensor_tensor(out=image(acc[d][j % 2][:, :]), in0=window(d, j),
                                                       scalar=col("scan_w", d * KS + j),
                                                       in1=image(acc[d][(j - 1) % 2][:, :]), op0=ALU.mult, op1=ALU.add)\
                            .then_inc(ev(f"scan{d}"), 1)
                return step

            def gated(d):
                def step(n, nb):
                    dve.wait_ge(ev(f"scan{d}"), scan_count(n, KS - 1))
                    dve.wait_ge(ev(f"gate_ok{d // 2}"), n)
                    nc.vector.scalar_tensor_tensor(out=prod[d][:, :], in0=gates[:, d, :], scalar=1.0,
                                                   in1=acc[d][(KS - 1) % 2][:, :], op0=ALU.add, op1=ALU.mult)\
                        .then_inc(ev(f"prod{d}"), 1)
                return step

            def scan_sum(n, nb):
                dve.wait_ge(ev("prod2"), n)
                dve.wait_ge(ev("prod3"), n)
                nc.vector.tensor_tensor(o_b[:, :], prod[2][:, :], prod[3][:, :], ALU.add).then_inc(ev("o_b"), 1)
                dve.wait_ge(ev("o_a"), n)
                dve.wait_ge(ev("o_b"), n)
                nc.vector.tensor_tensor(o_sum[:, :], o_a[:, :], o_b[:, :], ALU.add).then_inc(ev("o_ok"), 1)

            def fuse(n, nb):
                bk = bank_of("fuse", n)
                dve.wait_ge(ev("fuse_mm"), n)
                nc.vector.scalar_tensor_tensor(out=x4[:, :], in0=bk[:, 0:PIX], scalar=col("fuse_b"), in1=x3[:, :],
                                               op0=ALU.add, op1=ALU.add).then_inc(ev("x4_ok"), 1)
                dve.wait_ge(ev("x4_ok"), n)
                stats(x4, st2, mv2, n, "st2_ok", "mv2_ok")

            def ff(b):
                def step(n, nb):
                    dve.wait_ge(ev(f"ff_act{b}"), n)
                    nc.vector.scalar_tensor_tensor(out=ff_u[b][:, :], in0=ff_g[b][:, :], scalar=1.0, in1=ff_a[b][:, :],
                                                   op0=ALU.add, op1=ALU.mult).then_inc(ev(f"ff_u{b}"), 1)
                return step

            def ff2(n, nb):
                bk = bank_of("ff2", n)
                dve.wait_ge(ev("out_mm"), n)
                dve.wait_ge(stored, 16 * n - 16)
                nc.vector.scalar_tensor_tensor(out=y_out[:, :], in0=bk[:, 0:PIX], scalar=col("ff2_b"), in1=x4[:, :],
                                               op0=ALU.add, op1=ALU.add).then_inc(ev("y_out_ok"), 1)

            steps_a = {"qk": qk, "attn": attn, "attn_norm": attn_norm, "x1": x1_step, "off_t": off_t,
                       "hat": hat_step, "hat_y": hat_y, "split": split}
            steps_b = {"logit0": logit(0), "logit1": logit(1), "nrm0": soft(0), "nrm1": soft(1),
                       "x3": x3_step, "dw0": dw(0), "dw1": dw(1), "dw2": dw(2)}
            steps_c = {"scan_t1": scan(1), "scan_t2": scan(2), "scan_t3": scan(3), "scan_t4": scan(4),
                       "gated0": gated(0), "gated1": gated(1), "gated2": gated(2),
                       "gated3": gated(3), "scan_sum": scan_sum, "fuse": fuse,
                       "u0": ff(0), "u1": ff(1), "ff2": ff2}

            def iteration(n, do_a, do_m, do_b, do_c):
                once(dve, n, 2, par_late, 16)
                once(dve, n, 2, prep_act, 6)
                walk(dve, PLAN["dve"], steps_a, steps_b, steps_c, main, n, do_a, do_m, do_b, do_c, last_a)

            def last_a(n):
                weights(n, 0)

            nc.vector.memset(mix[:, :], 0.0).then_inc(zero_ok, 1)
            nc.vector.memset(z_pad[:, :, :], 0.0).then_inc(zero_ok, 1)
            nc.vector.memset(y_pad[:, :, :], 0.0).then_inc(zero_ok, 1)
            nc.vector.memset(parts[:, :, AXES:4 * GROUPS, :, :], 0.0).then_inc(zero_ok, 1)
            nc.vector.memset(x1_pad[:, :, :], 0.0).then_inc(zero_ok, 1)
            dve.wait_ge(zero_ok, 5)
            dve.wait_ge(par_first, 16)
            schedule(dve, iteration)
            finish(PLAN_END["dve"], steps_b, steps_c)

        @block.gpsimd
        def _(pool):
            def hat_step(n):
                once(pool, n, 1, par_in, 16)
                pool.wait_ge(ev("pos_ok"), n)
                groups = 2 * AXES if is_first(n) else 4 * AXES
                nc.gpsimd.tensor_tensor(dist[:, 0:groups, :], pos[:, 0:groups].unsqueeze(2).to_broadcast([P, groups, H]),
                                        part("iota").unsqueeze(1).to_broadcast([P, groups, H]), ALU.subtract)\
                    .then_inc(ev("dist_ok"), 1)

            def split(n):
                pool.wait_ge(ev("high_ok"), n)
                g = 2 if is_first(n) else 4
                nc.gpsimd.tensor_tensor(parts[:, 0:g, 0:AXES, 1, :], hat[:, 0:g, :, :], parts[:, 0:g, 0:AXES, 0, :],
                                        ALU.subtract).then_inc(ev("low_ok"), 1)

            def norm(src_mv, scl, gain, mv_ok, var_ok, rstd_ok, g_ok, m_ok, h_ok):
                def step(n, *_):
                    settle(pool)
                    pool.wait_ge(ev(mv_ok), n)
                    nc.gpsimd.tensor_scalar(scl[:, 0:1], src_mv[:, 1:2], LN_EPS, 1.0, ALU.add, ALU.mult)\
                        .then_inc(ev(var_ok), 1)
                    pool.wait_ge(ev(var_ok), n)
                    nc.gpsimd.tensor_tensor(scl[:, 1:2], scl[:, 0:1], half[:, :], ALU.pow).then_inc(ev(rstd_ok), 1)
                    pool.wait_ge(ev(rstd_ok), n)
                    nc.gpsimd.tensor_tensor(scl[:, 2:3], scl[:, 1:2], col(gain, 0), ALU.mult).then_inc(ev(g_ok), 1)
                    pool.wait_ge(ev(g_ok), n)
                    nc.gpsimd.tensor_tensor(scl[:, 4:5], src_mv[:, 0:1], scl[:, 2:3], ALU.mult).then_inc(ev(m_ok), 1)
                    pool.wait_ge(ev(m_ok), n)
                    nc.gpsimd.tensor_tensor(scl[:, 3:4], col(gain, 1), scl[:, 4:5], ALU.subtract)\
                        .then_inc(ev(h_ok), 1)
                return step

            def scan3(n, nb):
                d = 3
                settle(pool)
                pool.wait_ge(ev("y_ok"), n)
                a = d * KS
                for j in range(1, KS):
                    nc.gpsimd.tensor_scalar(image(g_tmp[j % 2][:, :]), y_pad[:, j:j + H, 2:2 + W], col("scan_w", a + j),
                                            0.0, ALU.mult, ALU.add).then_inc(ev("term"), 1)
                    pool.wait_ge(ev("term"), n * (KS - 1) - (KS - 1) + j)
                    pool.wait_ge(ev(f"scan{d}"), scan_count(n, j - 1))
                    nc.gpsimd.tensor_tensor(acc[d][j % 2][:, :], acc[d][(j - 1) % 2][:, :], g_tmp[j % 2][:, :], ALU.add)\
                        .then_inc(ev(f"scan{d}"), 1)

            def scan_end(n, nb):
                pool.wait_ge(ev("prod0"), n)
                pool.wait_ge(ev("prod1"), n)
                nc.gpsimd.tensor_tensor(o_a[:, :], prod[0][:, :], prod[1][:, :], ALU.add).then_inc(ev("o_a"), 1)

            steps_a = {"hat": hat_step, "split": split}
            steps_b = {"x3": norm(mv1, sc1, "ln1", "mv1_ok", "var1_ok", "rstd1_ok", "g1_ok", "m1_ok", "h1_ok")}
            steps_c = {"fuse": norm(mv2, sc2, "ln2", "mv2_ok", "var2_ok", "rstd2_ok", "g2_ok", "m2_ok", "h2_ok"),
                       "scan3": scan3, "scan_end": scan_end}

            def prepare():
                pool.wait_ge(par_late, 16)
                nc.gpsimd.tensor_scalar(bn_s[:, 0:1], col("bn", 1), BN_EPS, 1.0, ALU.add, ALU.mult)\
                    .then_inc(bn_step, 1)
                pool.wait_ge(bn_step, 1)
                nc.gpsimd.tensor_tensor(bn_s[:, 1:2], bn_s[:, 0:1], half[:, :], ALU.pow).then_inc(bn_step, 1)
                pool.wait_ge(bn_step, 2)
                nc.gpsimd.tensor_tensor(bn_s[:, 2:3], bn_s[:, 1:2], col("bn", 0), ALU.mult).then_inc(bn_step, 1)
                nc.gpsimd.tensor_tensor(bn_s[:, 4:5], col("bn", 4), col("bn", 2), ALU.subtract).then_inc(bn_step, 1)
                pool.wait_ge(bn_step, 4)
                nc.gpsimd.tensor_scalar(bn_s[:, 3:4], bn_s[:, 4:5], bn_s[:, 2:3], col("bn", 3), ALU.mult, ALU.add)\
                    .then_inc(bn_step, 1)

            def iteration(n, do_a, do_m, do_b, do_c):
                if isinstance(n, int) and n == 1:
                    prepare()
                walk(pool, PLAN["pool"], steps_a, steps_b, steps_c, lambda n, s: None, n, do_a, do_m, do_b, do_c,
                     lambda n: None)

            nc.gpsimd.memset(half[:, :], -0.5).then_inc(half_ok, 1)
            pool.wait_ge(half_ok, 1)
            schedule(pool, iteration)
            finish(PLAN_END["pool"], steps_b, steps_c)


def _pack(a):
    f = np.float32
    wt = lambda w: np.ascontiguousarray(w.T)

    def twice(m):
        k, n = m.shape
        out = np.zeros((2, k, 2, n), f)
        out[0, :, 0], out[1, :, 1] = m, m
        return out.reshape(2 * k, 2 * n)

    def both(v):
        v = np.asarray(v).reshape(C, -1)
        return np.concatenate([v, v], 0)

    def spread(v):
        return np.broadcast_to(np.asarray(v).reshape(1, -1), (P, np.asarray(v).size))

    d = {"ident": np.eye(P, dtype=f)}
    d["qk_w"] = twice(np.concatenate([wt(a["L0_conv_wq"]), wt(a["L0_conv_wk"])], 1))
    d["qk_b"] = spread(np.concatenate([a["L0_conv_bq"], a["L0_conv_bk"]] * 2))
    wv, bv = a["L0_conv_wv"], a["L0_conv_bv"]
    d["av_w"] = np.concatenate([np.concatenate([wv, wv, bv[:, None]], 1), np.zeros((P - C, P + 1), f)], 0)
    w = np.zeros((TAPS, C, OM), f)
    w[:, :, 0:AXES + TAPS] = a["L1_conv_w_off"].reshape(AXES + TAPS, C, TAPS).transpose(2, 1, 0)
    d["off_w"] = np.concatenate([twice(w[t]) for t in range(TAPS)], 1)
    b = np.zeros((4, OM), f)
    b[:, 0:AXES + TAPS] = a["L1_conv_b_off"]
    d["off_b"] = b.reshape(P, 1)
    p, h, k = np.arange(P)[:, None, None], np.arange(HALVES)[None, :, None], np.arange(TAPS)[None, None, :]
    yx = np.stack([HALF_ROWS * h + p // W + k // 3 - 1 + 0 * k, p % W + k % 3 - 1 + 0 * h], -1)
    d["base"] = np.repeat(yx.reshape(P, HALVES, 1, AXES), 2, 2).reshape(P, 4 * AXES).astype(f) * f(UNIT)
    d["iota"] = spread(np.arange(H, dtype=f) * f(UNIT))
    w = a["L1_conv_w_dcn"].reshape(C, C, TAPS).transpose(2, 1, 0)
    d["dcn_w"] = np.concatenate([twice(w[t]) for t in range(TAPS)], 1)
    d["bn"] = np.concatenate([both(a["L1_conv_" + n]) for n in
                              ("gamma", "running_var", "running_mean", "beta", "b_dcn")], 1)
    for n in "qkvp":
        w = a["L2_conv_w" + n]
        d[n + "_w"] = twice(w if n == "v" else wt(w))
        d[n + "_b"] = both(a["L2_conv_b" + n])
    for n in ("1", "2"):
        d["ln" + n] = np.concatenate([both(a[f"L3_conv_ln{n}_w"]), both(a[f"L3_conv_ln{n}_b"])], 1)
    d["dw_w"] = both(a["L3_conv_dw_w"].reshape(TAPS, C).T)
    d["dw_b"] = both(a["L3_conv_dw_b"])
    taps = [a[f"L3_conv_{n}_dw_w"].reshape(KS, C)[::r] for n, r in (("lr", 1), ("rl", -1), ("tb", 1), ("bt", -1))]
    d["scan_w"] = both(np.concatenate(taps, 0).T)
    names = ("lr", "rl", "tb", "bt")
    d["scan_b"] = both(np.stack([a[f"L3_conv_{n}_dw_b"] for n in names], 1))
    d["gate_w"] = np.concatenate([twice(wt(a[f"L3_conv_{n}_g_w"])) for n in names], 1)
    d["gate_b"] = both(np.stack([a[f"L3_conv_{n}_g_b"] for n in names], 1))
    d["fuse_w"] = twice(wt(a["L3_conv_fuse_w"]))
    d["fuse_b"] = both(a["L3_conv_fuse_b"])
    w = wt(a["L3_conv_ff1_w"])
    d["ff1_w"] = np.concatenate([w, w], 0)
    d["ff1_b"] = a["L3_conv_ff1_b"].reshape(2, HID).T
    d["ff2_w"] = wt(a["L3_conv_ff2_w"])
    d["ff2_b"] = both(a["L3_conv_ff2_b"])
    return np.ascontiguousarray(np.concatenate([np.asarray(d[n], f).reshape(P, k) for n, k in PARTS], 1))


def _selectors():
    row = np.arange(P).reshape(4, 2, H, 1)
    slot, i = row // SLOT, row % H
    q = np.arange(P).reshape(1, 1, 1, P)
    out = [np.eye(P)]
    for odd in range(2):
        out.append(((slot == 2 * odd + 1) & (i == q % W)).reshape(P, P))
    for odd in range(2):
        for h in range(HALVES):
            out.append(((slot == 2 * odd) & (i == HALF_ROWS * h + q // W)).reshape(P, P))
    return np.ascontiguousarray(np.concatenate(out, 1).astype(np.float16))


def kernel(**inputs):
    import concourse.bacc as bacc
    from concourse.bass_utils import run_bass_kernel_spmd

    a = {k: np.asarray(v) for k, v in inputs.items()}
    arrays = {
        "in_x": np.ascontiguousarray(a["x"].reshape(PAIRS, P, PIX)),
        "in_par": _pack(a),
        "in_sel": _selectors(),
    }
    nc = bacc.Bacc("TRN2", target_bir_lowering=False, num_devices=1)
    args = [nc.dram_tensor(n, v.shape, mybir.dt.from_np(v.dtype), kind="ExternalInput").ap() for n, v in arrays.items()]
    args.append(nc.dram_tensor("out_y", (PAIRS, P, PIX), F32, kind="ExternalOutput").ap())
    program(nc, *args)
    r = run_bass_kernel_spmd(nc, [arrays], core_ids=[0])
    return np.asarray(r.results[0]["out_y"]).reshape(IMAGES, C, H, W)
```

```python
from contextlib import ExitStack

import numpy as np

import concourse.bass as bass
from concourse import mybir

F32 = mybir.dt.float32
F16 = mybir.dt.float16
ALU = mybir.AluOpType
ACT = mybir.ActivationFunctionType
AX_X = mybir.AxisListType.X

IMAGES, C, H, W = 16, 64, 16, 16
PIX = H * W
PAIRS = IMAGES // 2
P = 128
HALVES = PIX // P
HALF_ROWS = H // HALVES
TAPS = 9
CHUNKS = (TAPS + 1) // 2
AXES = 2 * TAPS
OM = 32
GROUPS = 5
SLOT = 2 * H
SCANS, KS = 4, 5
HID = 2 * C
PW = W + 2
SW = W + 4
UNIT = float(2 ** 12)
BN_EPS, LN_EPS = 1e-5, 1e-6
QK_SCALE = float(C) ** -0.5

PARTS = [
    ("qk_w", 2 * P), ("qk_b", 2 * P), ("ident", P), ("av_w", P + 1), ("off_w", TAPS * 2 * OM), ("off_b", 1),
    ("base", 4 * AXES), ("iota", H), ("dcn_w", TAPS * P), ("bn", 5), ("q_w", P), ("k_w", P), ("v_w", P),
    ("p_w", P), ("v_b", 1), ("q_b", 1), ("k_b", 1), ("p_b", 1), ("ln1", 2), ("dw_w", TAPS), ("dw_b", 1),
    ("scan_w", SCANS * KS), ("scan_b", SCANS), ("gate_w", SCANS * P), ("gate_b", SCANS), ("fuse_w", P),
    ("fuse_b", 1), ("ln2", 2), ("ff1_w", 2 * HID), ("ff1_b", 2), ("ff2_w", C), ("ff2_b", 1),
]
AT, PACK = {}, 0
for _name, _n in PARTS:
    AT[_name] = (PACK, PACK + _n)
    PACK += _n
FIRST = AT["av_w"][0]
EARLY = AT["dcn_w"][0]

SLOTS = 2 * TAPS
PLAN = {
    "pe": {0: ["qk", "qk2"], 1: ["attn", "v2"], 2: ["logit0", "attn_t"], 3: ["mix"], 4: ["logit1", "x1"],
           6: ["fuse", "wx0", "off", "et0"], 7: ["off_t", "et1"], 8: ["av", "ff0"], 11: ["wx1"], 12: ["ff1", "wx2"],
           14: ["wx3"], 15: ["tr0", "gate0"], 16: ["tr1", "ff2", "gate1"], 17: ["tr2"]},
    "act": {0: ["scan_first", "qk2", "attn", "v2"], 2: ["attn_t", "soft0", "mix"], 5: ["soft1"],
            6: ["off", "wx0", "et0"], 7: ["et1"], 8: ["ln2", "off_t"], 9: ["ff0"], 10: ["abs", "ln1", "dw_first"],
            11: ["wx1"], 12: ["split", "wx2"], 13: ["ff1"], 14: ["wx3", "tr0", "gate0", "tr1"], 16: ["gate1"],
            17: ["tr2"]},
    "dve": {1: ["scan_t1", "qk", "scan_t2"], 2: ["attn", "scan_t3", "attn_norm"],
            3: ["logit0", "scan_t4", "gated3", "gated2"], 4: ["gated0", "gated1"],
            5: ["scan_sum", "x1", "logit1", "nrm0", "nrm1"], 6: ["fuse"], 8: ["off_t"], 9: ["x3"], 10: ["u0"],
            11: ["hat"], 12: ["hat_y", "dw0"], 13: ["dw1"], 14: ["dw2", "split"], 15: ["u1"], 17: ["ff2"]},
    "pool": {0: ["scan3", "scan_end"], 9: ["fuse"], 10: ["hat"], 15: ["x3", "split"]},
}
PLAN_END = {
    "pe": ["b.qk2", "b.v2", "b.logit0", "b.logit1", "b.et1", "b.et0", "c.fuse", "b.av", "c.ff0", "c.ff1", "b.gate0",
           "c.ff2", "b.gate1", "d.fuse", "d.ff0", "d.ff1", "d.ff2"],
    "act": ["c.scan_first", "b.qk2", "b.soft0", "b.soft1", "b.et0", "b.et1", "b.v2", "c.ln2", "b.ln1", "b.dw_first",
            "c.ff0", "c.ff1", "d.scan_first", "b.gate1", "b.gate0", "d.ln2", "d.ff0", "d.ff1"],
    "dve": ["c.scan_t1", "c.scan_t2", "c.scan_t3", "b.logit0", "b.logit1", "c.scan_t4", "c.gated0", "b.nrm1",
            "c.gated2", "b.nrm0", "c.gated1", "c.gated3", "c.scan_sum", "c.fuse", "b.x3", "b.dw0", "b.dw1", "b.dw2",
            "c.u0", "c.u1", "d.scan_t1", "d.scan_t2", "d.scan_t3", "d.scan_t4", "d.gated0", "d.gated1", "d.gated2",
            "d.gated3", "c.ff2", "d.scan_sum", "d.fuse", "d.u0", "d.u1", "d.ff2"],
    "pool": ["c.scan3", "c.scan_end", "c.fuse", "b.x3", "d.scan3", "d.scan_end", "d.fuse"],
}


def program(nc, x, par, sel, out):
    ctx = ExitStack()
    with ctx:
        def sb(name, shape, dt=F32):
            return ctx.enter_context(nc.sbuf_tensor("sb_" + name, shape, dt))

        def bank(name):
            return ctx.enter_context(nc.psum_tensor("ps_" + name, [P, 512], F32))

        def sem(name):
            return ctx.enter_context(nc.semaphore(name))

        par_sb = sb("par", [P, PACK])
        sel_sb = sb("sel", [P, 7 * P], F16)
        half = sb("half", [P, 1])
        bn_s = sb("bn_s", [P, 5])
        pv_w = sb("pv_w", [P, P])
        pv_b = sb("pv_b", [P, 1])
        fuse_h = sb("fuse_h", [P, P])
        ff2_h = sb("ff2_h", [P, C])
        gate_bh = sb("gate_bh", [P, SCANS])
        ff1_bh = sb("ff1_bh", [P, 1])
        x_in = sb("x_in", [P, PIX])
        qk_sb = sb("qk", [P, HALVES, 2, 2, C])
        a_max = sb("a_max", [P, 1])
        a_neg = sb("a_neg", [P, 1])
        a_exp = sb("a_exp", [P, C])
        a_sum = sb("a_sum", [P, 1])
        a_rec = sb("a_rec", [P, 1])
        a_nrm = sb("a_nrm", [P, C])
        at_sb = sb("at", [C, P])
        mix = sb("mix", [P, P])
        mix_b = sb("mix_b", [P, 1])
        x1 = sb("x1", [P, PIX])
        x1_pad = sb("x1_pad", [P, H + 2, PW])
        off = sb("off", [P, P])
        pos = sb("pos", [P, 4 * AXES])
        msk = sb("msk", [P, 4, TAPS])
        dist = sb("dist", [P, 4 * AXES, H])
        hat = sb("hat", [P, 4, AXES, H])
        parts = sb("parts", [P, 4, 4 * GROUPS, 2, H], F16)
        hats = sb("hats", [P, GROUPS, 2 * PIX], F16)
        w_x = sb("w_x", [P, HALVES, TAPS, P])
        xe = [sb(f"xe{i}", [P, 2 * PIX]) for i in range(2)]
        wt = [[sb(f"wt{i}{h}", [P, 2 * PIX]) for h in range(HALVES)] for i in range(2)]
        x2 = sb("x2", [P, PIX])
        q2 = sb("q2", [P, PIX])
        k2 = sb("k2", [P, PIX])
        v2 = sb("v2", [P, HALVES, P])
        b_max = [sb(f"b_max{b}", [P, HALVES]) for b in range(2)]
        b_neg = [sb(f"b_neg{b}", [P, HALVES]) for b in range(2)]
        b_sum = [sb(f"b_sum{b}", [P, HALVES]) for b in range(2)]
        b_rec = [sb(f"b_rec{b}", [P, HALVES]) for b in range(2)]
        b_exp = [sb(f"b_exp{b}", [P, HALVES, PIX]) for b in range(2)]
        b_dia = [sb(f"b_dia{b}", [P, HALVES, P]) for b in range(2)]
        e_t = [sb(f"e_t{b}", [P, HALVES, PIX]) for b in range(2)]
        x3 = sb("x3", [P, PIX])
        st1, mv1, sc1 = sb("st1", [P, 6]), sb("mv1", [P, 2]), sb("sc1", [P, 5])
        z_pad = sb("z_pad", [P, H + 2, PW])
        dw_acc = [sb(f"dw_acc{i}", [P, PIX]) for i in range(2)]
        y_pad = sb("y_pad", [P, H + 4, SW])
        gates = sb("gates", [P, SCANS, PIX])
        acc = [[sb(f"acc{d}{i}", [P, PIX]) for i in range(2)] for d in range(SCANS)]
        prod = [sb(f"prod{d}", [P, PIX]) for d in range(SCANS)]
        g_tmp = [sb(f"g_tmp{i}", [P, PIX]) for i in range(2)]
        o_a, o_b, o_sum = sb("o_a", [P, PIX]), sb("o_b", [P, PIX]), sb("o_sum", [P, PIX])
        x4 = sb("x4", [P, PIX])
        st2, mv2, sc2 = sb("st2", [P, 6]), sb("mv2", [P, 2]), sb("sc2", [P, 5])
        z2 = sb("z2", [P, PIX])
        ff_a = [sb(f"ff_a{b}", [P, PIX]) for b in range(2)]
        ff_g = [sb(f"ff_g{b}", [P, PIX]) for b in range(2)]
        ff_u = [sb(f"ff_u{b}", [P, PIX]) for b in range(2)]
        y_out = sb("y_out", [P, PIX])

        def part(name, rows=P):
            a, b = AT[name]
            return par_sb[0:rows, a:b]

        def col(name, i=0):
            a = AT[name][0] + i
            return par_sb[:, a:a + 1]

        def image(ap):
            return ap.rearrange("p (h w) -> p h w", h=H)

        def is_first(n):
            return isinstance(n, int) and n == 1

        def is_last(n):
            return isinstance(n, int) and n == PAIRS

        yb = [bank(f"yb{h}") for h in range(HALVES)]
        xb = bank("xb")
        wx = bank("wx")
        cv = bank("cv")
        ma = bank("ma")
        mb = bank("mb")
        mc = bank("mc")

        def bank_of(step, n):
            if not is_last(n):
                return mc if step in ("fuse", "ff0", "ff1", "ff2") else mb
            return {"qk2": cv, "v2": wx, "logit0": yb[0], "logit1": yb[1], "et0": xb, "et1": ma, "av": cv,
                    "gate0": yb[0], "gate1": yb[1], "fuse": xb, "ff0": wx, "ff1": ma, "ff2": cv}[step]

        def bank_wx(c, n):
            return (wx, cv, yb[0], yb[1], xb)[c] if is_first(n) else wx

        def bank_tr(index, n):
            return (ma, mb, mc)[index] if is_first(n) else ma

        par_first, par_in, par_late, sel_in = sem("par_first"), sem("par_in"), sem("par_late"), sem("sel_in")
        zero_ok, half_ok = sem("zero_ok"), sem("half_ok")
        prep_mm, prep_act, bn_step = sem("prep_mm"), sem("prep_act"), sem("bn_step")
        x_loaded, stored = sem("x_loaded"), sem("stored")
        S = {}

        def ev(name):
            if name not in S:
                S[name] = sem(name)
            return S[name]

        names_a = ["qk_mm", "qk_ok", "attn_mm", "a_max_ok", "a_neg_ok", "a_exp_ok", "a_rec_ok", "a_nrm_ok",
                   "at_mm", "at_ok", "mix_mm", "mix_ok", "x1_mm", "x1_ok", "x1_pad_ok", "off_mm", "off_ok",
                   "pos_mm", "pos_ok", "tanh_ok", "msk_ok", "dist_ok", "abs_ok", "hat_ok", "hat_y_ok",
                   "high_ok", "low_ok", "tr_mm0", "tr_mm1", "tr_mm2", "hats_ok0", "hats_ok1", "hats_ok2",
                   "wx_mm", "wx_ok"]
        names_m = ["xb_mm", "xe_ok", "smp_mm", "yb_mm", "wt_ok", "x2_ok"]
        names_a += ["dist_ok_dve", "low_ok_dve"]
        names_b = ["qk2_mm", "qk2_ok", "v2_mm", "v2_ok", "x3_mm", "x3_ok", "st1_ok", "mv1_ok",
                   "var1_ok", "rstd1_ok", "g1_ok", "m1_ok", "h1_ok", "z_ok", "dw_step0", "dw_step1", "y_ok",
                   "gate_mm0", "gate_mm1", "gate_ok0", "gate_ok1", "o_a", "o_b", "o_ok"]
        names_b += [f"scan{d}" for d in range(SCANS)]
        names_b += [f"prod{d}" for d in range(SCANS)] + ["term"]
        names_b += [f"{e}{b}" for b in range(2) for e in ("logit_mm", "max_ok", "neg_ok", "exp_ok", "rec_ok",
                                                         "nrm_ok", "et_mm", "et_ok")]
        names_c = ["fuse_mm", "x4_ok", "st2_ok", "mv2_ok", "var2_ok", "rstd2_ok", "g2_ok", "m2_ok", "h2_ok", "z2_ok",
                   "ff_mm0", "ff_mm1", "ff_act0", "ff_act1", "ff_u0", "ff_u1", "out_mm", "y_out_ok"]
        for name in names_a + names_m + names_b + names_c:
            ev(name)

        def tap(n, k):
            return n * TAPS - TAPS + (k + 1)

        def slot(n, s):
            return n * SLOTS - SLOTS + (s + 1)

        def chunk(n, c):
            return n * CHUNKS - CHUNKS + (c + 1)

        def scan_count(n, j):
            return n * KS - KS + (j + 1)

        def dw_count(n, t):
            total = (TAPS + 1 - t % 2) // 2
            return n * total - total + (t // 2 + 1)

        def window(d, j):
            return y_pad[:, 2:2 + H, j:j + W] if d < 2 else y_pad[:, j:j + H, 2:2 + W]

        def dw_source(t):
            return z_pad[:, t // 3:t // 3 + H, t % 3:t % 3 + W]

        def wait_past(eng, semaphore, value):
            if not isinstance(value, int) or value > 0:
                eng.wait_ge(semaphore, value)

        def once(eng, n, first, semaphore, count):
            if isinstance(n, int) and n == first:
                eng.wait_ge(semaphore, count)

        def settle(eng):
            eng.wait_ge(par_first, 16)

        def schedule(eng, iteration):
            iteration(0, True, False, False, False)
            iteration(1, True, True, False, False)
            iteration(2, True, True, True, False)
            iteration(3, True, True, True, True)
            with eng.Fori(4, PAIRS) as n:
                iteration(n, True, True, True, True)
            iteration(PAIRS, False, True, True, True)

        def finish(plan_end, steps_b, steps_c):
            for entry in plan_end:
                chain, step = entry.split(".")
                if chain == "b":
                    steps_b[step](PAIRS)
                elif chain == "c":
                    steps_c[step](PAIRS - 1, PAIRS)
                else:
                    steps_c[step](PAIRS, PAIRS)

        def walk(eng, plan, steps_a, steps_b, steps_c, main, n, do_a, do_m, do_b, do_c, last_a):
            after, before, before2 = n + 1, n - 1, n - 2
            if not isinstance(n, int):
                for value in (after, before, before2):
                    eng.lower_val(value)
            for s in range(SLOTS):
                if do_m:
                    main(n, s)
                for step in plan.get(s, ()):
                    if step in steps_a:
                        if do_a:
                            steps_a[step](after)
                    elif step in steps_b:
                        if do_b:
                            steps_b[step](before)
                    elif do_c:
                        steps_c[step](before2, before if do_b else before2)
            if do_a:
                last_a(after, 0)
            if do_m:
                main(n, SLOTS)
            if do_a:
                last_a(after, 1)

        block = ctx.enter_context(nc.Block())

        @block.sync
        def _(sp):
            k = AT["qk_b"][0]
            sp.dma_start(par_sb[:, 0:k], par[:, 0:k]).then_inc(par_first, 16)
            sp.dma_start(x_in[:, :], x[0, :, :]).then_inc(x_loaded, 16)
            sp.dma_start(par_sb[:, k:FIRST], par[:, k:FIRST]).then_inc(par_first, 16)
            sp.dma_start(par_sb[:, FIRST:EARLY], par[:, FIRST:EARLY]).then_inc(par_in, 16)
            sp.dma_start(sel_sb[:, :], sel[:, :]).then_inc(sel_in, 16)
            sp.dma_start(par_sb[:, EARLY:PACK], par[:, EARLY:PACK]).then_inc(par_late, 16)

            def load(n):
                sp.wait_ge(ev("x1_pad_ok"), n)
                sp.dma_start(x_in[:, :], x[n, :, :]).then_inc(x_loaded, 16)

            def store(n):
                sp.wait_ge(ev("y_out_ok"), n)
                sp.dma_start(out[n - 1, :, :], y_out[:, :]).then_inc(stored, 16)

            for n in range(1, 4):
                load(n)
            with sp.Fori(4, PAIRS) as n:
                store(n - 3)
                load(n)
            for n in range(PAIRS - 3, PAIRS + 1):
                store(n)
            sp.wait_ge(stored, 16 * PAIRS)

        @block.tensor
        def _(pe):
            ident = part("ident")
            ident16 = sel_sb[:, 0:P]

            def qk(n):
                pe.wait_ge(x_loaded, 16 * n)
                pe.wait_ge(ev("hats_ok2"), n - 1)
                for h in range(HALVES):
                    mm = nc.tensor.matmul(ma[:, 2 * P * h:2 * P * (h + 1)], x_in[:, P * h:P * (h + 1)],
                                          part("qk_w"), start=True, stop=True)
                mm.then_inc(ev("qk_mm"), 1)

            def attn(n):
                pe.wait_ge(ev("qk_ok"), n)
                for h in range(HALVES):
                    for b in range(2):
                        mm = nc.tensor.matmul(ma[C * b:C * (b + 1), 0:C], qk_sb[:, h, b, 0, :], qk_sb[:, h, b, 1, :],
                                              start=(h == 0), stop=(h == HALVES - 1))
                mm.then_inc(ev("attn_mm"), 1)

            def attn_t(n):
                once(pe, n, 1, par_first, 32)
                settle(pe)
                pe.wait_ge(ev("a_nrm_ok"), n)
                nc.tensor.transpose(ma[0:C, 0:P], a_nrm[:, :], ident).then_inc(ev("at_mm"), 1)

            def mix_step(n):
                once(pe, n, 1, par_in, 16)
                pe.wait_ge(ev("at_ok"), n)
                a, b = AT["av_w"]
                nc.tensor.matmul(ma[:, 0:P], par_sb[0:C, a:b - 1], at_sb[:, :], start=True, stop=True)
                nc.tensor.matmul(ma[:, P:P + 1], at_sb[:, :], par_sb[0:C, b - 1:b], start=True, stop=True)\
                    .then_inc(ev("mix_mm"), 1)

            def x1_step(n):
                pe.wait_ge(ev("mix_ok"), n)
                nc.tensor.matmul(ma[:, 0:PIX], mix[:, :], x_in[:, :], start=True, stop=True).then_inc(ev("x1_mm"), 1)

            def off_step(n):
                pe.wait_ge(ev("x1_pad_ok"), n)
                a = AT["off_w"][0]
                for t in range(TAPS):
                    for h in range(HALVES):
                        r = t // 3 + HALF_ROWS * h
                        mm = nc.tensor.matmul(ma[C * h:C * (h + 1), 0:P],
                                              par_sb[:, a + 2 * OM * t:a + 2 * OM * (t + 1)],
                                              x1_pad[:, r:r + HALF_ROWS, t % 3:t % 3 + W],
                                              start=(t == 0), stop=(t == TAPS - 1))
                mm.then_inc(ev("off_mm"), 1)

            def off_t(n):
                pe.wait_ge(ev("off_ok"), n)
                nc.tensor.transpose(ma[:, 0:P], off[:, :], ident).then_inc(ev("pos_mm"), 1)
                if is_first(n):
                    for c in range(CHUNKS):
                        wx_step(c)(n)

            def tr(g0, g1, index):
                def step(n):
                    if index == 0:
                        once(pe, n, 1, sel_in, 16)
                        pe.wait_ge(ev("high_ok"), n)
                        pe.wait_ge(ev("low_ok"), n)
                        once(pe, n, 1, ev("low_ok_dve"), 1)
                        pe.wait_ge(ev("tanh_ok"), n)
                    elif not is_first(n):
                        pe.wait_ge(ev(f"hats_ok{index - 1}"), n)
                    bk = bank_tr(index, n)[:, :].bitcast(F16)
                    for g in range(g0, g1):
                        for b in range(2):
                            for h in range(HALVES):
                                at = 2 * PIX * (g - g0) + PIX * b + P * h
                                mm = nc.tensor.transpose(bk[:, at:at + P], parts[:, 2 * h + b, 4 * g:4 * g + 4, :, :],
                                                         ident16)
                    mm.then_inc(ev(f"tr_mm{index}"), 1)
                return step

            def wx_step(c):
                def step(n):
                    once(pe, n, 1, par_late, 16)
                    pe.wait_ge(ev("x1_ok"), n)
                    if not is_first(n):
                        pe.wait_ge(ev("wx_ok"), chunk(n, c - 1))
                    a = AT["dcn_w"][0] + 2 * P * c
                    k = P * min(2, TAPS - 2 * c)
                    for h in range(HALVES):
                        mm = nc.tensor.matmul(bank_wx(c, n)[:, 2 * P * h:2 * P * h + k], x1[:, P * h:P * (h + 1)],
                                              par_sb[:, a:a + k], start=True, stop=True)
                    mm.then_inc(ev("wx_mm"), 1)
                return step

            def spread(n, s):
                k, h = divmod(s, 2)
                g, odd = divmod(k, 2)
                if h == 0:
                    if k % 4 == 0:
                        pe.wait_ge(ev(f"hats_ok{k // 4}"), n)
                    wait_past(pe, ev("xe_ok"), tap(n, k - 1))
                    nc.tensor.matmul(xb[:, :], sel_sb[:, P * (1 + odd):P * (2 + odd)], hats[:, g, :],
                                     start=True, stop=True).then_inc(ev("xb_mm"), 1)
                wait_past(pe, ev("wt_ok"), slot(n, s - 2))
                nc.tensor.matmul(yb[h][:, :], sel_sb[:, P * (3 + 2 * odd + h):P * (4 + 2 * odd + h)], hats[:, g, :],
                                 start=True, stop=True).then_inc(ev("yb_mm"), 1)

            def main(n, s):
                if s == SLOTS:
                    return
                k, h = divmod(s, 2)
                if s + 2 < SLOTS:
                    spread(n, s + 2)
                if h == 0 and k % 2 == 0:
                    pe.wait_ge(ev("wx_ok"), chunk(n, k // 2))
                pe.wait_ge(ev("wt_ok"), slot(n, s))
                if s == 0:
                    pe.wait_ge(ev("x2_ok"), n - 1)
                for b in range(2):
                    mm = nc.tensor.matmul(cv[C * b:C * (b + 1), 0:PIX], w_x[:, h, k, C * b:C * (b + 1)],
                                          wt[k % 2][h][:, PIX * b:PIX * (b + 1)], start=(s == 0), stop=(s == SLOTS - 1))
                if h == 1:
                    mm.then_inc(ev("smp_mm"), 1)

            def qk2(n):
                bk = bank_of("qk2", n)
                pe.wait_ge(ev("x2_ok"), n)
                if not is_last(n):
                    pe.wait_ge(ev("gate_ok1"), n - 1)
                nc.tensor.matmul(bk[:, 0:PIX], part("q_w"), x2[:, :], start=True, stop=True)
                nc.tensor.matmul(bk[:, PIX:2 * PIX], part("k_w"), x2[:, :], start=True, stop=True)\
                    .then_inc(ev("qk2_mm"), 1)

            def v2_step(n):
                bk = bank_of("v2", n)
                if not is_last(n):
                    pe.wait_ge(ev("qk2_ok"), n)
                for h in range(HALVES):
                    mm = nc.tensor.matmul(bk[:, P * h:P * (h + 1)], x2[:, P * h:P * (h + 1)], pv_w[:, :],
                                          start=True, stop=True)
                mm.then_inc(ev("v2_mm"), 1)

            def logit(b):
                def step(n):
                    bk = bank_of(f"logit{b}", n)
                    if b == 0:
                        pe.wait_ge(ev("qk2_ok"), n)
                    if not is_last(n):
                        pe.wait_ge(ev("v2_ok" if b == 0 else "exp_ok0"), n)
                    for h in range(HALVES):
                        mm = nc.tensor.matmul(bk[:, PIX * h:PIX * (h + 1)], q2[C * b:C * (b + 1), P * h:P * (h + 1)],
                                              k2[C * b:C * (b + 1), :], start=True, stop=True)
                    mm.then_inc(ev(f"logit_mm{b}"), 1)
                return step

            def e_transpose(b):
                def step(n):
                    bk = bank_of(f"et{b}", n)
                    pe.wait_ge(ev(f"nrm_ok{b}"), n)
                    if not is_last(n):
                        pe.wait_ge(ev("exp_ok1" if b == 0 else "et_ok0"), n)
                    for j in range(HALVES):
                        for h in range(HALVES):
                            mm = nc.tensor.matmul(bk[:, PIX * j + P * h:PIX * j + P * (h + 1)],
                                                  b_exp[b][:, h, P * j:P * (j + 1)], b_dia[b][:, h, :],
                                                  start=True, stop=True)
                    mm.then_inc(ev(f"et_mm{b}"), 1)
                return step

            def av(n):
                bk = bank_of("av", n)
                pe.wait_ge(ev("et_ok1"), n)
                pe.wait_ge(ev("v2_ok"), n)
                for j in range(HALVES):
                    for b in range(2):
                        mm = nc.tensor.matmul(bk[C * b:C * (b + 1), 0:PIX], v2[:, j, C * b:C * (b + 1)],
                                              e_t[b][:, j, :], start=(j == 0), stop=(j == HALVES - 1))
                mm.then_inc(ev("x3_mm"), 1)

            def gate(i):
                def step(n):
                    bk = bank_of(f"gate{i}", n)
                    if i == 0:
                        pe.wait_ge(ev("y_ok"), n)
                    if not is_last(n):
                        pe.wait_ge(ev("x3_ok" if i == 0 else "gate_ok0"), n)
                    for j in range(2):
                        a = AT["gate_w"][0] + P * (2 * i + j)
                        mm = nc.tensor.matmul(bk[:, PIX * j:PIX * (j + 1)], par_sb[:, a:a + P],
                                              y_pad[:, 2:2 + H, 2:2 + W], start=True, stop=True)
                    mm.then_inc(ev(f"gate_mm{i}"), 1)
                return step

            def fuse(n, nb):
                bk = bank_of("fuse", n)
                pe.wait_ge(ev("o_ok"), n)
                if not is_last(n):
                    pe.wait_ge(ev("y_out_ok"), n - 1)
                nc.tensor.matmul(bk[:, 0:PIX], fuse_h[:, :], o_sum[:, :], start=True, stop=True)\
                    .then_inc(ev("fuse_mm"), 1)

            def ff(b):
                def step(n, nb):
                    bk = bank_of(f"ff{b}", n)
                    pe.wait_ge(ev("z2_ok"), n)
                    if b == 1 and not is_last(n):
                        pe.wait_ge(ev("ff_act0"), n)
                    a = AT["ff1_w"][0]
                    for j in range(2):
                        mm = nc.tensor.matmul(bk[:, PIX * j:PIX * (j + 1)],
                                              par_sb[C * b:C * (b + 1), a + HID * j:a + HID * (j + 1)],
                                              z2[C * b:C * (b + 1), :], start=True, stop=True)
                    mm.then_inc(ev(f"ff_mm{b}"), 1)
                return step

            def ff2(n, nb):
                bk = bank_of("ff2", n)
                pe.wait_ge(ev("ff_u0"), n)
                pe.wait_ge(ev("ff_u1"), n)
                for b in range(2):
                    mm = nc.tensor.matmul(bk[C * b:C * (b + 1), 0:PIX], ff2_h[:, :], ff_u[b][:, :],
                                          start=True, stop=True)
                mm.then_inc(ev("out_mm"), 1)

            def wx_plan(c):
                return lambda n: None if is_first(n) else wx_step(c)(n)

            steps_a = {"qk": qk, "attn": attn, "attn_t": attn_t, "mix": mix_step, "x1": x1_step, "off": off_step,
                       "off_t": off_t, "tr0": tr(0, 2, 0), "tr1": tr(2, 4, 1), "tr2": tr(4, 5, 2),
                       "wx0": wx_plan(0), "wx1": wx_plan(1), "wx2": wx_plan(2), "wx3": wx_plan(3)}
            steps_b = {"qk2": qk2, "v2": v2_step, "logit0": logit(0), "logit1": logit(1), "et0": e_transpose(0),
                       "et1": e_transpose(1), "av": av, "gate0": gate(0),
                       "gate1": gate(1)}
            steps_c = {"fuse": fuse, "ff0": ff(0), "ff1": ff(1), "ff2": ff2}

            def last_a(n, moment):
                if moment == 0:
                    once(pe, n, 1, ev("wx_ok"), CHUNKS)
                    spread(n, 0)
                    spread(n, 1)
                elif not is_first(n):
                    wx_step(CHUNKS - 1)(n)

            def prepare():
                pe.wait_ge(par_late, 16)
                pe.wait_ge(ev("hats_ok1"), 1)
                nc.tensor.matmul(mb[:, 0:P], part("v_w"), part("p_w"), start=True, stop=True)
                nc.tensor.matmul(mb[:, P:P + 1], part("p_w"), col("v_b"), start=True, stop=True).then_inc(prep_mm, 1)

            def iteration(n, do_a, do_m, do_b, do_c):
                if isinstance(n, int) and n == 1:
                    prepare()
                once(pe, n, 2, prep_act, 6)
                walk(pe, PLAN["pe"], steps_a, steps_b, steps_c, main, n, do_a, do_m, do_b, do_c, last_a)

            pe.wait_ge(par_first, 16)
            schedule(pe, iteration)
            finish(PLAN_END["pe"], steps_b, steps_c)

        @block.scalar
        def _(act):
            def attn(n):
                act.wait_ge(ev("a_neg_ok"), n)
                nc.scalar.activation(a_exp[:, :], ma[:, 0:C], ACT.Exp, bias=a_neg[:, 0:1], scale=QK_SCALE,
                                     accum_out=a_sum[:, 0:1]).then_inc(ev("a_exp_ok"), 1)

            def attn_t(n):
                act.wait_ge(ev("at_mm"), n)
                nc.scalar.activation(at_sb[:, :], ma[0:C, 0:P], ACT.Copy).then_inc(ev("at_ok"), 1)

            def mix_step(n):
                once(act, n, 1, zero_ok, 5)
                act.wait_ge(ev("mix_mm"), n)
                for b in range(2):
                    r = slice(C * b, C * (b + 1))
                    nc.scalar.activation(mix[r, r], ma[r, r], ACT.Copy)
                nc.scalar.activation(mix_b[:, :], ma[:, P:P + 1], ACT.Copy).then_inc(ev("mix_ok"), 1)

            def off_step(n):
                once(act, n, 1, par_in, 16)
                act.wait_ge(ev("off_mm"), n)
                nc.scalar.activation(off[:, :], ma[:, 0:P], ACT.Identity, bias=col("off_b"))\
                    .then_inc(ev("off_ok"), 1)

            def off_t(n):
                act.wait_ge(ev("pos_ok"), n)
                nc.scalar.activation(msk[:, :, :], ma[:, 0:4 * OM].rearrange("p (g m) -> p g m", m=OM)[:, :, AXES:AXES + TAPS],
                                     ACT.Tanh, scale=0.5).then_inc(ev("tanh_ok"), 1)
                if is_first(n):
                    wx_step(0)(n)

            def hat_step(n):
                act.wait_ge(ev("dist_ok"), n)
                once(act, n, 1, ev("dist_ok_dve"), 1)
                nc.scalar.activation(hat[:, :, :, :].rearrange("p g a i -> p (g a i)"),
                                     dist[:, :, :].rearrange("p a i -> p (a i)"), ACT.Abs).then_inc(ev("abs_ok"), 1)
                if is_first(n):
                    for c in range(1, CHUNKS - 1):
                        wx_step(c)(n)

            def split(n):
                act.wait_ge(ev("hat_y_ok"), n)
                act.wait_ge(ev("tr_mm2"), n - 1)
                nc.scalar.activation(parts[:, :, 0:AXES, 0, :], hat[:, :, :, :], ACT.Copy)\
                    .then_inc(ev("high_ok"), 1)
                if is_first(n):
                    wx_step(CHUNKS - 1)(n)

            def tr(g0, g1, index):
                def step(n):
                    act.wait_ge(ev(f"tr_mm{index}"), n)
                    k = 2 * PIX * (g1 - g0)
                    bk = bank_tr(index, n)[:, :].bitcast(F16)
                    nc.scalar.activation(hats[:, g0:g1, :].rearrange("p g q -> p (g q)"), bk[:, 0:k], ACT.Copy)\
                        .then_inc(ev(f"hats_ok{index}"), 1)
                return step

            def wx_step(c):
                def step(n):
                    k = min(2, TAPS - 2 * c)
                    act.wait_ge(ev("wx_mm"), chunk(n, c))
                    wait_past(act, ev("smp_mm"), tap(n - 1, 2 * c + k - 1))
                    nc.scalar.activation(w_x[:, :, 2 * c:2 * c + k, :].rearrange("p h k c -> p h (k c)"),
                                         bank_wx(c, n)[:, :].rearrange("p (h c) -> p h c", h=HALVES)[:, :, 0:P * k],
                                         ACT.Copy,
                                         scale=0.5 / UNIT / UNIT).then_inc(ev("wx_ok"), 1)
                return step

            def columns(n, k):
                act.wait_ge(ev("xb_mm"), tap(n, k))
                wait_past(act, ev("wt_ok"), slot(n, 2 * k - 3))
                nc.scalar.activation(xe[k % 2][:, :], xb[:, :], ACT.Copy).then_inc(ev("xe_ok"), 1)

            def main(n, s):
                if s == SLOTS:
                    once(act, n, 1, bn_step, 5)
                    act.wait_ge(ev("smp_mm"), tap(n, TAPS - 1))
                    nc.scalar.activation(x2[:, :], cv[:, 0:PIX], ACT.Relu, bias=bn_s[:, 3:4], scale=bn_s[:, 2:3])\
                        .then_inc(ev("x2_ok"), 1)
                    return
                k, h = divmod(s, 2)
                if h == 0 and k + 1 < TAPS:
                    columns(n, k + 1)

            def qk2(n):
                bk = bank_of("qk2", n)
                act.wait_ge(ev("qk2_mm"), n)
                nc.scalar.activation(q2[:, :], bk[:, 0:PIX], ACT.Identity, bias=col("q_b"))
                nc.scalar.activation(k2[:, :], bk[:, PIX:2 * PIX], ACT.Identity, bias=col("k_b"))\
                    .then_inc(ev("qk2_ok"), 1)

            def soft(b):
                def step(n):
                    bk = bank_of(f"logit{b}", n)
                    act.wait_ge(ev(f"neg_ok{b}"), n)
                    for h in range(HALVES):
                        last = nc.scalar.activation(b_exp[b][:, h, :], bk[:, PIX * h:PIX * (h + 1)], ACT.Exp,
                                                    bias=b_neg[b][:, h:h + 1], scale=QK_SCALE,
                                                    accum_out=b_sum[b][:, h:h + 1])
                    last.then_inc(ev(f"exp_ok{b}"), 1)
                return step

            def e_transpose(b):
                def step(n):
                    bk = bank_of(f"et{b}", n)
                    act.wait_ge(ev(f"et_mm{b}"), n)
                    nc.scalar.activation(e_t[b][:, :, :].rearrange("p j i -> p (j i)"), bk[:, :], ACT.Copy)\
                        .then_inc(ev(f"et_ok{b}"), 1)
                return step

            def v2_step(n):
                bk = bank_of("v2", n)
                act.wait_ge(ev("v2_mm"), n)
                nc.scalar.activation(v2[:, :, :].rearrange("p h c -> p (h c)"), bk[:, 0:PIX], ACT.Copy)\
                    .then_inc(ev("v2_ok"), 1)

            def ln1(n):
                act.wait_ge(ev("h1_ok"), n)
                act.wait_ge(ev("y_ok"), n - 1)
                nc.scalar.activation(z_pad[:, 1:1 + H, 1:1 + W], image(x3[:, :]), ACT.Identity, bias=sc1[:, 3:4],
                                     scale=sc1[:, 2:3]).then_inc(ev("z_ok"), 1)

            def dw_first(n):
                act.wait_ge(ev("z_ok"), n)
                nc.scalar.activation(image(dw_acc[0][:, :]), dw_source(0), ACT.Identity, bias=col("dw_b"),
                                     scale=col("dw_w", 0)).then_inc(ev("dw_step0"), 1)
                nc.scalar.activation(image(dw_acc[1][:, :]), dw_source(1), ACT.Copy,
                                     scale=col("dw_w", 1)).then_inc(ev("dw_step1"), 1)

            def ln2(n, nb):
                act.wait_ge(ev("h2_ok"), n)
                nc.scalar.activation(z2[:, :], x4[:, :], ACT.Identity, bias=sc2[:, 3:4], scale=sc2[:, 2:3])\
                    .then_inc(ev("z2_ok"), 1)

            def scan_first(n, nb):
                act.wait_ge(ev("y_ok"), n)
                for d in range(SCANS):
                    act.wait_ge(ev(f"prod{d}"), n - 1)
                    nc.scalar.activation(image(acc[d][0][:, :]), window(d, 0), ACT.Identity, bias=col("scan_b", d),
                                         scale=col("scan_w", d * KS)).then_inc(ev(f"scan{d}"), 1)

            def gate(i):
                def step(n):
                    bk = bank_of(f"gate{i}", n)
                    act.wait_ge(ev(f"gate_mm{i}"), n)
                    for j in range(2):
                        d = 2 * i + j
                        last = nc.scalar.activation(gates[:, d, :], bk[:, PIX * j:PIX * (j + 1)], ACT.Tanh,
                                                    bias=gate_bh[:, d:d + 1], scale=0.5)
                    last.then_inc(ev(f"gate_ok{i}"), 1)
                return step

            def ff(b):
                def step(n, nb):
                    bk = bank_of(f"ff{b}", n)
                    act.wait_ge(ev(f"ff_mm{b}"), n)
                    nc.scalar.activation(ff_a[b][:, :], bk[:, 0:PIX], ACT.Identity, bias=col("ff1_b", 0))
                    nc.scalar.activation(ff_g[b][:, :], bk[:, PIX:2 * PIX], ACT.Tanh, bias=ff1_bh[:, 0:1], scale=0.5)\
                        .then_inc(ev(f"ff_act{b}"), 1)
                return step

            def wx_plan(c):
                return lambda n: None if is_first(n) else wx_step(c)(n)

            steps_a = {"attn": attn, "attn_t": attn_t, "mix": mix_step, "off": off_step, "off_t": off_t,
                       "abs": hat_step, "split": split, "tr0": tr(0, 2, 0), "tr1": tr(2, 4, 1), "tr2": tr(4, 5, 2),
                       "wx0": wx_plan(0), "wx1": wx_plan(1), "wx2": wx_plan(2), "wx3": wx_plan(3)}
            steps_b = {"qk2": qk2, "soft0": soft(0), "soft1": soft(1), "et0": e_transpose(0), "et1": e_transpose(1),
                       "v2": v2_step, "gate0": gate(0), "gate1": gate(1), "ln1": ln1,
                       "dw_first": dw_first}
            steps_c = {"ff0": ff(0), "ff1": ff(1), "ln2": ln2, "scan_first": scan_first}

            def prepare():
                act.wait_ge(par_late, 16)
                nc.scalar.mul(fuse_h[:, :], part("fuse_w"), 0.5).then_inc(prep_act, 1)
                nc.scalar.mul(ff2_h[:, :], part("ff2_w"), 0.5).then_inc(prep_act, 1)
                nc.scalar.mul(gate_bh[:, :], part("gate_b"), 0.5).then_inc(prep_act, 1)
                nc.scalar.mul(ff1_bh[:, :], col("ff1_b", 1), 0.5).then_inc(prep_act, 1)
                act.wait_ge(prep_mm, 1)
                nc.scalar.activation(pv_w[:, :], mb[:, 0:P], ACT.Copy).then_inc(prep_act, 1)
                nc.scalar.activation(pv_b[:, :], mb[:, P:P + 1], ACT.Identity, bias=col("p_b")).then_inc(prep_act, 1)

            def iteration(n, do_a, do_m, do_b, do_c):
                if isinstance(n, int) and n == 1:
                    prepare()
                once(act, n, 2, prep_act, 6)
                walk(act, PLAN["act"], steps_a, steps_b, steps_c, main, n, do_a, do_m, do_b, do_c, last_a)

            def last_a(n, moment):
                if moment == 0:
                    columns(n, 0)
                elif not is_first(n):
                    wx_step(CHUNKS - 1)(n)

            schedule(act, iteration)
            finish(PLAN_END["act"], steps_b, steps_c)

        @block.vector
        def _(dve):
            def qk(n):
                dve.wait_ge(ev("qk_mm"), n)
                nc.vector.tensor_tensor(qk_sb[:, :, :, :, :].rearrange("p h b k c -> p h (b k c)"),
                                        ma[:, :].rearrange("p (h c) -> p h c", h=HALVES),
                                        part("qk_b").unsqueeze(1).to_broadcast([P, HALVES, 2 * P]),
                                        ALU.add).then_inc(ev("qk_ok"), 1)

            def attn(n):
                dve.wait_ge(ev("attn_mm"), n)
                nc.vector.tensor_reduce(a_max[:, :], ma[:, 0:C], AX_X, ALU.max).then_inc(ev("a_max_ok"), 1)
                dve.wait_ge(ev("a_max_ok"), n)
                nc.vector.tensor_scalar(a_neg[:, :], a_max[:, :], -QK_SCALE, None, ALU.mult)\
                    .then_inc(ev("a_neg_ok"), 1)

            def attn_norm(n):
                dve.wait_ge(ev("a_exp_ok"), n)
                nc.vector.reciprocal(a_rec[:, :], a_sum[:, :]).then_inc(ev("a_rec_ok"), 1)
                dve.wait_ge(ev("a_rec_ok"), n)
                nc.vector.tensor_scalar(a_nrm[:, :], a_exp[:, :], a_rec[:, 0:1], None, ALU.mult)\
                    .then_inc(ev("a_nrm_ok"), 1)

            def x1_step(n):
                dve.wait_ge(ev("x1_mm"), n)
                nc.vector.scalar_tensor_tensor(out=x1[:, :], in0=ma[:, 0:PIX], scalar=mix_b[:, 0:1], in1=x_in[:, :],
                                               op0=ALU.add, op1=ALU.add).then_inc(ev("x1_ok"), 1)
                nc.vector.scalar_tensor_tensor(out=x1_pad[:, 1:1 + H, 1:1 + W], in0=image(ma[:, 0:PIX]),
                                               scalar=mix_b[:, 0:1], in1=image(x_in[:, :]),
                                               op0=ALU.add, op1=ALU.add).then_inc(ev("x1_pad_ok"), 1)

            def off_t(n):
                once(dve, n, 1, par_in, 16)
                dve.wait_ge(ev("pos_mm"), n)
                nc.vector.scalar_tensor_tensor(
                    out=pos[:, :].rearrange("p (g a) -> p g a", g=4),
                    in0=ma[:, 0:4 * OM].rearrange("p (g m) -> p g m", m=OM)[:, :, 0:AXES], scalar=UNIT,
                    in1=part("base").rearrange("p (g a) -> p g a", g=4), op0=ALU.mult, op1=ALU.add)\
                    .then_inc(ev("pos_ok"), 1)

            def hat_step(n):
                if is_first(n):
                    a = 2 * AXES
                    dve.wait_ge(ev("pos_ok"), n)
                    nc.vector.tensor_tensor(dist[:, a:2 * a, :], pos[:, a:2 * a].unsqueeze(2).to_broadcast([P, a, H]),
                                            part("iota").unsqueeze(1).to_broadcast([P, a, H]), ALU.subtract)\
                        .then_inc(ev("dist_ok_dve"), 1)
                dve.wait_ge(ev("tanh_ok"), n)
                nc.vector.tensor_scalar(msk[:, :, :], msk[:, :, :], 1.0, None, ALU.add).then_inc(ev("msk_ok"), 1)

            def hat_y(n):
                dve.wait_ge(ev("abs_ok"), n)
                nc.vector.tensor_scalar(hat[:, :, :, :], hat[:, :, :, :], UNIT, 0.0, ALU.subtract, ALU.min)\
                    .then_inc(ev("hat_ok"), 1)
                dve.wait_ge(ev("hat_ok"), n)
                dve.wait_ge(ev("msk_ok"), n)
                for g in range(4):
                    rows = hat[:, g, 0:AXES:2, :]
                    last = nc.vector.tensor_tensor(rows, rows, msk[:, g, :].unsqueeze(2).to_broadcast([P, TAPS, H]),
                                                   ALU.mult)
                last.then_inc(ev("hat_y_ok"), 1)

            def split(n):
                if is_first(n):
                    dve.wait_ge(ev("high_ok"), n)
                    nc.vector.tensor_tensor(parts[:, 2:4, 0:AXES, 1, :], hat[:, 2:4, :, :], parts[:, 2:4, 0:AXES, 0, :],
                                            ALU.subtract).then_inc(ev("low_ok_dve"), 1)

            def main(n, s):
                if s + 1 < SLOTS:
                    weights(n, s + 1)

            def weights(n, s):
                k, h = divmod(s, 2)
                dve.wait_ge(ev("yb_mm"), slot(n, s))
                if h == 0:
                    dve.wait_ge(ev("xe_ok"), tap(n, k))
                nc.vector.tensor_tensor(wt[k % 2][h][:, :], yb[h][:, :], xe[k % 2][:, :], ALU.mult)\
                    .then_inc(ev("wt_ok"), 1)

            def logit(b):
                def step(n):
                    bk = bank_of(f"logit{b}", n)
                    dve.wait_ge(ev(f"logit_mm{b}"), n)
                    nc.vector.tensor_reduce(b_max[b][:, :], bk[:, :].rearrange("p (h j) -> p h j", h=HALVES), AX_X,
                                            ALU.max).then_inc(ev(f"max_ok{b}"), 1)
                    dve.wait_ge(ev(f"max_ok{b}"), n)
                    nc.vector.tensor_scalar(b_neg[b][:, :], b_max[b][:, :], -QK_SCALE, None, ALU.mult)\
                        .then_inc(ev(f"neg_ok{b}"), 1)
                return step

            def soft(b):
                def step(n):
                    dve.wait_ge(ev(f"exp_ok{b}"), n)
                    nc.vector.reciprocal(b_rec[b][:, :], b_sum[b][:, :]).then_inc(ev(f"rec_ok{b}"), 1)
                    dve.wait_ge(ev(f"rec_ok{b}"), n)
                    for h in range(HALVES):
                        last = nc.vector.tensor_scalar(b_dia[b][:, h, :], part("ident"), b_rec[b][:, h:h + 1], None,
                                                       ALU.mult)
                    last.then_inc(ev(f"nrm_ok{b}"), 1)
                return step

            def stats(src, st, mv, n, st_ok, mv_ok):
                nc.vector.bn_stats(st[:, :], src[:, :]).then_inc(ev(st_ok), 1)
                settle(dve)
                dve.wait_ge(ev(st_ok), n)
                nc.vector.bn_aggr(mv[:, :], st[:, :]).then_inc(ev(mv_ok), 1)

            def x3_step(n):
                bk = bank_of("av", n)
                dve.wait_ge(ev("x3_mm"), n)
                nc.vector.scalar_tensor_tensor(out=x3[:, :], in0=bk[:, 0:PIX], scalar=pv_b[:, 0:1], in1=x2[:, :],
                                               op0=ALU.add, op1=ALU.add).then_inc(ev("x3_ok"), 1)
                dve.wait_ge(ev("x3_ok"), n)
                stats(x3, st1, mv1, n, "st1_ok", "mv1_ok")

            def dw(part_of):
                def step(n):
                    for t in ((2, 3), (4, 5), (6, 7, 8))[part_of]:
                        sum_of = image(dw_acc[t % 2][:, :])
                        dve.wait_ge(ev(f"dw_step{t % 2}"), dw_count(n, t - 2))
                        nc.vector.scalar_tensor_tensor(out=sum_of, in0=dw_source(t), scalar=col("dw_w", t), in1=sum_of,
                                                       op0=ALU.mult, op1=ALU.add).then_inc(ev(f"dw_step{t % 2}"), 1)
                    if part_of == 2:
                        dve.wait_ge(ev("dw_step0"), dw_count(n, TAPS - 1))
                        dve.wait_ge(ev("dw_step1"), dw_count(n, TAPS - 2))
                        nc.vector.tensor_tensor(y_pad[:, 2:2 + H, 2:2 + W], image(dw_acc[0][:, :]),
                                                image(dw_acc[1][:, :]), ALU.add).then_inc(ev("y_ok"), 1)
                return step

            def scan(j):
                def step(n, nb):
                    for d in range(3):
                        dve.wait_ge(ev(f"scan{d}"), scan_count(n, j - 1))
                        nc.vector.scalar_tensor_tensor(out=image(acc[d][j % 2][:, :]), in0=window(d, j),
                                                       scalar=col("scan_w", d * KS + j),
                                                       in1=image(acc[d][(j - 1) % 2][:, :]), op0=ALU.mult, op1=ALU.add)\
                            .then_inc(ev(f"scan{d}"), 1)
                return step

            def gated(d):
                def step(n, nb):
                    dve.wait_ge(ev(f"scan{d}"), scan_count(n, KS - 1))
                    dve.wait_ge(ev(f"gate_ok{d // 2}"), n)
                    nc.vector.scalar_tensor_tensor(out=prod[d][:, :], in0=gates[:, d, :], scalar=1.0,
                                                   in1=acc[d][(KS - 1) % 2][:, :], op0=ALU.add, op1=ALU.mult)\
                        .then_inc(ev(f"prod{d}"), 1)
                return step

            def scan_sum(n, nb):
                dve.wait_ge(ev("prod2"), n)
                dve.wait_ge(ev("prod3"), n)
                nc.vector.tensor_tensor(o_b[:, :], prod[2][:, :], prod[3][:, :], ALU.add).then_inc(ev("o_b"), 1)
                dve.wait_ge(ev("o_a"), n)
                dve.wait_ge(ev("o_b"), n)
                nc.vector.tensor_tensor(o_sum[:, :], o_a[:, :], o_b[:, :], ALU.add).then_inc(ev("o_ok"), 1)

            def fuse(n, nb):
                bk = bank_of("fuse", n)
                dve.wait_ge(ev("fuse_mm"), n)
                nc.vector.scalar_tensor_tensor(out=x4[:, :], in0=bk[:, 0:PIX], scalar=col("fuse_b"), in1=x3[:, :],
                                               op0=ALU.add, op1=ALU.add).then_inc(ev("x4_ok"), 1)
                dve.wait_ge(ev("x4_ok"), n)
                stats(x4, st2, mv2, n, "st2_ok", "mv2_ok")

            def ff(b):
                def step(n, nb):
                    dve.wait_ge(ev(f"ff_act{b}"), n)
                    nc.vector.scalar_tensor_tensor(out=ff_u[b][:, :], in0=ff_g[b][:, :], scalar=1.0, in1=ff_a[b][:, :],
                                                   op0=ALU.add, op1=ALU.mult).then_inc(ev(f"ff_u{b}"), 1)
                return step

            def ff2(n, nb):
                bk = bank_of("ff2", n)
                dve.wait_ge(ev("out_mm"), n)
                dve.wait_ge(stored, 16 * n - 16)
                nc.vector.scalar_tensor_tensor(out=y_out[:, :], in0=bk[:, 0:PIX], scalar=col("ff2_b"), in1=x4[:, :],
                                               op0=ALU.add, op1=ALU.add).then_inc(ev("y_out_ok"), 1)

            steps_a = {"qk": qk, "attn": attn, "attn_norm": attn_norm, "x1": x1_step, "off_t": off_t,
                       "hat": hat_step, "hat_y": hat_y, "split": split}
            steps_b = {"logit0": logit(0), "logit1": logit(1), "nrm0": soft(0), "nrm1": soft(1),
                       "x3": x3_step, "dw0": dw(0), "dw1": dw(1), "dw2": dw(2)}
            steps_c = {"scan_t1": scan(1), "scan_t2": scan(2), "scan_t3": scan(3), "scan_t4": scan(4),
                       "gated0": gated(0), "gated1": gated(1), "gated2": gated(2),
                       "gated3": gated(3), "scan_sum": scan_sum, "fuse": fuse,
                       "u0": ff(0), "u1": ff(1), "ff2": ff2}

            def iteration(n, do_a, do_m, do_b, do_c):
                once(dve, n, 2, par_late, 16)
                once(dve, n, 2, prep_act, 6)
                walk(dve, PLAN["dve"], steps_a, steps_b, steps_c, main, n, do_a, do_m, do_b, do_c, last_a)

            def last_a(n, moment):
                if moment == 0:
                    weights(n, 0)

            nc.vector.memset(mix[:, :], 0.0).then_inc(zero_ok, 1)
            nc.vector.memset(z_pad[:, :, :], 0.0).then_inc(zero_ok, 1)
            nc.vector.memset(y_pad[:, :, :], 0.0).then_inc(zero_ok, 1)
            nc.vector.memset(parts[:, :, AXES:4 * GROUPS, :, :], 0.0).then_inc(zero_ok, 1)
            nc.vector.memset(x1_pad[:, :, :], 0.0).then_inc(zero_ok, 1)
            dve.wait_ge(zero_ok, 5)
            dve.wait_ge(par_first, 32)
            schedule(dve, iteration)
            finish(PLAN_END["dve"], steps_b, steps_c)

        @block.gpsimd
        def _(pool):
            def hat_step(n):
                once(pool, n, 1, par_in, 16)
                pool.wait_ge(ev("pos_ok"), n)
                groups = 2 * AXES if is_first(n) else 4 * AXES
                nc.gpsimd.tensor_tensor(dist[:, 0:groups, :], pos[:, 0:groups].unsqueeze(2).to_broadcast([P, groups, H]),
                                        part("iota").unsqueeze(1).to_broadcast([P, groups, H]), ALU.subtract)\
                    .then_inc(ev("dist_ok"), 1)

            def split(n):
                pool.wait_ge(ev("high_ok"), n)
                g = 2 if is_first(n) else 4
                nc.gpsimd.tensor_tensor(parts[:, 0:g, 0:AXES, 1, :], hat[:, 0:g, :, :], parts[:, 0:g, 0:AXES, 0, :],
                                        ALU.subtract).then_inc(ev("low_ok"), 1)

            def norm(src_mv, scl, gain, mv_ok, var_ok, rstd_ok, g_ok, m_ok, h_ok):
                def step(n, *_):
                    settle(pool)
                    pool.wait_ge(ev(mv_ok), n)
                    nc.gpsimd.tensor_scalar(scl[:, 0:1], src_mv[:, 1:2], LN_EPS, 1.0, ALU.add, ALU.mult)\
                        .then_inc(ev(var_ok), 1)
                    pool.wait_ge(ev(var_ok), n)
                    nc.gpsimd.tensor_tensor(scl[:, 1:2], scl[:, 0:1], half[:, :], ALU.pow).then_inc(ev(rstd_ok), 1)
                    pool.wait_ge(ev(rstd_ok), n)
                    nc.gpsimd.tensor_tensor(scl[:, 2:3], scl[:, 1:2], col(gain, 0), ALU.mult).then_inc(ev(g_ok), 1)
                    pool.wait_ge(ev(g_ok), n)
                    nc.gpsimd.tensor_tensor(scl[:, 4:5], src_mv[:, 0:1], scl[:, 2:3], ALU.mult).then_inc(ev(m_ok), 1)
                    pool.wait_ge(ev(m_ok), n)
                    nc.gpsimd.tensor_tensor(scl[:, 3:4], col(gain, 1), scl[:, 4:5], ALU.subtract)\
                        .then_inc(ev(h_ok), 1)
                return step

            def scan3(n, nb):
                d = 3
                settle(pool)
                pool.wait_ge(ev("y_ok"), n)
                a = d * KS
                for j in range(1, KS):
                    nc.gpsimd.tensor_scalar(image(g_tmp[j % 2][:, :]), y_pad[:, j:j + H, 2:2 + W], col("scan_w", a + j),
                                            0.0, ALU.mult, ALU.add).then_inc(ev("term"), 1)
                    pool.wait_ge(ev("term"), n * (KS - 1) - (KS - 1) + j)
                    pool.wait_ge(ev(f"scan{d}"), scan_count(n, j - 1))
                    nc.gpsimd.tensor_tensor(acc[d][j % 2][:, :], acc[d][(j - 1) % 2][:, :], g_tmp[j % 2][:, :], ALU.add)\
                        .then_inc(ev(f"scan{d}"), 1)

            def scan_end(n, nb):
                pool.wait_ge(ev("prod0"), n)
                pool.wait_ge(ev("prod1"), n)
                nc.gpsimd.tensor_tensor(o_a[:, :], prod[0][:, :], prod[1][:, :], ALU.add).then_inc(ev("o_a"), 1)

            steps_a = {"hat": hat_step, "split": split}
            steps_b = {"x3": norm(mv1, sc1, "ln1", "mv1_ok", "var1_ok", "rstd1_ok", "g1_ok", "m1_ok", "h1_ok")}
            steps_c = {"fuse": norm(mv2, sc2, "ln2", "mv2_ok", "var2_ok", "rstd2_ok", "g2_ok", "m2_ok", "h2_ok"),
                       "scan3": scan3, "scan_end": scan_end}

            def prepare():
                pool.wait_ge(par_late, 16)
                nc.gpsimd.tensor_scalar(bn_s[:, 0:1], col("bn", 1), BN_EPS, 1.0, ALU.add, ALU.mult)\
                    .then_inc(bn_step, 1)
                pool.wait_ge(bn_step, 1)
                nc.gpsimd.tensor_tensor(bn_s[:, 1:2], bn_s[:, 0:1], half[:, :], ALU.pow).then_inc(bn_step, 1)
                pool.wait_ge(bn_step, 2)
                nc.gpsimd.tensor_tensor(bn_s[:, 2:3], bn_s[:, 1:2], col("bn", 0), ALU.mult).then_inc(bn_step, 1)
                nc.gpsimd.tensor_tensor(bn_s[:, 4:5], col("bn", 4), col("bn", 2), ALU.subtract).then_inc(bn_step, 1)
                pool.wait_ge(bn_step, 4)
                nc.gpsimd.tensor_scalar(bn_s[:, 3:4], bn_s[:, 4:5], bn_s[:, 2:3], col("bn", 3), ALU.mult, ALU.add)\
                    .then_inc(bn_step, 1)

            def iteration(n, do_a, do_m, do_b, do_c):
                if isinstance(n, int) and n == 1:
                    prepare()
                walk(pool, PLAN["pool"], steps_a, steps_b, steps_c, lambda n, s: None, n, do_a, do_m, do_b, do_c,
                     lambda n, moment: None)

            nc.gpsimd.memset(half[:, :], -0.5).then_inc(half_ok, 1)
            pool.wait_ge(half_ok, 1)
            schedule(pool, iteration)
            finish(PLAN_END["pool"], steps_b, steps_c)


def _pack(a):
    f = np.float32
    wt = lambda w: np.ascontiguousarray(w.T)

    def twice(m):
        k, n = m.shape
        out = np.zeros((2, k, 2, n), f)
        out[0, :, 0], out[1, :, 1] = m, m
        return out.reshape(2 * k, 2 * n)

    def both(v):
        v = np.asarray(v).reshape(C, -1)
        return np.concatenate([v, v], 0)

    def spread(v):
        return np.broadcast_to(np.asarray(v).reshape(1, -1), (P, np.asarray(v).size))

    d = {"ident": np.eye(P, dtype=f)}
    d["qk_w"] = twice(np.concatenate([wt(a["L0_conv_wq"]), wt(a["L0_conv_wk"])], 1))
    d["qk_b"] = spread(np.concatenate([a["L0_conv_bq"], a["L0_conv_bk"]] * 2))
    wv, bv = a["L0_conv_wv"], a["L0_conv_bv"]
    d["av_w"] = np.concatenate([np.concatenate([wv, wv, bv[:, None]], 1), np.zeros((P - C, P + 1), f)], 0)
    w = np.zeros((TAPS, C, OM), f)
    w[:, :, 0:AXES + TAPS] = a["L1_conv_w_off"].reshape(AXES + TAPS, C, TAPS).transpose(2, 1, 0)
    d["off_w"] = np.concatenate([twice(w[t]) for t in range(TAPS)], 1)
    b = np.zeros((4, OM), f)
    b[:, 0:AXES + TAPS] = a["L1_conv_b_off"]
    d["off_b"] = b.reshape(P, 1)
    p, h, k = np.arange(P)[:, None, None], np.arange(HALVES)[None, :, None], np.arange(TAPS)[None, None, :]
    yx = np.stack([HALF_ROWS * h + p // W + k // 3 - 1 + 0 * k, p % W + k % 3 - 1 + 0 * h], -1)
    d["base"] = np.repeat(yx.reshape(P, HALVES, 1, AXES), 2, 2).reshape(P, 4 * AXES).astype(f) * f(UNIT)
    d["iota"] = spread(np.arange(H, dtype=f) * f(UNIT))
    w = a["L1_conv_w_dcn"].reshape(C, C, TAPS).transpose(2, 1, 0)
    d["dcn_w"] = np.concatenate([twice(w[t]) for t in range(TAPS)], 1)
    d["bn"] = np.concatenate([both(a["L1_conv_" + n]) for n in
                              ("gamma", "running_var", "running_mean", "beta", "b_dcn")], 1)
    for n in "qkvp":
        w = a["L2_conv_w" + n]
        d[n + "_w"] = twice(w if n == "v" else wt(w))
        d[n + "_b"] = both(a["L2_conv_b" + n])
    for n in ("1", "2"):
        d["ln" + n] = np.concatenate([both(a[f"L3_conv_ln{n}_w"]), both(a[f"L3_conv_ln{n}_b"])], 1)
    d["dw_w"] = both(a["L3_conv_dw_w"].reshape(TAPS, C).T)
    d["dw_b"] = both(a["L3_conv_dw_b"])
    taps = [a[f"L3_conv_{n}_dw_w"].reshape(KS, C)[::r] for n, r in (("lr", 1), ("rl", -1), ("tb", 1), ("bt", -1))]
    d["scan_w"] = both(np.concatenate(taps, 0).T)
    names = ("lr", "rl", "tb", "bt")
    d["scan_b"] = both(np.stack([a[f"L3_conv_{n}_dw_b"] for n in names], 1))
    d["gate_w"] = np.concatenate([twice(wt(a[f"L3_conv_{n}_g_w"])) for n in names], 1)
    d["gate_b"] = both(np.stack([a[f"L3_conv_{n}_g_b"] for n in names], 1))
    d["fuse_w"] = twice(wt(a["L3_conv_fuse_w"]))
    d["fuse_b"] = both(a["L3_conv_fuse_b"])
    w = wt(a["L3_conv_ff1_w"])
    d["ff1_w"] = np.concatenate([w, w], 0)
    d["ff1_b"] = a["L3_conv_ff1_b"].reshape(2, HID).T
    d["ff2_w"] = wt(a["L3_conv_ff2_w"])
    d["ff2_b"] = both(a["L3_conv_ff2_b"])
    return np.ascontiguousarray(np.concatenate([np.asarray(d[n], f).reshape(P, k) for n, k in PARTS], 1))


def _selectors():
    row = np.arange(P).reshape(4, 2, H, 1)
    slot, i = row // SLOT, row % H
    q = np.arange(P).reshape(1, 1, 1, P)
    out = [np.eye(P)]
    for odd in range(2):
        out.append(((slot == 2 * odd + 1) & (i == q % W)).reshape(P, P))
    for odd in range(2):
        for h in range(HALVES):
            out.append(((slot == 2 * odd) & (i == HALF_ROWS * h + q // W)).reshape(P, P))
    return np.ascontiguousarray(np.concatenate(out, 1).astype(np.float16))


def kernel(**inputs):
    import concourse.bacc as bacc
    from concourse.bass_utils import run_bass_kernel_spmd

    a = {k: np.asarray(v) for k, v in inputs.items()}
    arrays = {
        "in_x": np.ascontiguousarray(a["x"].reshape(PAIRS, P, PIX)),
        "in_par": _pack(a),
        "in_sel": _selectors(),
    }
    nc = bacc.Bacc("TRN2", target_bir_lowering=False, num_devices=1)
    args = [nc.dram_tensor(n, v.shape, mybir.dt.from_np(v.dtype), kind="ExternalInput").ap() for n, v in arrays.items()]
    args.append(nc.dram_tensor("out_y", (PAIRS, P, PIX), F32, kind="ExternalOutput").ap())
    program(nc, *args)
    r = run_bass_kernel_spmd(nc, [arrays], core_ids=[0])
    return np.asarray(r.results[0]["out_y"]).reshape(IMAGES, C, H, W)
```
